# Optimizing a Trainium2 kernel written in Bass

```python
import numpy as np
import jax
import jax.numpy as jnp

def _softmax(x, axis=-1):
    return jax.nn.softmax(x, axis=axis)

def _gelu(x):
    return jax.nn.gelu(x, approximate=True)

def _silu(x):
    return jax.nn.silu(x)

def _sigmoid(x):
    return jax.nn.sigmoid(x)

def _layernorm(x, axis=-1, eps=1e-05):
    m = jnp.mean(x, axis=axis, keepdims=True)
    v = jnp.var(x, axis=axis, keepdims=True)
    return (x - m) / jnp.sqrt(v + eps)

def _scatter_add(tgt, idx, src, axis=0):
    return tgt.at[idx].add(src)

def _segment_sum(src, seg, n):
    return jax.ops.segment_sum(src, seg, n)
kernel_name = 'mk_pixart_seq_d4_seqx_r4_77e580'

def setup_inputs(seed: int=0):
    np.random.seed(seed)
    _w = jnp.asarray

    def _rec_inputs():
        import jax
        import jax.numpy as jnp
        _rk = jax.random.key(seed)
        x = -0.0003929 + 0.9999 * jax.random.normal(jax.random.fold_in(_rk, 1), (4, 1024, 256), jnp.float32)
        _lenS = 1024 - jax.random.randint(jax.random.fold_in(_rk, 7), (4,), 0, max(1, 1024 // 4) + 1, jnp.int32)
        _lenS2 = 77 - jax.random.randint(jax.random.fold_in(_rk, 8), (4,), 0, max(1, 77 // 4) + 1, jnp.int32)
        cond_1024 = 0.00782532 + 1.00527 * jax.random.normal(jax.random.fold_in(_rk, 11), (4, 256), jnp.float32)
        _ctx_1024P = jax.random.normal(jax.random.fold_in(_rk, 12), (4, 16, 256), jnp.float32)
        _ctx_1024c = jax.random.dirichlet(jax.random.fold_in(_rk, 512), 0.3 * jnp.ones((16,), jnp.float32), (4, 77))
        _ctx_1024t = jnp.einsum('bsk,bkd->bsd', _ctx_1024c, _ctx_1024P)
        _ctx_1024t = _ctx_1024t * jax.lax.rsqrt(jnp.mean(jnp.square(_ctx_1024t)) + 1e-12) * 0.953939
        ctx_1024 = -0.000761806 + 0.999296 * (_ctx_1024t + 0.3 * jax.random.normal(jax.random.fold_in(_rk, 612), (4, 77, 256), jnp.float32))
        _validS = jnp.arange(1024)[None, :] < _lenS[:, None]
        _validS2 = jnp.arange(77)[None, :] < _lenS2[:, None]
        _causal = jnp.tril(jnp.ones((1024, 1024), dtype=bool))
        mask_BxS2_ik0 = jnp.where(jnp.broadcast_to(_validS2[:, :], (4, 77)), 0, 1).astype(jnp.int32)
        return (x, cond_1024, ctx_1024, mask_BxS2_ik0)
    x, cond_1024, ctx_1024, mask_BxS2_ik0 = _rec_inputs()

    def _L0_xcond_setup():
        import jax, jax.numpy as jnp
        import numpy as np
        H = 256
        RH = 2 * H
        E = 3
        B, T, P = (8, 512, 64)
        LN_EPS = 1e-05

        def _layer_norm(x, gamma, beta):
            mu = jnp.mean(x, axis=-1, keepdims=True)
            var = jnp.mean(jnp.square(x - mu), axis=-1, keepdims=True)
            return (x - mu) * jax.lax.rsqrt(var + LN_EPS) * gamma + beta
        key = jax.random.key(seed)
        ks = jax.random.split(key, 24)
        s = lambda fan_in: 1.0 / np.sqrt(fan_in)
        inp = {'mix_hidden_states': jax.random.normal(ks[0], (B, T, H), jnp.float32), 'global_anchor': jax.random.normal(ks[1], (B, H), jnp.float32), 'prototype_bank': jax.random.normal(ks[2], (B, P, H), jnp.float32), 'ln_gamma': jnp.ones((H,), jnp.float32), 'ln_beta': jnp.zeros((H,), jnp.float32), 'Wq': jax.random.normal(ks[3], (H, H), jnp.float32) * s(H), 'Wk': jax.random.normal(ks[4], (H, H), jnp.float32) * s(H), 'Wv': jax.random.normal(ks[5], (H, H), jnp.float32) * s(H), 'router_W': jax.random.normal(ks[6], (3 * H, E), jnp.float32) * s(3 * H), 'router_b': jnp.zeros((E,), jnp.float32), 'e_w1': jax.random.normal(ks[7], (E, 3 * H, RH), jnp.float32) * s(3 * H), 'e_b1': jnp.zeros((E, RH), jnp.float32), 'e_w2': jax.random.normal(ks[8], (E, RH, H), jnp.float32) * s(RH), 'e_b2': jnp.zeros((E, H), jnp.float32), 'gate_w1': jax.random.normal(ks[9], (3 * H, H), jnp.float32) * s(3 * H), 'gate_b1': jnp.zeros((H,), jnp.float32), 'gate_w2': jax.random.normal(ks[10], (H, H), jnp.float32) * s(H), 'gate_b2': jnp.zeros((H,), jnp.float32), 'out_w': jax.random.normal(ks[11], (H, H), jnp.float32) * s(H), 'out_b': jnp.zeros((H,), jnp.float32)}
        return inp
    _L0_xcond_all = _L0_xcond_setup()
    _L0_xcond_in = {k: v for k, v in _L0_xcond_all.items() if k in ('ln_gamma', 'ln_beta', 'Wq', 'Wk', 'Wv', 'router_W', 'router_b', 'e_w1', 'e_b1', 'e_w2', 'e_b2', 'gate_w1', 'gate_b1', 'gate_w2', 'gate_b2', 'out_w', 'out_b')}
    del _L0_xcond_all

    def _L1_xcond_setup():
        import jax, jax.numpy as jnp
        import numpy as np
        D = 256
        H = 16
        HD = D // H
        FF = 4 * D
        B, NQ, NK = (8, 256, 128)
        EPS = 1e-05

        def layernorm(x, g, b):
            m = jnp.mean(x, axis=-1, keepdims=True)
            v = jnp.mean(jnp.square(x - m), axis=-1, keepdims=True)
            return (x - m) * jax.lax.rsqrt(v + EPS) * g + b

        def mha(x, ctx, wq, bq, wk, bk, wv, bv, wo, bo, mask=None):
            Bq, Nq, _ = x.shape
            Nk = ctx.shape[1]
            q = (x @ wq + bq).reshape(Bq, Nq, H, HD)
            k = (ctx @ wk + bk).reshape(Bq, Nk, H, HD)
            v = (ctx @ wv + bv).reshape(Bq, Nk, H, HD)
            scores = jnp.einsum('bqhd,bkhd->bhqk', q, k) / np.sqrt(HD)
            if mask is not None:
                scores = jnp.where(mask[:, None, None, :].astype(bool), scores, -jnp.inf)
            attn = jax.nn.softmax(scores.astype(jnp.float32), axis=-1).astype(scores.dtype)
            out = jnp.einsum('bhqk,bkhd->bqhd', attn, v).reshape(Bq, Nq, D)
            return out @ wo + bo
        key = jax.random.key(seed)
        ks = jax.random.split(key, 40)
        rn = lambda k, shape, s=0.02: jax.random.normal(k, shape, jnp.float32) * s
        inp = {'x': jax.random.normal(ks[0], (B, NQ, D), jnp.float32), 't_emb': jax.random.normal(ks[1], (B, D), jnp.float32), 'context_emb': jax.random.normal(ks[2], (B, NK, D), jnp.float32), 'mask': jax.random.randint(ks[3], (B, NK), 0, 2, jnp.int32), 'ln1_g': jnp.ones((D,), jnp.float32), 'ln1_b': jnp.zeros((D,), jnp.float32), 'ln3_g': jnp.ones((D,), jnp.float32), 'ln3_b': jnp.zeros((D,), jnp.float32), 'ln2_g': jnp.ones((D,), jnp.float32), 'ln2_b': jnp.zeros((D,), jnp.float32), 'sa_wq': rn(ks[4], (D, D)), 'sa_bq': jnp.zeros((D,), jnp.float32), 'sa_wk': rn(ks[5], (D, D)), 'sa_bk': jnp.zeros((D,), jnp.float32), 'sa_wv': rn(ks[6], (D, D)), 'sa_bv': jnp.zeros((D,), jnp.float32), 'sa_wo': rn(ks[7], (D, D)), 'sa_bo': jnp.zeros((D,), jnp.float32), 'ca_wq': rn(ks[8], (D, D)), 'ca_bq': jnp.zeros((D,), jnp.float32), 'ca_wk': rn(ks[9], (D, D)), 'ca_bk': jnp.zeros((D,), jnp.float32), 'ca_wv': rn(ks[10], (D, D)), 'ca_bv': jnp.zeros((D,), jnp.float32), 'ca_wo': rn(ks[11], (D, D)), 'ca_bo': jnp.zeros((D,), jnp.float32), 'tp_w': rn(ks[12], (D, 3 * D)), 'tp_b': jnp.zeros((3 * D,), jnp.float32), 'w1': rn(ks[13], (D, FF)), 'b1': jnp.zeros((FF,), jnp.float32), 'w2': rn(ks[14], (FF, D)), 'b2': jnp.zeros((D,), jnp.float32)}
        return inp
    _L1_xcond_all = _L1_xcond_setup()
    _L1_xcond_in = {k: v for k, v in _L1_xcond_all.items() if k in ('ln1_g', 'ln1_b', 'ln3_g', 'ln3_b', 'ln2_g', 'ln2_b', 'sa_wq', 'sa_bq', 'sa_wk', 'sa_bk', 'sa_wv', 'sa_bv', 'sa_wo', 'sa_bo', 'ca_wq', 'ca_bq', 'ca_wk', 'ca_bk', 'ca_wv', 'ca_bv', 'ca_wo', 'ca_bo', 'tp_w', 'tp_b', 'w1', 'b1', 'w2', 'b2')}
    del _L1_xcond_all

    def _L2_xcond_setup():
        import jax, jax.numpy as jnp
        import numpy as np
        D = 256
        H = 16
        HD = D // H
        MLP = 4 * D
        EPS = 1e-06
        SCALE = HD ** (-0.5)

        def _p(key, shape, s=0.02):
            return jax.random.normal(key, shape, dtype=jnp.float32) * s

        def _ln(x):
            mu = jnp.mean(x, axis=-1, keepdims=True)
            var = jnp.var(x, axis=-1, keepdims=True)
            return (x - mu) * jax.lax.rsqrt(var + EPS)

        def _heads(t):
            B, L, _ = t.shape
            return t.reshape(B, L, H, HD).transpose(0, 2, 1, 3)

        def _attend(q, k, v):
            attn = jnp.einsum('bhnd,bhsd->bhns', q, k) * SCALE
            attn = jax.nn.softmax(attn, axis=-1)
            o = jnp.einsum('bhns,bhsd->bhnd', attn, v)
            B, _, N, _ = q.shape
            return o.transpose(0, 2, 1, 3).reshape(B, N, D)
        key = jax.random.key(seed)
        ks = jax.random.split(key, 24)
        B, N, S = (4, 256, 77)
        return {'x': jax.random.normal(ks[0], (B, N, D), dtype=jnp.float32), 't_emb': jax.random.normal(ks[1], (B, D), dtype=jnp.float32), 'context': jax.random.normal(ks[2], (B, S, D), dtype=jnp.float32), 'adaln_w': _p(ks[3], (D, 6 * D)), 'adaln_b': _p(ks[4], (6 * D,)), 'qkv_w': _p(ks[5], (D, 3 * D)), 'qkv_b': _p(ks[6], (3 * D,)), 'sa_proj_w': _p(ks[7], (D, D)), 'sa_proj_b': _p(ks[8], (D,)), 'q_w': _p(ks[9], (D, D)), 'q_b': _p(ks[10], (D,)), 'kv_w': _p(ks[11], (D, 2 * D)), 'kv_b': _p(ks[12], (2 * D,)), 'ca_proj_w': _p(ks[13], (D, D)), 'ca_proj_b': _p(ks[14], (D,)), 'fc1_w': _p(ks[15], (D, MLP)), 'fc1_b': _p(ks[16], (MLP,)), 'fc2_w': _p(ks[17], (MLP, D)), 'fc2_b': _p(ks[18], (D,))}
    _L2_xcond_all = _L2_xcond_setup()
    _L2_xcond_in = {k: v for k, v in _L2_xcond_all.items() if k in ('adaln_w', 'adaln_b', 'qkv_w', 'qkv_b', 'sa_proj_w', 'sa_proj_b', 'q_w', 'q_b', 'kv_w', 'kv_b', 'ca_proj_w', 'ca_proj_b', 'fc1_w', 'fc1_b', 'fc2_w', 'fc2_b')}
    del _L2_xcond_all

    def _L3_xcond_setup():
        import jax, jax.numpy as jnp
        import numpy as np
        EPS = 1e-05

        def _ada_ln(x, c, W_ss, b_ss):
            mu = jnp.mean(x, axis=-1, keepdims=True)
            var = jnp.mean((x - mu) ** 2, axis=-1, keepdims=True)
            h = (x - mu) / jnp.sqrt(var + EPS)
            ss = jax.nn.silu(c) @ W_ss + b_ss
            scale, bias = jnp.split(ss, 2, axis=-1)
            return (1.0 + scale)[:, None, :] * h + bias[:, None, :]
        key = jax.random.key(seed)
        ks = jax.random.split(key, 12)
        B, Lq, Lkv, H = (8, 512, 128, 256)
        s = 0.02
        return {'x_q': jax.random.normal(ks[0], (B, Lq, H), jnp.float32), 'x_kv': jax.random.normal(ks[1], (B, Lkv, H), jnp.float32), 't_vec': jax.random.normal(ks[2], (B, H), jnp.float32), 'Wq': jax.random.normal(ks[3], (H, H), jnp.float32) * s, 'bq': jnp.zeros((H,), jnp.float32), 'Wkv': jax.random.normal(ks[4], (H, 2 * H), jnp.float32) * s, 'bkv': jnp.zeros((2 * H,), jnp.float32), 'Wp': jax.random.normal(ks[5], (H, H), jnp.float32) * s, 'bp': jnp.zeros((H,), jnp.float32), 'Wss_q': jax.random.normal(ks[6], (H, 2 * H), jnp.float32) * s, 'bss_q': jnp.zeros((2 * H,), jnp.float32), 'Wss_kv': jax.random.normal(ks[7], (H, 2 * H), jnp.float32) * s, 'bss_kv': jnp.zeros((2 * H,), jnp.float32)}
    _L3_xcond_all = _L3_xcond_setup()
    _L3_xcond_in = {k: v for k, v in _L3_xcond_all.items() if k in ('Wq', 'bq', 'Wkv', 'bkv', 'Wp', 'bp', 'Wss_q', 'bss_q', 'Wss_kv', 'bss_kv')}
    del _L3_xcond_all
    return {'x': x, 'cond_1024': cond_1024, 'ctx_1024': ctx_1024, 'mask_BxS2_ik0': mask_BxS2_ik0, 'L0_xcond_ln_gamma': _L0_xcond_in['ln_gamma'], 'L0_xcond_ln_beta': _L0_xcond_in['ln_beta'], 'L0_xcond_Wq': _L0_xcond_in['Wq'], 'L0_xcond_Wk': _L0_xcond_in['Wk'], 'L0_xcond_Wv': _L0_xcond_in['Wv'], 'L0_xcond_router_W': _L0_xcond_in['router_W'], 'L0_xcond_router_b': _L0_xcond_in['router_b'], 'L0_xcond_e_w1': _L0_xcond_in['e_w1'], 'L0_xcond_e_b1': _L0_xcond_in['e_b1'], 'L0_xcond_e_w2': _L0_xcond_in['e_w2'], 'L0_xcond_e_b2': _L0_xcond_in['e_b2'], 'L0_xcond_gate_w1': _L0_xcond_in['gate_w1'], 'L0_xcond_gate_b1': _L0_xcond_in['gate_b1'], 'L0_xcond_gate_w2': _L0_xcond_in['gate_w2'], 'L0_xcond_gate_b2': _L0_xcond_in['gate_b2'], 'L0_xcond_out_w': _L0_xcond_in['out_w'], 'L0_xcond_out_b': _L0_xcond_in['out_b'], 'L1_xcond_ln1_g': _L1_xcond_in['ln1_g'], 'L1_xcond_ln1_b': _L1_xcond_in['ln1_b'], 'L1_xcond_ln3_g': _L1_xcond_in['ln3_g'], 'L1_xcond_ln3_b': _L1_xcond_in['ln3_b'], 'L1_xcond_ln2_g': _L1_xcond_in['ln2_g'], 'L1_xcond_ln2_b': _L1_xcond_in['ln2_b'], 'L1_xcond_sa_wq': _L1_xcond_in['sa_wq'], 'L1_xcond_sa_bq': _L1_xcond_in['sa_bq'], 'L1_xcond_sa_wk': _L1_xcond_in['sa_wk'], 'L1_xcond_sa_bk': _L1_xcond_in['sa_bk'], 'L1_xcond_sa_wv': _L1_xcond_in['sa_wv'], 'L1_xcond_sa_bv': _L1_xcond_in['sa_bv'], 'L1_xcond_sa_wo': _L1_xcond_in['sa_wo'], 'L1_xcond_sa_bo': _L1_xcond_in['sa_bo'], 'L1_xcond_ca_wq': _L1_xcond_in['ca_wq'], 'L1_xcond_ca_bq': _L1_xcond_in['ca_bq'], 'L1_xcond_ca_wk': _L1_xcond_in['ca_wk'], 'L1_xcond_ca_bk': _L1_xcond_in['ca_bk'], 'L1_xcond_ca_wv': _L1_xcond_in['ca_wv'], 'L1_xcond_ca_bv': _L1_xcond_in['ca_bv'], 'L1_xcond_ca_wo': _L1_xcond_in['ca_wo'], 'L1_xcond_ca_bo': _L1_xcond_in['ca_bo'], 'L1_xcond_tp_w': _L1_xcond_in['tp_w'], 'L1_xcond_tp_b': _L1_xcond_in['tp_b'], 'L1_xcond_w1': _L1_xcond_in['w1'], 'L1_xcond_b1': _L1_xcond_in['b1'], 'L1_xcond_w2': _L1_xcond_in['w2'], 'L1_xcond_b2': _L1_xcond_in['b2'], 'L2_xcond_adaln_w': _L2_xcond_in['adaln_w'], 'L2_xcond_adaln_b': _L2_xcond_in['adaln_b'], 'L2_xcond_qkv_w': _L2_xcond_in['qkv_w'], 'L2_xcond_qkv_b': _L2_xcond_in['qkv_b'], 'L2_xcond_sa_proj_w': _L2_xcond_in['sa_proj_w'], 'L2_xcond_sa_proj_b': _L2_xcond_in['sa_proj_b'], 'L2_xcond_q_w': _L2_xcond_in['q_w'], 'L2_xcond_q_b': _L2_xcond_in['q_b'], 'L2_xcond_kv_w': _L2_xcond_in['kv_w'], 'L2_xcond_kv_b': _L2_xcond_in['kv_b'], 'L2_xcond_ca_proj_w': _L2_xcond_in['ca_proj_w'], 'L2_xcond_ca_proj_b': _L2_xcond_in['ca_proj_b'], 'L2_xcond_fc1_w': _L2_xcond_in['fc1_w'], 'L2_xcond_fc1_b': _L2_xcond_in['fc1_b'], 'L2_xcond_fc2_w': _L2_xcond_in['fc2_w'], 'L2_xcond_fc2_b': _L2_xcond_in['fc2_b'], 'L3_xcond_Wq': _L3_xcond_in['Wq'], 'L3_xcond_bq': _L3_xcond_in['bq'], 'L3_xcond_Wkv': _L3_xcond_in['Wkv'], 'L3_xcond_bkv': _L3_xcond_in['bkv'], 'L3_xcond_Wp': _L3_xcond_in['Wp'], 'L3_xcond_bp': _L3_xcond_in['bp'], 'L3_xcond_Wss_q': _L3_xcond_in['Wss_q'], 'L3_xcond_bss_q': _L3_xcond_in['bss_q'], 'L3_xcond_Wss_kv': _L3_xcond_in['Wss_kv'], 'L3_xcond_bss_kv': _L3_xcond_in['bss_kv']}

def reference(x, cond_1024, ctx_1024, mask_BxS2_ik0, L0_xcond_ln_gamma, L0_xcond_ln_beta, L0_xcond_Wq, L0_xcond_Wk, L0_xcond_Wv, L0_xcond_router_W, L0_xcond_router_b, L0_xcond_e_w1, L0_xcond_e_b1, L0_xcond_e_w2, L0_xcond_e_b2, L0_xcond_gate_w1, L0_xcond_gate_b1, L0_xcond_gate_w2, L0_xcond_gate_b2, L0_xcond_out_w, L0_xcond_out_b, L1_xcond_ln1_g, L1_xcond_ln1_b, L1_xcond_ln3_g, L1_xcond_ln3_b, L1_xcond_ln2_g, L1_xcond_ln2_b, L1_xcond_sa_wq, L1_xcond_sa_bq, L1_xcond_sa_wk, L1_xcond_sa_bk, L1_xcond_sa_wv, L1_xcond_sa_bv, L1_xcond_sa_wo, L1_xcond_sa_bo, L1_xcond_ca_wq, L1_xcond_ca_bq, L1_xcond_ca_wk, L1_xcond_ca_bk, L1_xcond_ca_wv, L1_xcond_ca_bv, L1_xcond_ca_wo, L1_xcond_ca_bo, L1_xcond_tp_w, L1_xcond_tp_b, L1_xcond_w1, L1_xcond_b1, L1_xcond_w2, L1_xcond_b2, L2_xcond_adaln_w, L2_xcond_adaln_b, L2_xcond_qkv_w, L2_xcond_qkv_b, L2_xcond_sa_proj_w, L2_xcond_sa_proj_b, L2_xcond_q_w, L2_xcond_q_b, L2_xcond_kv_w, L2_xcond_kv_b, L2_xcond_ca_proj_w, L2_xcond_ca_proj_b, L2_xcond_fc1_w, L2_xcond_fc1_b, L2_xcond_fc2_w, L2_xcond_fc2_b, L3_xcond_Wq, L3_xcond_bq, L3_xcond_Wkv, L3_xcond_bkv, L3_xcond_Wp, L3_xcond_bp, L3_xcond_Wss_q, L3_xcond_bss_q, L3_xcond_Wss_kv, L3_xcond_bss_kv):
    import jax
    import jax.numpy as jnp

    def _L0_xcond_ref(mix_hidden_states, global_anchor, prototype_bank, ln_gamma, ln_beta, Wq, Wk, Wv, router_W, router_b, e_w1, e_b1, e_w2, e_b2, gate_w1, gate_b1, gate_w2, gate_b2, out_w, out_b):
        import jax, jax.numpy as jnp
        import numpy as np
        H = 256
        RH = 2 * H
        E = 3
        B, T, P = (8, 512, 64)
        LN_EPS = 1e-05

        def _layer_norm(x, gamma, beta):
            mu = jnp.mean(x, axis=-1, keepdims=True)
            var = jnp.mean(jnp.square(x - mu), axis=-1, keepdims=True)
            return (x - mu) * jax.lax.rsqrt(var + LN_EPS) * gamma + beta
        x = mix_hidden_states
        nx = _layer_norm(x, ln_gamma, ln_beta)
        q = nx @ Wq
        k = prototype_bank @ Wk
        v = prototype_bank @ Wv
        scores = jnp.einsum('bth,bph->btp', q, k) * H ** (-0.5)
        weights = jax.nn.softmax(scores, axis=-1)
        evidence = jnp.einsum('btp,bph->bth', weights, v)
        anchor = jnp.broadcast_to(global_anchor[:, None, :], nx.shape)
        combined = jnp.concatenate([nx, evidence, anchor], axis=-1)
        router_logits = combined @ router_W + router_b
        router_probs = jax.nn.softmax(router_logits, axis=-1)
        h = jax.nn.silu(jnp.einsum('btc,ecr->bter', combined, e_w1) + e_b1)
        expert_out = jnp.einsum('bter,erh->bteh', h, e_w2) + e_b2
        routed = jnp.sum(expert_out * router_probs[..., None], axis=-2)
        g = jax.nn.sigmoid(jax.nn.silu(combined @ gate_w1 + gate_b1) @ gate_w2 + gate_b2)
        refined_delta = g * (routed @ out_w + out_b)
        return x + refined_delta

    def _L1_xcond_ref(x, t_emb, context_emb, mask, ln1_g, ln1_b, ln3_g, ln3_b, ln2_g, ln2_b, sa_wq, sa_bq, sa_wk, sa_bk, sa_wv, sa_bv, sa_wo, sa_bo, ca_wq, ca_bq, ca_wk, ca_bk, ca_wv, ca_bv, ca_wo, ca_bo, tp_w, tp_b, w1, b1, w2, b2):
        import jax, jax.numpy as jnp
        import numpy as np
        D = 256
        H = 16
        HD = D // H
        FF = 4 * D
        B, NQ, NK = (8, 256, 128)
        EPS = 1e-05

        def layernorm(x, g, b):
            m = jnp.mean(x, axis=-1, keepdims=True)
            v = jnp.mean(jnp.square(x - m), axis=-1, keepdims=True)
            return (x - m) * jax.lax.rsqrt(v + EPS) * g + b

        def mha(x, ctx, wq, bq, wk, bk, wv, bv, wo, bo, mask=None):
            Bq, Nq, _ = x.shape
            Nk = ctx.shape[1]
            q = (x @ wq + bq).reshape(Bq, Nq, H, HD)
            k = (ctx @ wk + bk).reshape(Bq, Nk, H, HD)
            v = (ctx @ wv + bv).reshape(Bq, Nk, H, HD)
            scores = jnp.einsum('bqhd,bkhd->bhqk', q, k) / np.sqrt(HD)
            if mask is not None:
                scores = jnp.where(mask[:, None, None, :].astype(bool), scores, -jnp.inf)
            attn = jax.nn.softmax(scores.astype(jnp.float32), axis=-1).astype(scores.dtype)
            out = jnp.einsum('bhqk,bkhd->bqhd', attn, v).reshape(Bq, Nq, D)
            return out @ wo + bo
        t_biases = jax.nn.silu(t_emb) @ tp_w + tp_b
        t_sa, t_ca, t_mlp = jnp.split(t_biases, 3, axis=-1)
        h = layernorm(x, ln1_g, ln1_b)
        h = mha(h, h, sa_wq, sa_bq, sa_wk, sa_bk, sa_wv, sa_bv, sa_wo, sa_bo)
        x = x + h + t_sa[:, None, :]
        h = layernorm(x, ln3_g, ln3_b)
        h = mha(h, context_emb, ca_wq, ca_bq, ca_wk, ca_bk, ca_wv, ca_bv, ca_wo, ca_bo, mask=mask)
        x = x + h + t_ca[:, None, :]
        h = layernorm(x, ln2_g, ln2_b)
        h = jax.nn.gelu(h @ w1 + b1, approximate=False) @ w2 + b2
        x = x + h + t_mlp[:, None, :]
        return x

    def _L2_xcond_ref(x, t_emb, context, adaln_w, adaln_b, qkv_w, qkv_b, sa_proj_w, sa_proj_b, q_w, q_b, kv_w, kv_b, ca_proj_w, ca_proj_b, fc1_w, fc1_b, fc2_w, fc2_b):
        import jax, jax.numpy as jnp
        import numpy as np
        D = 256
        H = 16
        HD = D // H
        MLP = 4 * D
        EPS = 1e-06
        SCALE = HD ** (-0.5)

        def _p(key, shape, s=0.02):
            return jax.random.normal(key, shape, dtype=jnp.float32) * s

        def _ln(x):
            mu = jnp.mean(x, axis=-1, keepdims=True)
            var = jnp.var(x, axis=-1, keepdims=True)
            return (x - mu) * jax.lax.rsqrt(var + EPS)

        def _heads(t):
            B, L, _ = t.shape
            return t.reshape(B, L, H, HD).transpose(0, 2, 1, 3)

        def _attend(q, k, v):
            attn = jnp.einsum('bhnd,bhsd->bhns', q, k) * SCALE
            attn = jax.nn.softmax(attn, axis=-1)
            o = jnp.einsum('bhns,bhsd->bhnd', attn, v)
            B, _, N, _ = q.shape
            return o.transpose(0, 2, 1, 3).reshape(B, N, D)
        B, N, _ = x.shape
        S = context.shape[1]
        mod = jax.nn.silu(t_emb) @ adaln_w + adaln_b
        sh_sa, sc_sa, g_sa, sh_ff, sc_ff, g_ff = jnp.split(mod[:, None, :], 6, axis=-1)
        xm = _ln(x) * (1.0 + sc_sa) + sh_sa
        qkv = (xm @ qkv_w + qkv_b).reshape(B, N, 3, H, HD)
        q = qkv[:, :, 0].transpose(0, 2, 1, 3)
        k = qkv[:, :, 1].transpose(0, 2, 1, 3)
        v = qkv[:, :, 2].transpose(0, 2, 1, 3)
        x_sa = _attend(q, k, v) @ sa_proj_w + sa_proj_b
        x = x + g_sa * x_sa
        xn = _ln(x)
        q = _heads(xn @ q_w + q_b)
        kv = (context @ kv_w + kv_b).reshape(B, S, 2, H, HD)
        k = kv[:, :, 0].transpose(0, 2, 1, 3)
        v = kv[:, :, 1].transpose(0, 2, 1, 3)
        x_ca = _attend(q, k, v) @ ca_proj_w + ca_proj_b
        x = x + x_ca
        xm = _ln(x) * (1.0 + sc_ff) + sh_ff
        h = jax.nn.gelu(xm @ fc1_w + fc1_b, approximate=True)
        x_ff = h @ fc2_w + fc2_b
        x = x + g_ff * x_ff
        return x

    def _L3_xcond_ref(x_q, x_kv, t_vec, Wq, bq, Wkv, bkv, Wp, bp, Wss_q, bss_q, Wss_kv, bss_kv):
        import jax, jax.numpy as jnp
        import numpy as np
        EPS = 1e-05

        def _ada_ln(x, c, W_ss, b_ss):
            mu = jnp.mean(x, axis=-1, keepdims=True)
            var = jnp.mean((x - mu) ** 2, axis=-1, keepdims=True)
            h = (x - mu) / jnp.sqrt(var + EPS)
            ss = jax.nn.silu(c) @ W_ss + b_ss
            scale, bias = jnp.split(ss, 2, axis=-1)
            return (1.0 + scale)[:, None, :] * h + bias[:, None, :]
        B, Lq, H = x_q.shape
        Lkv = x_kv.shape[1]
        nh = 16
        dh = H // nh
        xq = _ada_ln(x_q, t_vec, Wss_q, bss_q)
        xkv = _ada_ln(x_kv, t_vec, Wss_kv, bss_kv)
        q = (xq @ Wq + bq).reshape(B, Lq, nh, dh)
        kv = (xkv @ Wkv + bkv).reshape(B, Lkv, 2, nh, dh)
        k = kv[:, :, 0]
        v = kv[:, :, 1]
        scores = jnp.einsum('bqhd,bkhd->bhqk', q, k) / jnp.sqrt(jnp.float32(dh))
        attn = jax.nn.softmax(scores, axis=-1)
        out = jnp.einsum('bhqk,bkhd->bqhd', attn, v).reshape(B, Lq, H)
        return x_q + (out @ Wp + bp)
    x = _L0_xcond_ref(x, cond_1024, ctx_1024, L0_xcond_ln_gamma, L0_xcond_ln_beta, L0_xcond_Wq, L0_xcond_Wk, L0_xcond_Wv, L0_xcond_router_W, L0_xcond_router_b, L0_xcond_e_w1, L0_xcond_e_b1, L0_xcond_e_w2, L0_xcond_e_b2, L0_xcond_gate_w1, L0_xcond_gate_b1, L0_xcond_gate_w2, L0_xcond_gate_b2, L0_xcond_out_w, L0_xcond_out_b)
    x = _L1_xcond_ref(x, cond_1024, ctx_1024, mask_BxS2_ik0, L1_xcond_ln1_g, L1_xcond_ln1_b, L1_xcond_ln3_g, L1_xcond_ln3_b, L1_xcond_ln2_g, L1_xcond_ln2_b, L1_xcond_sa_wq, L1_xcond_sa_bq, L1_xcond_sa_wk, L1_xcond_sa_bk, L1_xcond_sa_wv, L1_xcond_sa_bv, L1_xcond_sa_wo, L1_xcond_sa_bo, L1_xcond_ca_wq, L1_xcond_ca_bq, L1_xcond_ca_wk, L1_xcond_ca_bk, L1_xcond_ca_wv, L1_xcond_ca_bv, L1_xcond_ca_wo, L1_xcond_ca_bo, L1_xcond_tp_w, L1_xcond_tp_b, L1_xcond_w1, L1_xcond_b1, L1_xcond_w2, L1_xcond_b2)
    x = _L2_xcond_ref(x, cond_1024, ctx_1024, L2_xcond_adaln_w, L2_xcond_adaln_b, L2_xcond_qkv_w, L2_xcond_qkv_b, L2_xcond_sa_proj_w, L2_xcond_sa_proj_b, L2_xcond_q_w, L2_xcond_q_b, L2_xcond_kv_w, L2_xcond_kv_b, L2_xcond_ca_proj_w, L2_xcond_ca_proj_b, L2_xcond_fc1_w, L2_xcond_fc1_b, L2_xcond_fc2_w, L2_xcond_fc2_b)
    x = _L3_xcond_ref(x, ctx_1024, cond_1024, L3_xcond_Wq, L3_xcond_bq, L3_xcond_Wkv, L3_xcond_bkv, L3_xcond_Wp, L3_xcond_bp, L3_xcond_Wss_q, L3_xcond_bss_q, L3_xcond_Wss_kv, L3_xcond_bss_kv)
    return x

_drawn_inputs = setup_inputs


def setup_inputs(seed=0):
    import zlib

    import numpy as np

    out = dict(_drawn_inputs(seed))
    spreads = {'L0_xcond_ln_gamma': (1.0, 0.583),
     'L0_xcond_ln_beta': (0.0, 0.69),
     'L0_xcond_router_b': (0.0, 0.8),
     'L0_xcond_e_b1': (0.0, 0.452),
     'L0_xcond_e_b2': (0.0, 0.288),
     'L0_xcond_gate_b1': (0.0, 0.8),
     'L0_xcond_gate_b2': (0.0, 0.8),
     'L0_xcond_out_b': (0.0, 0.1),
     'L1_xcond_ln1_g': (1.0, 0.6),
     'L1_xcond_ln1_b': (0.0, 0.72),
     'L1_xcond_ln3_g': (1.0, 0.6),
     'L1_xcond_ln3_b': (0.0, 0.8),
     'L1_xcond_ln2_g': (1.0, 0.6),
     'L1_xcond_ln2_b': (0.0, 0.8),
     'L1_xcond_sa_bq': (0.0, 0.8),
     'L1_xcond_sa_bk': (0.0, 2.0),
     'L1_xcond_sa_bv': (0.0, 0.27),
     'L1_xcond_sa_bo': (0.0, 0.1),
     'L1_xcond_ca_bq': (0.0, 0.8),
     'L1_xcond_ca_bk': (0.0, 2.0),
     'L1_xcond_ca_bv': (0.0, 0.292),
     'L1_xcond_ca_bo': (0.0, 0.1),
     'L1_xcond_tp_b': (0.0, 0.1),
     'L1_xcond_b1': (0.0, 0.1),
     'L1_xcond_b2': (0.0, 0.1),
     'L3_xcond_bq': (0.0, 2.0),
     'L3_xcond_bkv': (0.0, 0.285),
     'L3_xcond_bp': (0.0, 0.1),
     'L3_xcond_bss_q': (0.0, 2.0),
     'L3_xcond_bss_kv': (0.0, 0.783)}
    factors = {'L1_xcond_sa_wq': 8.0,
     'L1_xcond_sa_wk': 8.0,
     'L1_xcond_sa_wv': 3.588,
     'L1_xcond_ca_wq': 8.0,
     'L1_xcond_ca_wk': 8.0,
     'L2_xcond_adaln_b': 8.0,
     'L2_xcond_qkv_w': 6.432,
     'L2_xcond_qkv_b': 8.0,
     'L2_xcond_sa_proj_w': 7.351,
     'L2_xcond_sa_proj_b': 8.0,
     'L2_xcond_q_w': 43.717,
     'L2_xcond_q_b': 64.0,
     'L2_xcond_kv_b': 8.0,
     'L2_xcond_ca_proj_b': 3.261,
     'L2_xcond_fc1_w': 2.973,
     'L2_xcond_fc1_b': 8.0,
     'L2_xcond_fc2_w': 2.897,
     'L2_xcond_fc2_b': 8.0,
     'L3_xcond_Wq': 8.0,
     'L3_xcond_Wss_q': 8.0,
     'L3_xcond_Wss_kv': 2.819}
    for name, (base, spread) in spreads.items():
        noise = np.random.default_rng([zlib.crc32(name.encode()), seed]).standard_normal(out[name].shape)
        drawn = base * np.exp(spread * noise) if base else spread * noise
        out[name] = jnp.asarray(drawn.astype(out[name].dtype))
    for name, factor in factors.items():
        out[name] = (out[name] * factor).astype(out[name].dtype)
    return out
```

```python
from contextlib import ExitStack

import concourse.bass as bass
from concourse import mybir

F32 = mybir.dt.float32
F32R = mybir.dt.float32r
I32 = mybir.dt.int32
ACT = mybir.ActivationFunctionType
ALU = mybir.AluOpType
AX = mybir.AxisListType

P = 128
B, N, D, S = 4, 1024, 256, 77
KC = D // P
NT = N // P
HALF = 512
NH = N // HALF
TPH = HALF // P
HEADS, HD = 16, 16
GH = 4
GROUPS = HEADS // GH
SP_ = S + 1
E, RH = 3, 512
RM = E * RH // P
GM = D // P
FF = 4 * D
FM = FF // P
STACK = 64
MAXROW = 32
PAIRS = HEADS // 2
NSEL = 2 * 2 * (PAIRS // KC)
SEL = {"q": 0, "k": NSEL // 2}
MASKED = -1.0e30
SCALE = HD ** -0.5

COLS = [("L0_ln_gamma", 2), ("L0_ln_beta", 2), ("L0_e_b1", RM), ("L0_gate_b1", GM),
        ("L1_ln1_g", 2), ("L1_ln1_b", 2), ("L1_ln3_g", 2), ("L1_ln3_b", 2), ("L1_ln2_g", 2), ("L1_ln2_b", 2),
        ("L1_sa_bq", 2), ("L1_sa_bk", 2), ("L1_sa_bv", 2), ("L1_ca_bq", 2), ("L1_ca_bk", 2), ("L1_ca_bv", 2),
        ("L1_b1", FM), ("L2_adaln_b", 12), ("L2_qkv_b", 6), ("L2_q_b", 2), ("L2_kv_b", 4), ("L2_fc1_b", FM),
        ("L3_bq", 2), ("L3_bkv", 4), ("L3_bss_q", 4), ("L3_bss_kv", 4)]
COL, NCOL = {}, 0
for _n, _c in COLS:
    COL[_n] = NCOL
    NCOL += _c
ROWS = ["out_b", "gate_b2", "sa_bo", "tp_b0", "tp_b1", "tp_b2", "ca_bo", "b2", "sa_proj_b", "g_sa", "g_ff",
        "ca_proj_b", "fc2_b", "bp", "router_b"]
ROW = {n: i for i, n in enumerate(ROWS)}
NROW = len(ROWS)


class Marks:

    def __init__(self, known=None):
        self.known, self.count, self.at, self.bank = known, {}, {}, {}
        self.start, self.total = {}, {}

    def add(self, sem, step=None, by=1):
        self.count[sem.name] = self.count.get(sem.name, 0) + by
        if step is not None:
            assert (sem.name, step) not in self.at, step
            self.at[sem.name, step] = self.count[sem.name]
        return by

    def open(self, loop):
        self.before = dict(self.count)
        for name, n in self.count.items():
            self.start.setdefault((loop, name), n)

    def close(self, loop):
        for name, n in self.count.items():
            body = n - self.before.get(name, 0)
            if body:
                self.total[loop, name] = body
                self.count[name] += (B - 1) * body

    def upto(self, loop, it, sem, steps):
        if self.known is None:
            return it + 1
        k = self.known
        n = max([k.at[sem.name, step] for step in steps] or [k.start[loop, sem.name]])
        total = k.total.get((loop, sem.name), 0)
        return it * total + n if total else n

    def put(self, step, bank):
        self.bank[step] = bank

    def where(self, step):
        return 0 if self.known is None else self.known.bank[step]


def attention_schedule(cross):
    def stacks(pairs):
        out = []
        for pair in pairs:
            out += [("q", pair, 0), ("k", pair, 0)]
        for pair in pairs:
            out += [("q", pair, 1)] + [("k", pair, 1)] * (not cross)
        return out

    if cross:
        first = [("K", ("act", "dve")[i % 2]) + k for i, k in enumerate(stacks(range(HEADS // 2)))]
        later, maxima = [], []
        for n in range(NH):
            maxima += [("A", g, n, t, 0) for g in range(GROUPS) for t in range(TPH)] + [("M", 0, n)]
        units = [(g, n, 0) for n in range(NH) for g in range(GROUPS)]
        ahead, rate = len(maxima) // 2 + 2, 4
    else:
        first = [("K", "act" if k[0] == "q" else "dve") + k for k in stacks((0, 1))]
        later = [("K", "act") + k for g in range(1, GROUPS) for k in stacks((2 * g, 2 * g + 1))]
        maxima = []
        for g in range(GROUPS):
            for n in range(NH):
                maxima += [("A", g, n, t, j) for t in range(TPH) for j in range(GH)]
                if g or n:
                    maxima.insert(len(maxima) - TPH * GH + 2, ("M",) + divmod(NH * g + n - 1, NH))
        maxima.append(("M", GROUPS - 1, NH - 1))
        units = [(g, n, kt) for g in range(GROUPS) for n in range(NH) for kt in range(NT)]
        ahead, rate = 24, 17 / NT
    steps = list(first)
    taken = 0

    def more(upto):
        nonlocal taken
        upto = min(int(upto), len(maxima))
        out = maxima[taken:upto]
        taken = max(taken, upto)
        return out

    lead = more(ahead)
    per = -(-len(later) // len(lead))
    for i, step in enumerate(lead):
        steps += [step] + later[i * per:(i + 1) * per]
    pv, o, turn = None, None, None
    for u, unit in enumerate(units):
        steps += more(ahead + rate * (u + 0.5)) + [("S",) + unit + (j,) for j in range(2)]
        steps += more(ahead + rate * (u + 1)) + [("S",) + unit + (j,) for j in range(2, GH)]
        if turn is not None:
            steps.append(("OT",) + turn)
            turn = None
        if u:
            last = units[u - 1]
            steps.append(("PV",) + last)
            if last[:2] != unit[:2]:
                steps.append(("O",) + last[:2])
                turn = last[:2]
    steps += more(len(maxima))
    if turn is not None:
        steps.append(("OT",) + turn)
    steps += [("PV",) + units[-1], ("O",) + units[-1][:2], ("OT",) + units[-1][:2]]
    return steps


SELF, CROSS = attention_schedule(False), attention_schedule(True)


def stacked(e, lo, hi):
    return slice(STACK * e + lo, STACK * e + hi)


def stacks_for(cross, engine, g, n):
    return [k for k in (CROSS if cross else SELF) if k[0] == "K" and k[1] == engine
            and k[3] * 2 // GH == g and (k[2] == "k" or k[4] == n)]


def selections():
    import numpy as np

    out = np.zeros((P, NSEL, P), np.float32)
    for which, places in (("q", ((0, 16), (48,))), ("k", ((0, 48), (16,)))):
        for part in range(2):
            for pp in range(PAIRS // KC):
                for e in range(2):
                    for row in places[part]:
                        for d in range(HD):
                            out[(2 * pp + e) * HD + d, SEL[which] + part * (PAIRS // KC) + pp, STACK * e + row + d] = 1.0
    return out


def build(nc, T, M):
    ctx = ExitStack()
    with ctx:
        at = [16512]

        def place(name, shape, dt=F32, offset=None):
            size = 4
            for d in shape[1:]:
                size *= d
            size = -(-size // 32) * 32
            if offset is None:
                offset = at[0]
                at[0] += size
            return nc.alloc_sbuf_tensor_at(name, shape, dt, offset=offset)

        def sem(name):
            return ctx.enter_context(nc.semaphore(name))

        r1 = at[0]
        qs = place("qs", [P, PAIRS, N], F32R)
        ks = place("ks", [P, PAIRS, N], F32R)
        r1_end, at[0] = at[0], r1
        ew1 = place("ew1", [P, 6, E, RH])
        ew2 = place("ew2", [P, RM, D])
        gw1 = place("gw1", [P, 6, D])
        gw2 = place("gw2", [P, KC, D])
        outw = place("outw", [P, KC, D])
        wqT = place("wqT", [P, KC, D])
        wk0 = place("wk0", [P, KC, D])
        wv0 = place("wv0", [P, KC, D])
        assert at[0] <= r1_end
        at[0] = r1_end
        r2 = at[0]
        probs = place("probs", [P, 4, GH, HALF])
        r2_end, at[0] = at[0], r2
        qh = place("qh", [P, KC, N], F32R)
        ql = place("ql", [P, KC, N], F32R)
        kh = place("kh", [P, KC, N], F32R)
        kl = place("kl", [P, KC, N], F32R)
        assert at[0] <= r2_end
        at[0] = r2
        hid = place("hid", [P, NH, FM, HALF])
        at[0] = r2
        hid0 = place("hid0", [P, RM + GM, HALF])
        at[0] = r2
        sel_in = place("sel_in", [P, NSEL, P])
        at[0] = r2_end
        x = place("x", [P, NT, D])
        hT = place("hT", [P, KC, N])
        tok = place("tok", [P, NT, D])
        pb = place("pb", [P, E, HALF], offset=at[0] - 4 * NT * D)
        v = place("v", [P, NT, HEADS, 32])
        ow = place("ow", [P, N])
        wT = place("wT", [P, N], offset=at[0] - 4 * N)
        rT = place("rT", [P, KC, HALF])
        mrow = place("mrow", [P, N], offset=at[0] - 4 * N)
        slot = [place(f"slot{i}", [P, 2048]) for i in range(4)]
        after_slots, at[0] = at[0], at[0] - 3 * 4 * 2048
        u0 = place("u0", [P, RM * P + D + E])
        pT = place("pT", [E, N])
        kv0T = place("kv0T", [P, 2 * KC, SP_])
        a0 = place("a0", [P, KC, SP_])
        e1 = place("e1", [P, TPH, SP_])
        eb2 = place("eb2", [E, D])
        assert at[0] <= after_slots
        at[0] = after_slots
        adw = place("adw", [P, KC, 6 * D])
        tpw = place("tpw", [P, KC, 3 * D], offset=at[0] - 4 * KC * 6 * D)
        ident = place("ident", [P, P])
        sel = place("sel", [P, NSEL, P], F32R)
        cols = place("cols", [P, NCOL])
        rows = place("rows", [NROW, D])
        router = place("router", [P, 6, E])
        cond = place("cond", [P, KC])
        scond = place("scond", [P, KC])
        ctxT = place("ctxT", [P, KC, SP_])
        ctxk = place("ctxk", [S, D])
        kvT = place("kvT", [P, KC, SP_])
        e0 = place("e0", [P, TPH, SP_])
        e01 = (e0, e1)
        small = place("small", [P, 128])
        mi = place("mi", [P, SP_], I32)
        mic = place("mic", [S, 1], I32)
        mrowb, mcolb = place("mrowb", [P, SP_]), place("mcolb", [S, 1])
        mx = place("mx", [P, 2, TPH, HEADS])
        grow = place("grow", [P, D])
        rrow = place("rrow", [P, D])
        sg = place("sg", [P, 2, 2, D], offset=r2_end - 4 * N)
        assert 4 * (RM + GM) * HALF + 4 * N <= r2_end - r2

        st = small[:, 0:6 * NT].rearrange("p (t k) -> p t k", k=6)
        mv = small[:, 48:48 + 2 * NT].rearrange("p (t k) -> p t k", k=2)
        ve, rstd, nhalf = small[:, 64:72], small[:, 72:80], small[:, 80:88]
        b0 = small[:, 88:88 + RM + GM]
        nmx, es, rc4 = small[:, 102:110], small[:, 110:118], small[:, 118:126]
        lg = place("lg", [P, NT, E])
        ones_col = small[:, 126:127]
        rc = place("rc", [P, TPH * GH])
        rmx, rs, rrs = place("rmx", [P, NT]), place("rs", [P, NT]), place("rrs", [P, NT])
        mod = place("mod", [P, 12])
        mod3 = place("mod3", [P, 8])
        stc, mvc = place("stc", [S, 6]), place("mvc", [S, 2])
        vec, rstdc = place("vec", [S, 1]), place("rstdc", [S, 1])
        assert at[0] <= 229368, at[0]

        ps = ctx.enter_context(nc.psum_tensor("ps", [P, 8, HALF], F32))

        def w256(i, k, n=D):
            return slot[i][:, 512 * k:512 * k + KC * n].rearrange("p (c n) -> p c n", c=KC)

        W1 = slot[2][:].rearrange("p (c n) -> p c n", c=KC)
        W2 = slot[3][:].rearrange("p (c n) -> p c n", c=FM)

        mm_done, act_done, dve_done, pool_done = sem("mm_done"), sem("act_done"), sem("dve_done"), sem("pool_done")
        constants_loaded, constants_set = sem("constants_loaded"), sem("constants_set")
        experts_loaded = {name: sem(f"experts_{name}_loaded") for name in ("kv", "q", "in", "out")}
        x_loaded, conditions_loaded = sem("x_loaded"), sem("conditions_loaded")
        slot_loaded = [sem(f"slot{i}_loaded") for i in range(5)]
        maxima_stacked = [[sem(f"maxima_{g}_{n}_stacked") for n in range(NH)] for g in range(GROUPS)]
        x_stored, out_stored = sem("x_stored"), sem("out_stored")

        block = ctx.enter_context(nc.Block())

        def col(name, c):
            return cols[:, COL[name] + c:COL[name] + c + 1]

        ATT = {
            "L1sa": (False, w256(0, 0), w256(0, 1), w256(0, 2), w256(0, 3), ("L1_sa_bq", 0), ("L1_sa_bk", 0), ("L1_sa_bv", 0)),
            "L1ca": (True, w256(1, 0), w256(1, 1), w256(1, 2), w256(1, 3), ("L1_ca_bq", 0), ("L1_ca_bk", 0), ("L1_ca_bv", 0)),
            "L2sa": (False, w256(0, 0, 768)[:, :, 0:D], w256(0, 0, 768)[:, :, D:2 * D], w256(0, 0, 768)[:, :, 2 * D:],
                     w256(0, 3), ("L2_qkv_b", 0), ("L2_qkv_b", 2), ("L2_qkv_b", 4)),
            "L2ca": (True, w256(1, 0), w256(1, 1, 512)[:, :, 0:D], w256(1, 1, 512)[:, :, D:], w256(1, 3),
                     ("L2_q_b", 0), ("L2_kv_b", 0), ("L2_kv_b", 2)),
            "L3ca": (True, w256(2, 0), w256(2, 1, 512)[:, :, 0:D], w256(2, 1, 512)[:, :, D:], w256(2, 3),
                     ("L3_bq", 0), ("L3_bkv", 0), ("L3_bkv", 2)),
        }
        SLOT_OF = {"L1sa": slot_loaded[0], "L1ca": slot_loaded[1], "L2sa": slot_loaded[0], "L2ca": slot_loaded[1],
                   "L3ca": slot_loaded[2]}
        LN_OF = {"L1sa": "ln1", "L1ca": "ln3", "L2sa": "ln4", "L2ca": "ln5", "L3ca": "ln7"}
        XNEXT = {"ln3": "L1sa", "ln2": "L1ca", "ln4": "L1mlp", "ln5": "L2sa", "ln6": "L2ca", "ln7": "L2mlp"}
        LOADED = 16

        def wide(src):
            return src.rearrange("(c p) n -> p c n", p=P)

        def maxima_of(tag, g, n):
            return (n, HEADS, GH * g, ("M", 0, n)) if ATT[tag][0] else ((NH * g + n) % 2, GH, 0, ("M", g, n))

        @block.sync
        def _(sp):
            sp.dma_start(ident[:], T["ident"]).then_inc(constants_loaded, LOADED)
            sp.dma_start(router[:], wide(T["router_W"])).then_inc(constants_loaded, LOADED)
            sp.dma_start(cols[:], T["cols"]).then_inc(constants_loaded, LOADED)
            sp.dma_start(rows[:], T["rows"]).then_inc(constants_loaded, LOADED)
            sp.dma_start(eb2[:], T["e_b2"]).then_inc(constants_loaded, LOADED)
            sp.dma_start(sel_in[:], T["sel"]).then_inc(constants_loaded, LOADED)
            inner = [(ew1[:, c], T["L0_e_w1"][:, c * P:(c + 1) * P, :].rearrange("e p r -> p e r")) for c in (2, 3, 4, 5, 0, 1)]
            outer = [(ew2[:, e * 4:(e + 1) * 4], wide(T["L0_e_w2"][e])) for e in range(E)]
            for name, parts in (("kv", [(wk0[:], wide(T["L0_Wk"])), (wv0[:], wide(T["L0_Wv"]))]),
                                ("q", [(wqT[:], wide(T["L0_WqT"]))]),
                                ("in", inner + [(gw1[:], wide(T["L0_gate_w1"]))]),
                                ("out", outer + [(gw2[:], wide(T["L0_gate_w2"])), (outw[:], wide(T["L0_out_w"]))])):
                for i, (dst, src) in enumerate(parts):
                    sp.dma_start(dst, src).then_inc(experts_loaded[name], M.add(experts_loaded[name], i, LOADED))
            for k, n in enumerate(("wq", "wk", "wv", "wo")):
                sp.dma_start(w256(0, k), wide(T[f"L1_sa_{n}"])).then_inc(slot_loaded[0], M.add(slot_loaded[0], ("L1sa", k), LOADED))
            M.open("blocks")
            with sp.Fori(0, B) as it:
                def upto(sem, *steps):
                    return M.upto("blocks", it, sem, steps)

                sp.wait_ge(mm_done, upto(mm_done))
                sp.dma_start(tpw[:], wide(T["L1_tp_w"])).then_inc(slot_loaded[4], M.add(slot_loaded[4], "L1", LOADED))
                for k, n in enumerate(("wq", "wk", "wv", "wo")):
                    sp.dma_start(w256(1, k), wide(T[f"L1_ca_{n}"])).then_inc(slot_loaded[1], M.add(slot_loaded[1], ("L1ca", k), LOADED))
                sp.dma_start(W1, wide(T["L1_w1"])).then_inc(slot_loaded[2], M.add(slot_loaded[2], "L1mlp", LOADED))
                sp.dma_start(W2, wide(T["L1_w2"])).then_inc(slot_loaded[3], M.add(slot_loaded[3], "L1mlp", LOADED))

                def stack_maxima(tag):
                    if ATT[tag][0]:
                        order = [(g, n) for n in range(NH) for g in range(GROUPS)]
                    else:
                        order = [(g, n) for g in range(GROUPS) for n in range(NH)]
                    for g, n in order:
                        z, _, j0, step = maxima_of(tag, g, n)
                        sp.wait_ge(act_done, upto(act_done, (tag,) + step))
                        for j in range(GH):
                            h = GH * g + j
                            sp.dma_start(qs[stacked(h % 2, MAXROW, MAXROW + 1), h // 2, n * HALF:(n + 1) * HALF].bitcast(F32),
                                         mrow[j0 + j:j0 + j + 1, z * HALF:(z + 1) * HALF]
                                         ).then_inc(maxima_stacked[g][n], M.add(maxima_stacked[g][n], (tag, j), LOADED))

                stack_maxima("L1sa")
                sp.wait_ge(mm_done, upto(mm_done, ("L1sa", "o", 3)))
                sp.dma_start(w256(0, 0, 768), wide(T["L2_qkv_w"])).then_inc(slot_loaded[0], M.add(slot_loaded[0], ("L2sa", 0), LOADED))
                sp.dma_start(w256(0, 3), wide(T["L2_sa_proj_w"])).then_inc(slot_loaded[0], M.add(slot_loaded[0], ("L2sa", 3), LOADED))
                stack_maxima("L1ca")
                sp.wait_ge(mm_done, upto(mm_done, ("L1ca", "o", 3)))
                sp.dma_start(w256(1, 0), wide(T["L2_q_w"])).then_inc(slot_loaded[1], M.add(slot_loaded[1], ("L2ca", 0), LOADED))
                sp.dma_start(w256(1, 1, 512), wide(T["L2_kv_w"])).then_inc(slot_loaded[1], M.add(slot_loaded[1], ("L2ca", 1), LOADED))
                sp.dma_start(w256(1, 3), wide(T["L2_ca_proj_w"])).then_inc(slot_loaded[1], M.add(slot_loaded[1], ("L2ca", 3), LOADED))
                sp.wait_ge(mm_done, upto(mm_done, ("row", "L1mlp")))
                sp.dma_start(adw[:], wide(T["L2_adaln_w"])).then_inc(slot_loaded[4], M.add(slot_loaded[4], "L2", LOADED))
                sp.wait_ge(mm_done, upto(mm_done, ("L1mlp", "h", NH - 1, FM - 1)))
                sp.dma_start(W1, wide(T["L2_fc1_w"])).then_inc(slot_loaded[2], M.add(slot_loaded[2], "L2mlp", LOADED))
                sp.wait_ge(mm_done, upto(mm_done, ("L1mlp", "o", 3)))
                sp.dma_start(W2, wide(T["L2_fc2_w"])).then_inc(slot_loaded[3], M.add(slot_loaded[3], "L2mlp", LOADED))
                stack_maxima("L2sa")
                sp.wait_ge(mm_done, upto(mm_done, ("L2sa", "o", 3)))
                for k, n in enumerate(("wq", "wk", "wv", "wo")):
                    sp.dma_start(w256(0, k), wide(T[f"L1_sa_{n}"])).then_inc(slot_loaded[0], M.add(slot_loaded[0], None, LOADED))
                stack_maxima("L2ca")
                sp.wait_ge(mm_done, upto(mm_done, ("L2ca", "o", 3)))
                sp.dma_start(w256(1, 0, 512), wide(T["L3_Wss_q"])).then_inc(slot_loaded[1], M.add(slot_loaded[1], None, LOADED))
                sp.dma_start(w256(1, 2, 512), wide(T["L3_Wss_kv"])).then_inc(slot_loaded[1], M.add(slot_loaded[1], "L3ss", LOADED))
                sp.wait_ge(mm_done, upto(mm_done, ("L2mlp", "h", NH - 1, FM - 1)))
                sp.dma_start(w256(2, 0), wide(T["L3_Wq"])).then_inc(slot_loaded[2], M.add(slot_loaded[2], ("L3ca", 0), LOADED))
                sp.dma_start(w256(2, 1, 512), wide(T["L3_Wkv"])).then_inc(slot_loaded[2], M.add(slot_loaded[2], ("L3ca", 1), LOADED))
                sp.dma_start(w256(2, 3), wide(T["L3_Wp"])).then_inc(slot_loaded[2], M.add(slot_loaded[2], ("L3ca", 3), LOADED))
                stack_maxima("L3ca")
            M.close("blocks")

        @block.tensor
        def _(pe):
            owner = {}
            ring = [0]

            def mm(out, lhsT, rhs, start=True, stop=True):
                return pe.matmul(out, lhsT, rhs, start=start, stop=stop)

            def take(step, act=None, dve=None, banks=None):
                if banks is None:
                    banks = (ring[0] % 8,)
                    ring[0] += 1
                was = [owner[b] for b in banks if b in owner]
                for b in banks:
                    owner[b] = ("act", act) if act else ("dve", dve)
                M.put(step, banks[0])
                return banks[0], [s for e, s in was if e == "act"], [s for e, s in was if e == "dve"]

            def pick(name):
                r = ROW[name]
                return ident[0:NROW, r:r + 1].to_broadcast([NROW, P]), rows[:]

            def turn(upto, tag):
                for n in range(NH):
                    for c in range(KC):
                        b, act_was, dve_was = take((tag, "T", n, c), act=(tag, "hT", n, c))
                        pe.wait_ge(act_done, upto(act_done, *act_was))
                        for i in range(TPH):
                            t = TPH * n + i
                            pe.wait_ge(dve_done, upto(dve_done, (tag, "xh", t), *dve_was))
                            ins = pe.transpose(ps[:, b, i * P:(i + 1) * P], tok[:, t, c * P:(c + 1) * P], ident[:])
                        ins.then_inc(mm_done, M.add(mm_done, (tag, "T", n, c)))

            pe.wait_ge(constants_loaded, 6 * LOADED)
            pe.wait_ge(dve_done, 1)
            pe.transpose(ps[:, 0, 0:P], ident[:], ident[:]).then_inc(mm_done, M.add(mm_done))
            M.open("experts")
            with pe.Fori(0, B) as it:
                def upto(sem, *steps):
                    return M.upto("experts", it, sem, steps)

                b, act_was, dve_was = take(("L0", "kv"), act=("L0", "kv"))
                pe.wait_ge(act_done, upto(act_done))
                pe.wait_ge(dve_done, upto(dve_done))
                pe.wait_ge(conditions_loaded, upto(conditions_loaded, "experts"))
                pe.wait_ge(experts_loaded["kv"], 2 * LOADED)
                for i, w in enumerate((wk0, wv0)):
                    for c in range(KC):
                        o = (i * KC + c) * SP_
                        for k in range(KC):
                            ins = mm(ps[:, b, o:o + SP_], w[:, k, c * P:(c + 1) * P], ctxT[:, k, :], k == 0, k == KC - 1)
                ins.then_inc(mm_done, M.add(mm_done, ("L0", "kv")))
                b, act_was, dve_was = take(("L0", "a"), act=("L0", "a"))
                pe.wait_ge(act_done, upto(act_done, ("L0", "kv")))
                pe.wait_ge(experts_loaded["q"], LOADED)
                for c in range(KC):
                    for k in range(KC):
                        ins = mm(ps[:, b, c * SP_:(c + 1) * SP_], wqT[:, k, c * P:(c + 1) * P], kv0T[:, k, :], k == 0, k == KC - 1)
                ins.then_inc(mm_done, M.add(mm_done, ("L0", "a")))
                turn(upto, "ln0")
                for e in range(E + 1):
                    b, act_was, dve_was = take(("L0", "u", e), dve=("L0", "u", e))
                    pe.wait_ge(act_done, upto(act_done, *act_was))
                    pe.wait_ge(dve_done, upto(dve_done, *dve_was))
                    pe.wait_ge(experts_loaded["in"], 7 * LOADED)
                    for k in range(KC):
                        if e < E:
                            ins = mm(ps[0:S, b, :], kv0T[:, KC + k, 0:S], ew1[:, KC + k, e, :], k == 0, k == KC - 1)
                        else:
                            mm(ps[0:S, b, 0:D], kv0T[:, KC + k, 0:S], gw1[:, KC + k, :], k == 0, k == KC - 1)
                    if e == E:
                        for k in range(KC):
                            ins = mm(ps[0:S, b, D:D + E], kv0T[:, KC + k, 0:S], router[:, KC + k, :], k == 0, k == KC - 1)
                    ins.then_inc(mm_done, M.add(mm_done, ("L0", "u", e)))
                b, act_was, dve_was = take(("L0", "b"), dve=("L0", "b"))
                pe.wait_ge(act_done, upto(act_done, *act_was))
                pe.wait_ge(dve_done, upto(dve_done, *dve_was))
                for m in range(RM + GM):
                    for k in range(KC):
                        w = ew1[:, 2 * KC + k, m // 4, (m % 4) * P:(m % 4 + 1) * P] if m < RM else gw1[:, 2 * KC + k, (m - RM) * P:(m - RM + 1) * P]
                        ins = mm(ps[:, b, m:m + 1], w, cond[:, k:k + 1], k == 0, k == KC - 1)
                ins.then_inc(mm_done, M.add(mm_done, ("L0", "b")))
                for n in range(NH):
                    b, act_was, dve_was = take(("L0", "s", n), act=("L0", "e", n, TPH - 1))
                    pe.wait_ge(act_done, upto(act_done, ("L0", "a"), *(("ln0", "hT", n, c) for c in range(KC)), *act_was))
                    pe.wait_ge(dve_done, upto(dve_done, *dve_was))
                    for i in range(TPH):
                        t = TPH * n + i
                        for k in range(KC):
                            ins = mm(ps[:, b, i * SP_:i * SP_ + S], hT[:, k, t * P:(t + 1) * P], a0[:, k, 0:S], k == 0, k == KC - 1)
                    ins.then_inc(mm_done, M.add(mm_done, ("L0", "s", n)))
                for n in range(NH):
                    b, act_was, dve_was = take(("L0", "wT", n), act=("L0", "wT", n))
                    pe.wait_ge(act_done, upto(act_done, *act_was))
                    pe.wait_ge(dve_done, upto(dve_done, ("L0", "w", n), *dve_was))
                    for i in range(TPH):
                        ins = pe.transpose(ps[0:S, b, i * P:(i + 1) * P], e01[n][:, i, 0:S], ident[:])
                    ins.then_inc(mm_done, M.add(mm_done, ("L0", "wT", n)))
                b, act_was, dve_was = take(("L0", "r"), dve=("L0", "lg"))
                pe.wait_ge(act_done, upto(act_done, ("L0", "wT", NH - 1), *act_was))
                pe.wait_ge(dve_done, upto(dve_done, ("L0", "u", E), ("L0", "b"), *dve_was))
                for t in range(NT):
                    tt = slice(t * P, (t + 1) * P)
                    o = ps[:, b, t * E:(t + 1) * E]
                    for k in range(KC):
                        mm(o, hT[:, k, tt], router[:, k, :], k == 0, False)
                        mm(o, cond[:, k:k + 1].to_broadcast([P, P]), router[:, 2 * KC + k, :], False, False)
                    mm(o, wT[0:S, tt], u0[0:S, RM * P + D:], False, False)
                    lhs, rr = pick("router_b")
                    ins = mm(o, lhs, rr[:, 0:E], False, True)
                ins.then_inc(mm_done, M.add(mm_done, ("L0", "r")))
                for n in range(NH):
                    half = slice(n * HALF, (n + 1) * HALF)
                    for m in range(RM + GM):
                        b, act_was, dve_was = take(("L0", "h", n, m), act=("L0", "h", n, m))
                        pe.wait_ge(act_done, upto(act_done, *act_was))
                        pe.wait_ge(dve_done, upto(dve_done, *dve_was))
                        for k in range(KC):
                            w = ew1[:, k, m // 4, (m % 4) * P:(m % 4 + 1) * P] if m < RM else gw1[:, k, (m - RM) * P:(m - RM + 1) * P]
                            mm(ps[:, b, :], w, hT[:, k, half], k == 0, False)
                        ins = mm(ps[:, b, :], u0[0:S, m * P:(m + 1) * P], wT[0:S, half], False, True)
                        ins.then_inc(mm_done, M.add(mm_done, ("L0", "h", n, m)))
                        if m < E:
                            b, act_was, dve_was = take(("L0", "pb", n, m), act=("L0", "pb", n, m))
                            pe.wait_ge(act_done, upto(act_done, *act_was))
                            pe.wait_ge(dve_done, upto(dve_done, ("L0", "p"), *dve_was))
                            for i in range(TPH):
                                ins = mm(ps[:, b, i * P:(i + 1) * P], lg[:, TPH * n + i, m:m + 1].to_broadcast([P, P]), ident[:])
                            ins.then_inc(mm_done, M.add(mm_done, ("L0", "pb", n, m)))
                        if m == E:
                            b, act_was, dve_was = take(("L0", "pT", n), act=("L0", "pT", n))
                            pe.wait_ge(act_done, upto(act_done, *act_was))
                            pe.wait_ge(dve_done, upto(dve_done, *dve_was))
                            for i in range(TPH):
                                ins = pe.transpose(ps[0:E, b, i * P:(i + 1) * P], lg[:, TPH * n + i, :], ident[:])
                            ins.then_inc(mm_done, M.add(mm_done, ("L0", "pT", n)))
                    for i2 in range(2):
                        t2 = 2 * n + i2
                        b, act_was, dve_was = take(("L0", "g", t2), act=("L0", "g", t2))
                        pe.wait_ge(act_done, upto(act_done, *(("L0", "h", n, RM + c) for c in range(KC)), *act_was))
                        pe.wait_ge(dve_done, upto(dve_done, *dve_was))
                        pe.wait_ge(experts_loaded["out"], 5 * LOADED)
                        for i in range(2):
                            tt = slice((2 * i2 + i) * P, (2 * i2 + i + 1) * P)
                            mm(ps[:, b, i * D:(i + 1) * D], *pick("gate_b2"), True, False)
                            for k in range(KC):
                                ins = mm(ps[:, b, i * D:(i + 1) * D], hid0[:, RM + k, tt], gw2[:, k, :], False, k == KC - 1)
                        ins.then_inc(mm_done, M.add(mm_done, ("L0", "g", t2)))
                    for c in range(KC):
                        b, act_was, dve_was = take(("L0", "rt", n, c), act=("L0", "rt", n, c))
                        pe.wait_ge(act_done, upto(act_done, ("L0", "pT", n), *act_was))
                        pe.wait_ge(dve_done, upto(dve_done, *dve_was))
                        mm(ps[:, b, :], eb2[:, c * P:(c + 1) * P], pT[:, half], True, False)
                        for m in range(RM):
                            if c == 0:
                                pe.wait_ge(dve_done, upto(dve_done, ("L0", "hp", n, m)))
                            ins = mm(ps[:, b, :], ew2[:, m, c * P:(c + 1) * P], hid0[:, m, :], False, m == RM - 1)
                        ins.then_inc(mm_done, M.add(mm_done, ("L0", "rt", n, c)))
                    for i2 in range(2):
                        t2 = 2 * n + i2
                        b, act_was, dve_was = take(("L0", "o", t2), dve=("L0", "sg", t2))
                        pe.wait_ge(act_done, upto(act_done, *(("L0", "rt", n, c) for c in range(KC)), *act_was))
                        pe.wait_ge(dve_done, upto(dve_done, *dve_was))
                        for i in range(2):
                            tt = slice((2 * i2 + i) * P, (2 * i2 + i + 1) * P)
                            mm(ps[:, b, i * D:(i + 1) * D], *pick("out_b"), True, False)
                            for k in range(KC):
                                ins = mm(ps[:, b, i * D:(i + 1) * D], rT[:, k, tt], outw[:, k, :], False, k == KC - 1)
                        ins.then_inc(mm_done, M.add(mm_done, ("L0", "o", t2)))
            M.close("experts")

            owner.clear()
            M.open("blocks")
            with pe.Fori(0, B) as it:
                def upto(sem, *steps):
                    return M.upto("blocks", it, sem, steps)

                def row(tag, terms, reader):
                    b, act_was, dve_was = take(("row", tag), dve=reader)
                    pe.wait_ge(act_done, upto(act_done, "scond", *act_was))
                    pe.wait_ge(dve_done, upto(dve_done, *dve_was))
                    for i, (a, r) in enumerate(terms):
                        ins = mm(ps[:, b, 0:D], a, r, i == 0, i == len(terms) - 1)
                    ins.then_inc(mm_done, M.add(mm_done, ("row", tag)))

                def silu_cond(w):
                    return [(scond[:, c:c + 1].to_broadcast([P, P]), w[:, c, :]) for c in range(KC)]

                def attend(tag):
                    cross, wq, wk, wv, wo, *_ = ATT[tag]
                    ln = LN_OF[tag]
                    kw = S if cross else P
                    src = {"L3ca": kvT}.get(tag, ctxT if cross else hT)
                    for n in range(NH):
                        for c in range(KC):
                            if (n, c) == (0, 0):
                                pe.wait_ge(SLOT_OF[tag], upto(SLOT_OF[tag], (tag, 3)))
                            b, act_was, dve_was = take((tag, "q", c, n), dve=(tag, "ql", c, n))
                            pe.wait_ge(act_done, upto(act_done, *((ln, "hT", n, k) for k in range(KC)), *act_was))
                            pe.wait_ge(dve_done, upto(dve_done, *dve_was))
                            for k in range(KC):
                                ins = mm(ps[:, b, :], wq[:, k, c * P:(c + 1) * P], hT[:, k, n * HALF:(n + 1) * HALF],
                                         k == 0, k == KC - 1)
                            ins.then_inc(mm_done, M.add(mm_done, (tag, "q", c, n)))
                            if cross and n:
                                continue
                            kn = SP_ if cross else HALF
                            b, act_was, dve_was = take((tag, "k", c, n), dve=(tag, "kl", c, n))
                            pe.wait_ge(act_done, upto(act_done, *act_was))
                            pe.wait_ge(dve_done, upto(dve_done, *dve_was))
                            for k in range(KC):
                                ins = mm(ps[:, b, 0:kn], wk[:, k, c * P:(c + 1) * P], src[:, k, n * HALF:n * HALF + kn],
                                         k == 0, k == KC - 1)
                            ins.then_inc(mm_done, M.add(mm_done, (tag, "k", c, n)))
                    for t2 in range(1 if cross else NT // 2):
                        b, act_was, dve_was = take((tag, "v", t2), dve=(tag, "v", t2))
                        pe.wait_ge(act_done, upto(act_done, *act_was))
                        pe.wait_ge(dve_done, upto(dve_done, *dve_was))
                        for i in range(1 if cross else 2):
                            t = 2 * t2 + i
                            for k in range(KC):
                                ins = mm(ps[0:kw, b, i * D:(i + 1) * D], src[:, k, t * P:t * P + kw], wv[:, k, :],
                                         k == 0, k == KC - 1)
                        ins.then_inc(mm_done, M.add(mm_done, (tag, "v", t2)))
                    pairs, singles, unit = 0, 0, {}
                    for step in (CROSS if cross else SELF):
                        kind = step[0]
                        if kind == "K":
                            who, which, pair, n = step[1:]
                            hi, lo = (qh, ql) if which == "q" else (kh, kl)
                            c, pp = divmod(pair, PAIRS // KC)
                            kn = SP_ if cross and which == "k" else HALF
                            part = slice(n * HALF, n * HALF + kn)
                            name = (tag,) + step
                            b, act_was, dve_was = take(name, banks=(4 + singles % 3,), **{who: name})
                            singles += 1
                            pe.wait_ge(act_done, upto(act_done, *act_was))
                            pe.wait_ge(dve_done, upto(dve_done, (tag, which + "l", c, n), *dve_was))
                            s = SEL[which] + pp
                            mm(ps[:, b, 0:kn], sel[:, s, :], hi[:, c, part], True, False)
                            ins = mm(ps[:, b, 0:kn], sel[:, s + PAIRS // KC, :], lo[:, c, part], False, True)
                        elif kind == "A":
                            g, n, t, j = step[1:]
                            a = 2 * (pairs % 2)
                            pairs += 1
                            _, act_was, dve_was = take((tag,) + step, dve=(tag,) + step, banks=(a, a + 1))
                            heads = range(GH) if cross else [j]
                            pe.wait_ge(act_done, upto(act_done, *((tag,) + k for k in stacks_for(cross, "act", g, n)), *act_was))
                            pe.wait_ge(dve_done, upto(dve_done, *((tag,) + k for k in stacks_for(cross, "dve", g, n)), *dve_was))
                            for jj in heads:
                                h = GH * g + jj
                                r = stacked(h % 2, 0, STACK)
                                lhs = qs[r, h // 2, (TPH * n + t) * P:(TPH * n + t + 1) * P]
                                if cross:
                                    o = jj // 2 * SP_
                                    ins = mm(ps[:, a + h % 2, o:o + SP_], lhs, ks[r, h // 2, 0:SP_])
                                else:
                                    for i in range(2):
                                        ins = mm(ps[:, a + i, :], lhs, ks[r, h // 2, i * HALF:(i + 1) * HALF])
                        elif kind == "M":
                            g, n = step[1:]
                            z, w, _, _ = maxima_of(tag, g, n)
                            a = 2 * (pairs % 2)
                            pairs += 1
                            _, act_was, dve_was = take((tag,) + step, act=(tag,) + step, banks=(a, a + 1))
                            pe.wait_ge(act_done, upto(act_done, *act_was))
                            last = ("A", GROUPS - 1, n, TPH - 1, 0) if cross else ("A", g, n, TPH - 1, GH - 1)
                            pe.wait_ge(dve_done, upto(dve_done, (tag,) + last, *dve_was))
                            for t in range(TPH):
                                ins = pe.transpose(ps[0:w, a, t * P:(t + 1) * P], mx[:, z, t, 0:w], ident[:])
                        elif kind == "S":
                            g, n, kt, j = step[1:]
                            if (kt, j) == (0, 0):
                                pe.wait_ge(maxima_stacked[g][n], upto(maxima_stacked[g][n], (tag, GH - 1)))
                            b, act_was, dve_was = take((tag,) + step, act=(tag,) + step, banks=(4 + singles % 3,))
                            singles += 1
                            pe.wait_ge(act_done, upto(act_done, *act_was))
                            pe.wait_ge(dve_done, upto(dve_done, *dve_was))
                            h = GH * g + j
                            r = stacked(h % 2, 0, STACK)
                            ins = mm(ps[0:kw, b, :], ks[r, h // 2, kt * P:kt * P + kw], qs[r, h // 2, n * HALF:(n + 1) * HALF])
                        elif kind == "PV":
                            g, n, kt = step[1:]
                            u = unit.setdefault((g, n, kt), len(unit)) % 4
                            act_was = []
                            if kt == 0:
                                _, act_was, dve_was = take((tag,) + step, act=(tag, "O", g, n), banks=(7,))
                                pe.wait_ge(dve_done, upto(dve_done, *((tag, "v", t2) for t2 in range(1 if cross else NT // 2)), *dve_was))
                            pe.wait_ge(act_done, upto(act_done, (tag, "S", g, n, kt, GH - 1), *act_was))
                            for j in range(GH):
                                ins = mm(ps[32 * j:32 * j + 32, 7, :], v[0:kw, kt, GH * g + j, :],
                                         probs[0:kw, u, j, :], kt == 0, cross or kt == NT - 1)
                        elif kind == "OT":
                            g, n = step[1:]
                            a = 2 * (pairs % 2)
                            pairs += 1
                            _, act_was, dve_was = take((tag,) + step, dve=(tag, "tok", g, n), banks=(a, a + 1))
                            pe.wait_ge(act_done, upto(act_done, (tag, "O", g, n), *act_was))
                            pe.wait_ge(dve_done, upto(dve_done, *dve_was))
                            for i in range(TPH):
                                o = n * HALF + i * P
                                ins = pe.transpose(ps[:, a, i * P:(i + 1) * P], ow[:, o:o + P], ident[:])
                        if kind != "O":
                            ins.then_inc(mm_done, M.add(mm_done, (tag,) + step))
                    for n in range(NH):
                        for c in range(KC):
                            b, act_was, dve_was = take((tag, "aT", n, c), act=(tag, "aT", n, c))
                            pe.wait_ge(act_done, upto(act_done, *act_was))
                            pe.wait_ge(dve_done, upto(dve_done, *((tag, "tok", g, n) for g in range(GROUPS)), *dve_was))
                            for i in range(TPH):
                                ins = pe.transpose(ps[:, b, i * P:(i + 1) * P], tok[:, TPH * n + i, c * P:(c + 1) * P], ident[:])
                            ins.then_inc(mm_done, M.add(mm_done, (tag, "aT", n, c)))
                    for t2 in range(4):
                        b, act_was, dve_was = take((tag, "o", t2), dve=(tag, "x", t2))
                        pe.wait_ge(act_done, upto(act_done, *((tag, "aT", t2 // 2, c) for c in range(KC)), *act_was))
                        pe.wait_ge(dve_done, upto(dve_done, *dve_was))
                        for i in range(2):
                            t = 2 * t2 + i
                            for k in range(KC):
                                ins = mm(ps[:, b, i * D:(i + 1) * D], hT[:, k, t * P:(t + 1) * P], wo[:, k, :], k == 0, k == KC - 1)
                        ins.then_inc(mm_done, M.add(mm_done, (tag, "o", t2)))

                def mlp(tag, ln):
                    for n in range(NH):
                        for m in range(FM):
                            if (n, m) == (0, 0):
                                pe.wait_ge(slot_loaded[2], upto(slot_loaded[2], tag))
                            b, act_was, dve_was = take((tag, "h", n, m), act=(tag, "h", n, m))
                            pe.wait_ge(act_done, upto(act_done, *((ln, "hT", n, c) for c in range(KC)), *act_was))
                            pe.wait_ge(dve_done, upto(dve_done, *dve_was))
                            for k in range(KC):
                                ins = mm(ps[:, b, :], W1[:, k, m * P:(m + 1) * P], hT[:, k, n * HALF:(n + 1) * HALF], k == 0, k == KC - 1)
                            ins.then_inc(mm_done, M.add(mm_done, (tag, "h", n, m)))
                    for t2 in range(4):
                        n = t2 // 2
                        if t2 == 0:
                            pe.wait_ge(slot_loaded[3], upto(slot_loaded[3], tag))
                        b, act_was, dve_was = take((tag, "o", t2), dve=(tag, "x", t2))
                        pe.wait_ge(act_done, upto(act_done, (tag, "h", n, FM - 1), *act_was))
                        pe.wait_ge(dve_done, upto(dve_done, *dve_was))
                        for i in range(2):
                            o = ((2 * t2 + i) % TPH) * P
                            for m in range(FM):
                                ins = mm(ps[:, b, i * D:(i + 1) * D], hid[:, n, m, o:o + P], W2[:, m, :], m == 0, m == FM - 1)
                        ins.then_inc(mm_done, M.add(mm_done, (tag, "o", t2)))

                tp = [tpw[:, :, i * D:(i + 1) * D] for i in range(3)]
                turn(upto, "ln1")
                pe.wait_ge(slot_loaded[4], upto(slot_loaded[4], "L1"))
                row("L1sa", silu_cond(tp[0]) + [pick("tp_b0"), pick("sa_bo")], ("row", "L1sa"))
                attend("L1sa")
                row("L1ca", silu_cond(tp[1]) + [pick("tp_b1"), pick("ca_bo")], ("row", "L1ca"))
                turn(upto, "ln3")
                attend("L1ca")
                row("L1mlp", silu_cond(tp[2]) + [pick("tp_b2"), pick("b2")], ("row", "L1mlp"))
                turn(upto, "ln2")
                mlp("L1mlp", "ln2")
                b, act_was, dve_was = take("mod", dve="mod")
                pe.wait_ge(act_done, upto(act_done, "scond", *act_was))
                pe.wait_ge(dve_done, upto(dve_done, *dve_was))
                pe.wait_ge(slot_loaded[4], upto(slot_loaded[4], "L2"))
                for m in (0, 1, 2, 3, 6, 7, 8, 9):
                    for k in range(KC):
                        ins = mm(ps[:, b, m:m + 1], adw[:, k, m * P:(m + 1) * P], scond[:, k:k + 1], k == 0, k == KC - 1)
                ins.then_inc(mm_done, M.add(mm_done, "mod"))
                row("L2sa_g", silu_cond(adw[:, :, 2 * D:3 * D]) + [pick("g_sa")], ("grow", "L2sa"))
                row("L2sa", [pick("sa_proj_b")], ("rrow", "L2sa"))
                turn(upto, "ln4")
                attend("L2sa")
                row("L2ca", [pick("ca_proj_b")], ("row", "L2ca"))
                turn(upto, "ln5")
                attend("L2ca")
                row("L2mlp_g", silu_cond(adw[:, :, 5 * D:6 * D]) + [pick("g_ff")], ("grow", "L2mlp"))
                row("L2mlp", [pick("fc2_b")], ("rrow", "L2mlp"))
                turn(upto, "ln6")
                mlp("L2mlp", "ln6")
                b, act_was, dve_was = take("mod3", dve="mod3")
                pe.wait_ge(act_done, upto(act_done, *act_was))
                pe.wait_ge(dve_done, upto(dve_done, *dve_was))
                pe.wait_ge(slot_loaded[1], upto(slot_loaded[1], "L3ss"))
                for i in range(2):
                    for m in range(4):
                        for k in range(KC):
                            ins = mm(ps[:, b, 4 * i + m:4 * i + m + 1], w256(1, 2 * i, 512)[:, k, m * P:(m + 1) * P],
                                     scond[:, k:k + 1], k == 0, k == KC - 1)
                ins.then_inc(mm_done, M.add(mm_done, "mod3"))
                b, act_was, dve_was = take("cT", act="kvT")
                pe.wait_ge(act_done, upto(act_done, *act_was))
                pe.wait_ge(dve_done, upto(dve_done, "ctxn", *dve_was))
                for c in range(KC):
                    ins = pe.transpose(ps[:, b, c * S:(c + 1) * S], ctxk[:, c * P:(c + 1) * P], ident[0:S, 0:S])
                ins.then_inc(mm_done, M.add(mm_done, "cT"))
                row("L3ca", [pick("bp")], ("row", "L3ca"))
                turn(upto, "ln7")
                attend("L3ca")
            M.close("blocks")

        @block.scalar
        def _(act):
            def load_conditions(it, upto, loop):
                act.dma_start(ctxT[:], T["ctxT"][it].rearrange("(c p) s -> p c s", p=P)
                              ).then_inc(conditions_loaded, M.add(conditions_loaded, None, LOADED))
                act.dma_start(cond[:], T["condT"][it]).then_inc(conditions_loaded, M.add(conditions_loaded, loop, LOADED))

            def affine(upto, tag, gain, shift):
                for n in range(NH):
                    for c in range(KC):
                        act.wait_ge(mm_done, upto(mm_done, (tag, "T", n, c)))
                        src, dst = ps[:, M.where((tag, "T", n, c)), :], hT[:, c, n * HALF:(n + 1) * HALF]
                        if gain is None:
                            ins = act.activation(dst, src, ACT.Copy)
                        else:
                            ins = act.activation(dst, src, ACT.Identity, bias=shift(c), scale=gain(c))
                        ins.then_inc(act_done, M.add(act_done, (tag, "hT", n, c)))

            act.wait_ge(constants_loaded, 6 * LOADED)
            act.activation(small[:, 127:128], cols[:, 0:1], ACT.Copy).then_inc(act_done, M.add(act_done))
            M.open("experts")
            with act.Fori(0, B) as it:
                def upto(sem, *steps):
                    return M.upto("experts", it, sem, steps)

                act.dma_start(x[:], T["x"][it].rearrange("(t p) d -> p t d", p=P)).then_inc(x_loaded, M.add(x_loaded, "experts", LOADED))
                load_conditions(it, upto, "experts")
                act.wait_ge(mm_done, upto(mm_done, ("L0", "kv")))
                b = M.where(("L0", "kv"))
                act.activation(kv0T[:], ps[:, b, 0:2 * KC * SP_].rearrange("p (c s) -> p c s", s=SP_), ACT.Copy
                               ).then_inc(act_done, M.add(act_done, ("L0", "kv")))
                act.wait_ge(mm_done, upto(mm_done, ("L0", "a")))
                b = M.where(("L0", "a"))
                act.activation(a0[:], ps[:, b, 0:KC * SP_].rearrange("p (c s) -> p c s", s=SP_), ACT.Copy, scale=D ** -0.5
                               ).then_inc(act_done, M.add(act_done, ("L0", "a")))
                affine(upto, "ln0", lambda c: col("L0_ln_gamma", c), lambda c: col("L0_ln_beta", c))
                for n in range(NH):
                    b = M.where(("L0", "s", n))
                    act.wait_ge(dve_done, upto(dve_done, ("L0", "nmx", n)))
                    for i in range(TPH):
                        t = TPH * n + i
                        act.activation(e01[n][:, i, 0:S], ps[:, b, i * SP_:i * SP_ + S], ACT.Exp, bias=nmx[:, t:t + 1],
                                       accum_out=es[:, t:t + 1]).then_inc(act_done, M.add(act_done, ("L0", "e", n, i)))
                for n in range(NH):
                    act.wait_ge(mm_done, upto(mm_done, ("L0", "wT", n)))
                    act.activation(wT[0:S, n * HALF:(n + 1) * HALF], ps[0:S, M.where(("L0", "wT", n)), :], ACT.Copy
                                   ).then_inc(act_done, M.add(act_done, ("L0", "wT", n)))
                act.wait_ge(dve_done, upto(dve_done, ("L0", "lg")))
                act.activation(lg[:], lg[:], ACT.Exp).then_inc(act_done, M.add(act_done, ("L0", "le")))
                for n in range(NH):
                    half = slice(n * HALF, (n + 1) * HALF)
                    for m in range(RM + GM):
                        act.wait_ge(mm_done, upto(mm_done, ("L0", "h", n, m)))
                        act.activation(hid0[:, m, :], ps[:, M.where(("L0", "h", n, m)), :], ACT.Silu, bias=b0[:, m:m + 1]
                                       ).then_inc(act_done, M.add(act_done, ("L0", "h", n, m)))
                        if m < E:
                            act.wait_ge(mm_done, upto(mm_done, ("L0", "pb", n, m)))
                            if n:
                                act.wait_ge(dve_done, upto(dve_done, ("L0", "hp", n - 1, RM - 1)))
                            act.activation(pb[:, m, :], ps[:, M.where(("L0", "pb", n, m)), :], ACT.Copy
                                           ).then_inc(act_done, M.add(act_done, ("L0", "pb", n, m)))
                        if m == E:
                            act.wait_ge(mm_done, upto(mm_done, ("L0", "pT", n)))
                            act.activation(pT[:, half], ps[0:E, M.where(("L0", "pT", n)), :], ACT.Copy
                                           ).then_inc(act_done, M.add(act_done, ("L0", "pT", n)))
                    for i2 in range(2):
                        t2 = 2 * n + i2
                        act.wait_ge(mm_done, upto(mm_done, ("L0", "g", t2)))
                        if n:
                            act.wait_ge(dve_done, upto(dve_done, ("L0", "x", t2 - 2)))
                        act.activation(sg[:, i2], ps[:, M.where(("L0", "g", t2)), :].rearrange("p (i d) -> p i d", i=2),
                                       ACT.Tanh, scale=0.5).then_inc(act_done, M.add(act_done, ("L0", "g", t2)))
                    for c in range(KC):
                        act.wait_ge(mm_done, upto(mm_done, ("L0", "rt", n, c)))
                        act.activation(rT[:, c, :], ps[:, M.where(("L0", "rt", n, c)), :], ACT.Copy
                                       ).then_inc(act_done, M.add(act_done, ("L0", "rt", n, c)))
                for t2 in range(4):
                    act.wait_ge(dve_done, upto(dve_done, ("L0", "x", t2)))
                    act.dma_start(T["x0"][it].rearrange("(t p) d -> p t d", p=P)[:, 2 * t2:2 * t2 + 2, :],
                                  x[:, 2 * t2:2 * t2 + 2, :]).then_inc(x_stored, M.add(x_stored, t2, LOADED))
                act.wait_ge(x_stored, upto(x_stored, 3))
            M.close("experts")

            M.open("blocks")
            with act.Fori(0, B) as it:
                def upto(sem, *steps):
                    return M.upto("blocks", it, sem, steps)

                def attend(tag):
                    cross = ATT[tag][0]
                    bq, bk, bv = ATT[tag][5:]
                    kw = S if cross else P
                    for n in range(NH):
                        for c in range(KC):
                            act.wait_ge(mm_done, upto(mm_done, (tag, "q", c, n)))
                            act.activation(qh[:, c, n * HALF:(n + 1) * HALF], ps[:, M.where((tag, "q", c, n)), :], ACT.Identity,
                                           bias=col(bq[0], bq[1] + c)).then_inc(act_done, M.add(act_done, (tag, "qh", c, n)))
                            if cross and n:
                                continue
                            kn = SP_ if cross else HALF
                            act.wait_ge(mm_done, upto(mm_done, (tag, "k", c, n)))
                            act.activation(kh[:, c, n * HALF:n * HALF + kn], ps[:, M.where((tag, "k", c, n)), 0:kn], ACT.Identity,
                                           bias=col(bk[0], bk[1] + c)).then_inc(act_done, M.add(act_done, (tag, "kh", c, n)))
                    unit = {}
                    for step in (CROSS if cross else SELF):
                        kind, name = step[0], (tag,) + step
                        if kind == "K" and step[1] == "act":
                            which, pair, n = step[2:]
                            act.wait_ge(mm_done, upto(mm_done, name))
                            if which == "q":
                                act.activation(qs[:, pair, n * HALF:(n + 1) * HALF], ps[:, M.where(name), :], ACT.Copy
                                               ).then_inc(act_done, M.add(act_done, name))
                            else:
                                kn = SP_ if cross else HALF
                                act.activation(ks[:, pair, n * HALF:n * HALF + kn], ps[:, M.where(name), 0:kn], ACT.Identity,
                                               bias=ones_col).then_inc(act_done, M.add(act_done, name))
                        elif kind == "M":
                            g, n = step[1:]
                            z, w, _, _ = maxima_of(tag, g, n)
                            act.wait_ge(mm_done, upto(mm_done, name))
                            if not cross and NH * g + n >= 2:
                                act.wait_ge(maxima_stacked[g - 1][n], upto(maxima_stacked[g - 1][n], (tag, GH - 1)))
                            act.activation(mrow[0:w, z * HALF:(z + 1) * HALF], ps[0:w, M.where(name), :], ACT.Copy
                                           ).then_inc(act_done, M.add(act_done, name))
                        elif kind == "S":
                            g, n, kt, j = step[1:]
                            u = unit.setdefault((g, n, kt), len(unit))
                            act.wait_ge(mm_done, upto(mm_done, name, *[(tag, "PV") + k for k in list(unit)[u - 4:u - 3] if u >= 4]))
                            src, dst = ps[0:kw, M.where(name), :], probs[0:kw, u % 4, j, :]
                            if tag == "L1ca":
                                if (u, j) == (0, 0):
                                    act.wait_ge(dve_done, upto(dve_done, "mcolb"))
                                ins = act.activation(dst, src, ACT.Exp, bias=mcolb[:], scale=SCALE)
                            else:
                                ins = act.activation(dst, src, ACT.Exp, scale=SCALE)
                            ins.then_inc(act_done, M.add(act_done, name))
                        elif kind == "O":
                            g, n = step[1:]
                            act.wait_ge(mm_done, upto(mm_done, (tag, "PV", g, n, 0 if cross else NT - 1), *[(tag, "OT", g - 1, n)] * (g > 0)))
                            act.activation(ow[:, n * HALF:(n + 1) * HALF], ps[:, 7, :], ACT.Copy).then_inc(act_done, M.add(act_done, name))
                    for n in range(NH):
                        for c in range(KC):
                            act.wait_ge(mm_done, upto(mm_done, (tag, "aT", n, c)))
                            act.activation(hT[:, c, n * HALF:(n + 1) * HALF], ps[:, M.where((tag, "aT", n, c)), :], ACT.Identity,
                                           bias=col(bv[0], bv[1] + c)).then_inc(act_done, M.add(act_done, (tag, "aT", n, c)))

                def mlp(tag, func, bias):
                    for n in range(NH):
                        for m in range(FM):
                            act.wait_ge(mm_done, upto(mm_done, (tag, "h", n, m)))
                            act.activation(hid[:, n, m, :], ps[:, M.where((tag, "h", n, m)), :], func, bias=col(bias, m)
                                           ).then_inc(act_done, M.add(act_done, (tag, "h", n, m)))

                act.dma_start(x[:], T["x0"][it].rearrange("(t p) d -> p t d", p=P)).then_inc(x_loaded, M.add(x_loaded, "blocks", LOADED))
                load_conditions(it, upto, "blocks")
                act.dma_start(mi[:], T["mask"][it].to_broadcast([P, SP_])).then_inc(conditions_loaded, M.add(conditions_loaded, None, LOADED))
                act.dma_start(mic[:], T["maskT"][it]).then_inc(conditions_loaded, M.add(conditions_loaded, None, LOADED))
                act.dma_start(ctxk[:], T["ctx"][it]).then_inc(conditions_loaded, M.add(conditions_loaded, "all", LOADED))
                act.wait_ge(conditions_loaded, upto(conditions_loaded, "all"))
                act.activation(scond[:], cond[:], ACT.Silu).then_inc(act_done, M.add(act_done, "scond"))
                affine(upto, "ln1", lambda c: col("L1_ln1_g", c), lambda c: col("L1_ln1_b", c))
                attend("L1sa")
                affine(upto, "ln3", lambda c: col("L1_ln3_g", c), lambda c: col("L1_ln3_b", c))
                attend("L1ca")
                affine(upto, "ln2", lambda c: col("L1_ln2_g", c), lambda c: col("L1_ln2_b", c))
                mlp("L1mlp", ACT.Gelu, "L1_b1")
                act.wait_ge(dve_done, upto(dve_done, "mod"))
                affine(upto, "ln4", lambda c: mod[:, 2 + c:3 + c], lambda c: mod[:, c:c + 1])
                attend("L2sa")
                affine(upto, "ln5", None, None)
                attend("L2ca")
                affine(upto, "ln6", lambda c: mod[:, 8 + c:9 + c], lambda c: mod[:, 6 + c:7 + c])
                mlp("L2mlp", ACT.Gelu_apprx_tanh, "L2_fc1_b")
                act.wait_ge(mm_done, upto(mm_done, "cT"))
                act.wait_ge(dve_done, upto(dve_done, "mod3"))
                b = M.where("cT")
                for c in range(KC):
                    act.activation(kvT[:, c, 0:S], ps[:, b, c * S:(c + 1) * S], ACT.Identity, bias=mod3[:, 6 + c:7 + c],
                                   scale=mod3[:, 4 + c:5 + c]).then_inc(act_done, M.add(act_done, ("kvT", c)))
                    act.activation(kvT[:, c, S:SP_], ps[:, b, (c + 1) * S - 1:(c + 1) * S], ACT.Identity, bias=mod3[:, 6 + c:7 + c],
                                   scale=mod3[:, 4 + c:5 + c]).then_inc(act_done, M.add(act_done, "kvT" if c == KC - 1 else ("kvT2", c)))
                affine(upto, "ln7", lambda c: mod3[:, c:c + 1], lambda c: mod3[:, 2 + c:3 + c])
                attend("L3ca")
                for t2 in range(4):
                    act.wait_ge(dve_done, upto(dve_done, ("L3ca", "x", t2)))
                    act.dma_start(T["out"][it].rearrange("(t p) d -> p t d", p=P)[:, 2 * t2:2 * t2 + 2, :],
                                  x[:, 2 * t2:2 * t2 + 2, :]).then_inc(out_stored, M.add(out_stored, t2, LOADED))
                act.wait_ge(out_stored, upto(out_stored, 3))
            M.close("blocks")

        @block.vector
        def _(dve):
            def norm(upto, tag, eps):
                for t in range(NT):
                    if tag in ("ln0", "ln1"):
                        if t == 0:
                            dve.wait_ge(x_loaded, upto(x_loaded, {"ln0": "experts", "ln1": "blocks"}[tag]))
                    else:
                        dve.wait_ge(dve_done, upto(dve_done, (XNEXT[tag], "x", t // 2)))
                    dve.bn_stats(st[:, t, :], x[:, t, :]).then_inc(dve_done, M.add(dve_done, (tag, "st", t)))
                dve.wait_ge(dve_done, upto(dve_done, (tag, "st", NT - 1)))
                dve.memset(ve, 0.0)
                for t in range(NT):
                    dve.bn_aggr(mv[:, t, :], st[:, t, :]).then_inc(dve_done, M.add(dve_done, (tag, "ag", t)))
                dve.wait_ge(dve_done, upto(dve_done, (tag, "ag", NT - 1)))
                dve.tensor_scalar(ve, mv[:, :, 1], eps, None, ALU.add).then_inc(dve_done, M.add(dve_done, (tag, "ve")))
                dve.wait_ge(pool_done, upto(pool_done, (tag, "rstd")))
                for t in range(NT):
                    dve.tensor_scalar(tok[:, t, :], x[:, t, :], mv[:, t, 0:1], rstd[:, t:t + 1], ALU.subtract, ALU.mult
                                      ).then_inc(dve_done, M.add(dve_done, (tag, "xh", t)))

            dve.memset(nhalf, -0.5)
            dve.memset(v[:], 1.0)
            dve.memset(ones_col, 0.0).then_inc(constants_set, 1)
            dve.wait_ge(constants_set, 1)
            dve.memset(ones_col[32:48], 1.0)
            dve.memset(ones_col[96:112], 1.0)
            dve.wait_ge(constants_loaded, 6 * LOADED)
            dve.tensor_copy(sel[:], sel_in[:]).then_inc(dve_done, M.add(dve_done))
            dve.wait_ge(dve_done, 1)
            M.open("experts")
            with dve.Fori(0, B) as it:
                def upto(sem, *steps):
                    return M.upto("experts", it, sem, steps)

                norm(upto, "ln0", 1e-5)
                for e in range(E + 1):
                    w = RH if e < E else D + E
                    dve.wait_ge(mm_done, upto(mm_done, ("L0", "u", e)))
                    dve.tensor_copy(u0[0:S, e * RH:e * RH + w], ps[0:S, M.where(("L0", "u", e)), 0:w]
                                    ).then_inc(dve_done, M.add(dve_done, ("L0", "u", e)))
                dve.wait_ge(mm_done, upto(mm_done, ("L0", "b")))
                dve.tensor_tensor(b0, ps[:, M.where(("L0", "b")), 0:RM + GM], cols[:, COL["L0_e_b1"]:COL["L0_e_b1"] + RM + GM], ALU.add
                                  ).then_inc(dve_done, M.add(dve_done, ("L0", "b")))
                for n in range(NH):
                    tt = slice(TPH * n, TPH * n + TPH)
                    src = ps[:, M.where(("L0", "s", n)), 0:TPH * SP_].rearrange("p (t s) -> p t s", s=SP_)[:, :, 0:S]
                    dve.wait_ge(mm_done, upto(mm_done, ("L0", "s", n)))
                    dve.tensor_reduce(nmx[:, tt], src, AX.X, ALU.max, negate=True).then_inc(dve_done, M.add(dve_done, ("L0", "nmx", n)))
                for n in range(NH):
                    tt = slice(TPH * n, TPH * n + TPH)
                    dve.wait_ge(act_done, upto(act_done, ("L0", "e", n, TPH - 1)))
                    dve.reciprocal(rc4[:, tt], es[:, tt]).then_inc(dve_done, M.add(dve_done, ("L0", "rc4", n)))
                    dve.wait_ge(dve_done, upto(dve_done, ("L0", "rc4", n)))
                    dve.tensor_tensor(e01[n][:, :, 0:S], e01[n][:, :, 0:S], rc4[:, tt].unsqueeze(2).to_broadcast([P, TPH, S]), ALU.mult
                                      ).then_inc(dve_done, M.add(dve_done, ("L0", "w", n)))
                src = ps[:, M.where(("L0", "r")), 0:NT * E].rearrange("p (t e) -> p t e", e=E)
                dve.wait_ge(mm_done, upto(mm_done, ("L0", "r")))
                dve.tensor_reduce(rmx[:], src, AX.X, ALU.max, negate=True).then_inc(dve_done, M.add(dve_done, ("L0", "rmx")))
                dve.wait_ge(dve_done, upto(dve_done, ("L0", "rmx")))
                dve.tensor_tensor(lg[:], src, rmx[:].unsqueeze(2).to_broadcast([P, NT, E]), ALU.add
                                  ).then_inc(dve_done, M.add(dve_done, ("L0", "lg")))
                dve.wait_ge(act_done, upto(act_done, ("L0", "le")))
                dve.tensor_reduce(rs[:], lg[:], AX.X, ALU.add).then_inc(dve_done, M.add(dve_done, ("L0", "rs")))
                dve.wait_ge(dve_done, upto(dve_done, ("L0", "rs")))
                dve.reciprocal(rrs[:], rs[:]).then_inc(dve_done, M.add(dve_done, ("L0", "rrs")))
                dve.wait_ge(dve_done, upto(dve_done, ("L0", "rrs")))
                dve.tensor_tensor(lg[:], lg[:], rrs[:].unsqueeze(2).to_broadcast([P, NT, E]), ALU.mult
                                  ).then_inc(dve_done, M.add(dve_done, ("L0", "p")))
                for n in range(NH):
                    for m in range(RM):
                        dve.wait_ge(act_done, upto(act_done, ("L0", "pb", n, m // 4), ("L0", "h", n, m)))
                        dve.tensor_tensor(hid0[:, m, :], hid0[:, m, :], pb[:, m // 4, :], ALU.mult
                                          ).then_inc(dve_done, M.add(dve_done, ("L0", "hp", n, m)))
                    for i2 in range(2):
                        t2 = 2 * n + i2
                        xx = x[:, 2 * t2:2 * t2 + 2, :]
                        o = ps[:, M.where(("L0", "o", t2)), :].rearrange("p (i d) -> p i d", i=2)
                        dve.wait_ge(mm_done, upto(mm_done, ("L0", "o", t2)))
                        dve.wait_ge(act_done, upto(act_done, ("L0", "g", t2)))
                        dve.scalar_tensor_tensor(sg[:, i2], sg[:, i2], 1.0, o, ALU.add, ALU.mult
                                                 ).then_inc(dve_done, M.add(dve_done, ("L0", "sg", t2)))
                        dve.wait_ge(dve_done, upto(dve_done, ("L0", "sg", t2)))
                        dve.scalar_tensor_tensor(xx, sg[:, i2], 0.5, xx, ALU.mult, ALU.add
                                                 ).then_inc(dve_done, M.add(dve_done, ("L0", "x", t2)))
            M.close("experts")

            M.open("blocks")
            with dve.Fori(0, B) as it:
                def upto(sem, *steps):
                    return M.upto("blocks", it, sem, steps)

                def add_row(tag):
                    r = ps[:, M.where(("row", tag)), 0:D].unsqueeze(1).to_broadcast([P, NT, D])
                    dve.wait_ge(mm_done, upto(mm_done, ("row", tag)))
                    dve.wait_ge(dve_done, upto(dve_done, (LN_OF.get(tag, "ln2"), "xh", NT - 1)))
                    dve.tensor_tensor(x[:], x[:], r, ALU.add).then_inc(dve_done, M.add(dve_done, ("row", tag)))

                def add_gated_row(tag, ln):
                    dve.wait_ge(mm_done, upto(mm_done, ("row", tag + "_g")))
                    dve.tensor_copy(grow[:], ps[:, M.where(("row", tag + "_g")), 0:D]).then_inc(dve_done, M.add(dve_done, ("grow", tag)))
                    dve.wait_ge(mm_done, upto(mm_done, ("row", tag)))
                    dve.wait_ge(dve_done, upto(dve_done, ("grow", tag)))
                    dve.tensor_tensor(rrow[:], grow[:], ps[:, M.where(("row", tag)), 0:D], ALU.mult
                                      ).then_inc(dve_done, M.add(dve_done, ("rrow", tag)))
                    dve.wait_ge(dve_done, upto(dve_done, ("rrow", tag), (ln, "xh", NT - 1)))
                    dve.tensor_tensor(x[:], x[:], rrow[:].unsqueeze(1).to_broadcast([P, NT, D]), ALU.add
                                      ).then_inc(dve_done, M.add(dve_done, ("row", tag)))

                def residual(tag, gated):
                    for t2 in range(4):
                        src = ps[:, M.where((tag, "o", t2)), :].rearrange("p (i d) -> p i d", i=2)
                        xx = x[:, 2 * t2:2 * t2 + 2, :]
                        if gated:
                            tmp = tok[:, 2 * t2:2 * t2 + 2, :]
                            dve.wait_ge(mm_done, upto(mm_done, (tag, "o", t2)))
                            dve.tensor_tensor(tmp, src, grow[:].unsqueeze(1).to_broadcast([P, 2, D]), ALU.mult
                                              ).then_inc(dve_done, M.add(dve_done, (tag, "gx", t2)))
                            dve.wait_ge(dve_done, upto(dve_done, (tag, "gx", t2)))
                            src = tmp
                        else:
                            dve.wait_ge(mm_done, upto(mm_done, (tag, "o", t2)))
                            dve.wait_ge(dve_done, upto(dve_done, ("row", tag)))
                        dve.tensor_tensor(xx, xx, src, ALU.add).then_inc(dve_done, M.add(dve_done, (tag, "x", t2)))

                def split(tag, name, c, n, hi, lo, bias, kn):
                    part = slice(n * HALF, n * HALF + kn)
                    dve.wait_ge(act_done, upto(act_done, (tag, name + "h", c, n)))
                    dve.scalar_tensor_tensor(lo[:, c, part], ps[:, M.where((tag, name, c, n)), 0:kn], col(bias[0], bias[1] + c),
                                             hi[:, c, part].bitcast(F32), ALU.add, ALU.subtract
                                             ).then_inc(dve_done, M.add(dve_done, (tag, name + "l", c, n)))

                def attend(tag):
                    cross = ATT[tag][0]
                    bq, bk, bv = ATT[tag][5:]
                    kw = S if cross else P
                    for n in range(NH):
                        for c in range(KC):
                            split(tag, "q", c, n, qh, ql, bq, HALF)
                            if not (cross and n):
                                split(tag, "k", c, n, kh, kl, bk, SP_ if cross else HALF)
                    for t2 in range(1 if cross else NT // 2):
                        i = 1 if cross else 2
                        src = ps[0:kw, M.where((tag, "v", t2)), 0:i * D].rearrange("p (i h d) -> p i h d", i=i, d=HD)
                        dve.wait_ge(mm_done, upto(mm_done, (tag, "v", t2)))
                        dve.tensor_copy(v[0:kw, 2 * t2:2 * t2 + i, :, 0:HD], src).then_inc(dve_done, M.add(dve_done, (tag, "v", t2)))
                    turned, masked_before = [], None
                    for step in (CROSS if cross else SELF):
                        kind, name = step[0], (tag,) + step
                        if kind == "K" and step[1] == "dve":
                            which, pair, n = step[2:]
                            dve.wait_ge(mm_done, upto(mm_done, name))
                            if which == "q":
                                dve.tensor_copy(qs[:, pair, n * HALF:(n + 1) * HALF], ps[:, M.where(name), :]
                                                ).then_inc(dve_done, M.add(dve_done, name))
                            else:
                                kn = SP_ if cross else HALF
                                dve.tensor_scalar(ks[:, pair, n * HALF:n * HALF + kn], ps[:, M.where(name), 0:kn], ones_col, None, ALU.add
                                                  ).then_inc(dve_done, M.add(dve_done, name))
                        elif kind == "A":
                            g, n, t, j = step[1:]
                            z, w, j0, turn_step = maxima_of(tag, g, n)
                            a = M.where(name)
                            if not cross and NH * g + n >= 2:
                                dve.wait_ge(mm_done, upto(mm_done, name, (tag, "M", g - 1, n)))
                            else:
                                dve.wait_ge(mm_done, upto(mm_done, name))
                            if cross:
                                src = ps[:, a:a + 2, 0:2 * SP_].rearrange("p b (i s) -> p i b s", s=SP_)
                                if tag == "L1ca":
                                    masked = e0[:].rearrange("p (i b) s -> p i b s", b=2)
                                    dve.wait_ge(dve_done, upto(dve_done, masked_before or "mrowb"))
                                    dve.tensor_tensor(masked, src, mrowb[:].unsqueeze(1).unsqueeze(1).to_broadcast([P, 2, 2, SP_]), ALU.add
                                                      ).then_inc(dve_done, M.add(dve_done, (tag, "masked", g, n, t)))
                                    dve.wait_ge(dve_done, upto(dve_done, (tag, "masked", g, n, t)))
                                    masked_before = name
                                    src = masked
                                dve.tensor_reduce(mx[:, z, t, j0:j0 + GH].rearrange("p (i b) -> p i b", b=2), src, AX.X, ALU.max, negate=True
                                                  ).then_inc(dve_done, M.add(dve_done, name))
                            else:
                                dve.tensor_reduce(mx[:, z, t, j:j + 1], ps[:, a:a + 2, :], AX.XY, ALU.max, negate=True
                                                  ).then_inc(dve_done, M.add(dve_done, name))
                        elif kind == "OT":
                            g, n = step[1:]
                            o = ps[:, M.where(name), :].rearrange("p (t j d) -> p t j d", t=TPH, j=GH)
                            rcv = rc[:].rearrange("p (t j) -> p t j", j=GH)
                            dst = tok[:, TPH * n:TPH * n + TPH, GH * HD * g:GH * HD * (g + 1)].rearrange("p t (j d) -> p t j d", d=HD)
                            dve.wait_ge(mm_done, upto(mm_done, name))
                            if turned:
                                dve.wait_ge(dve_done, upto(dve_done, (tag, "tok") + turned[-1]))
                            dve.reciprocal(rcv, o[:, :, :, HD]).then_inc(dve_done, M.add(dve_done, (tag, "rc", g, n)))
                            dve.wait_ge(dve_done, upto(dve_done, (tag, "rc", g, n)))
                            dve.tensor_tensor(dst, o[:, :, :, 0:HD], rcv.unsqueeze(3).to_broadcast([P, TPH, GH, HD]), ALU.mult
                                              ).then_inc(dve_done, M.add(dve_done, (tag, "tok", g, n)))
                            turned.append((g, n))

                norm(upto, "ln1", 1e-5)
                dve.wait_ge(conditions_loaded, upto(conditions_loaded, "all"))
                dve.tensor_scalar(mrowb[:], mi[:], 0.0, MASKED, ALU.is_equal, ALU.mult).then_inc(dve_done, M.add(dve_done, "mrowb"))
                dve.tensor_scalar(mcolb[:], mic[:], 0.0, MASKED, ALU.is_equal, ALU.mult).then_inc(dve_done, M.add(dve_done, "mcolb"))
                add_row("L1sa")
                attend("L1sa")
                residual("L1sa", False)
                norm(upto, "ln3", 1e-5)
                add_row("L1ca")
                attend("L1ca")
                residual("L1ca", False)
                norm(upto, "ln2", 1e-5)
                add_row("L1mlp")
                residual("L1mlp", False)
                norm(upto, "ln4", 1e-6)
                dve.wait_ge(mm_done, upto(mm_done, "mod"))
                b = M.where("mod")
                ab = COL["L2_adaln_b"]
                for i in (0, 6):
                    dve.tensor_tensor(mod[:, i:i + 2], ps[:, b, i:i + 2], cols[:, ab + i:ab + i + 2], ALU.add
                                      ).then_inc(dve_done, M.add(dve_done, ("shift", i)))
                    dve.scalar_tensor_tensor(mod[:, i + 2:i + 4], ps[:, b, i + 2:i + 4], 1.0, cols[:, ab + i + 2:ab + i + 4], ALU.add, ALU.add
                                             ).then_inc(dve_done, M.add(dve_done, "mod" if i else ("scale", i)))
                add_gated_row("L2sa", "ln4")
                attend("L2sa")
                residual("L2sa", True)
                norm(upto, "ln5", 1e-6)
                add_row("L2ca")
                attend("L2ca")
                residual("L2ca", False)
                norm(upto, "ln6", 1e-6)
                add_gated_row("L2mlp", "ln6")
                residual("L2mlp", True)
                dve.bn_stats(stc[:], ctxk[:]).then_inc(dve_done, M.add(dve_done, "stc"))
                dve.wait_ge(dve_done, upto(dve_done, "stc"))
                dve.memset(vec[:], 0.0)
                dve.bn_aggr(mvc[:], stc[:]).then_inc(dve_done, M.add(dve_done, "agc"))
                dve.wait_ge(dve_done, upto(dve_done, "agc"))
                dve.tensor_scalar(vec[:], mvc[:, 1:2], 1e-5, None, ALU.add).then_inc(dve_done, M.add(dve_done, "vec"))
                norm(upto, "ln7", 1e-5)
                dve.wait_ge(pool_done, upto(pool_done, "rstdc"))
                dve.tensor_scalar(ctxk[:], ctxk[:], mvc[:, 0:1], rstdc[:], ALU.subtract, ALU.mult).then_inc(dve_done, M.add(dve_done, "ctxn"))
                dve.wait_ge(mm_done, upto(mm_done, "mod3"))
                b = M.where("mod3")
                for i, name in ((0, "L3_bss_q"), (4, "L3_bss_kv")):
                    cb = COL[name]
                    dve.scalar_tensor_tensor(mod3[:, i:i + 2], ps[:, b, i:i + 2], 1.0, cols[:, cb:cb + 2], ALU.add, ALU.add
                                             ).then_inc(dve_done, M.add(dve_done, ("scale3", i)))
                    dve.tensor_tensor(mod3[:, i + 2:i + 4], ps[:, b, i + 2:i + 4], cols[:, cb + 2:cb + 4], ALU.add
                                      ).then_inc(dve_done, M.add(dve_done, "mod3" if i else ("shift3", i)))
                add_row("L3ca")
                attend("L3ca")
                residual("L3ca", False)
            M.close("blocks")

        @block.gpsimd
        def _(pool):
            def rsqrt(upto, tag):
                pool.wait_ge(dve_done, upto(dve_done, (tag, "ve")))
                pool.tensor_tensor(rstd, ve, nhalf, ALU.pow).then_inc(pool_done, M.add(pool_done, (tag, "rstd")))

            pool.wait_ge(dve_done, 1)
            M.open("experts")
            with pool.Fori(0, B) as it:
                def upto(sem, *steps):
                    return M.upto("experts", it, sem, steps)

                rsqrt(upto, "ln0")
            M.close("experts")
            M.open("blocks")
            with pool.Fori(0, B) as it:
                def upto(sem, *steps):
                    return M.upto("blocks", it, sem, steps)

                for tag in ("ln1", "ln3", "ln2", "ln4", "ln5", "ln6"):
                    rsqrt(upto, tag)
                pool.wait_ge(dve_done, upto(dve_done, "vec"))
                pool.tensor_tensor(rstdc[:], vec[:], nhalf[0:S, 0:1], ALU.pow).then_inc(pool_done, M.add(pool_done, "rstdc"))
                rsqrt(upto, "ln7")
            M.close("blocks")


_OUT = (B, N, D)


def kernel(**inputs):
    import numpy as np
    import concourse.bacc as bacc
    from concourse.bass_utils import run_bass_kernel_spmd

    def given(name):
        for full in (name, name.replace("_", "_xcond_", 1)):
            if full in inputs:
                return np.asarray(inputs[full])
        raise KeyError(name)

    cols = np.concatenate([given(n).reshape(-1, P) for n, _ in COLS]).T
    tp_b, ada = given("L1_tp_b").reshape(3, D), given("L2_adaln_b").reshape(6, D)
    router_b = np.zeros((D,), np.float32)
    router_b[0:E] = given("L0_router_b")
    rows = np.stack([given("L0_out_b"), given("L0_gate_b2"), given("L1_sa_bo"), tp_b[0], tp_b[1], tp_b[2], given("L1_ca_bo"),
                     given("L1_b2"), given("L2_sa_proj_b"), ada[2], ada[5], given("L2_ca_proj_b"), given("L2_fc2_b"),
                     given("L3_bp"), router_b])
    ctx, cond, mask = given("ctx_1024"), given("cond_1024"), given("mask_BxS2_ik0")
    twice = np.concatenate([ctx, ctx[:, S - 1:S]], axis=1)
    arrays = {
        "x": given("x"), "ctx": ctx, "ctxT": twice.transpose(0, 2, 1), "condT": cond.reshape(B, KC, P).transpose(0, 2, 1),
        "mask": np.concatenate([mask, mask[:, S - 1:S]], axis=1).reshape(B, 1, SP_), "maskT": mask.reshape(B, S, 1),
        "cols": cols, "rows": rows, "ident": np.eye(P, dtype=np.float32), "sel": selections(),
        "e_b2": given("L0_e_b2"), "router_W": given("L0_router_W"), "L0_WqT": given("L0_Wq").T,
    }
    for n in ("L0_Wk", "L0_Wv", "L0_e_w1", "L0_e_w2", "L0_gate_w1", "L0_gate_w2", "L0_out_w", "L1_sa_wq", "L1_sa_wk", "L1_sa_wv",
              "L1_sa_wo", "L1_ca_wq", "L1_ca_wk", "L1_ca_wv", "L1_ca_wo", "L1_tp_w", "L1_w1", "L1_w2", "L2_adaln_w", "L2_qkv_w",
              "L2_sa_proj_w", "L2_q_w", "L2_kv_w", "L2_ca_proj_w", "L2_fc1_w", "L2_fc2_w", "L3_Wq", "L3_Wkv", "L3_Wp",
              "L3_Wss_q", "L3_Wss_kv"):
        arrays[n] = given(n)
    arrays = {n: np.ascontiguousarray(a) for n, a in arrays.items()}

    def program(marks):
        nc = bacc.Bacc("TRN2", target_bir_lowering=False, num_devices=1)
        T = {n: nc.dram_tensor(f"in_{n}", a.shape, mybir.dt.from_np(a.dtype), kind="ExternalInput").ap() for n, a in arrays.items()}
        T["x0"] = nc.dram_tensor("x_after_block0", _OUT, F32, kind="Internal").ap()
        T["out"] = nc.dram_tensor("out", _OUT, F32, kind="ExternalOutput").ap()
        build(nc, T, marks)
        return nc

    counted = Marks()
    program(counted)
    nc = program(Marks(counted))
    r = run_bass_kernel_spmd(nc, [{f"in_{n}": a for n, a in arrays.items()}], core_ids=[0])
    return r.results[0]["out"]
```

```python
from contextlib import ExitStack

import concourse.bass as bass
from concourse import mybir

F32 = mybir.dt.float32
F32R = mybir.dt.float32r
I32 = mybir.dt.int32
ACT = mybir.ActivationFunctionType
ALU = mybir.AluOpType
AX = mybir.AxisListType

P = 128
B, N, D, S = 4, 1024, 256, 77
KC = D // P
NT = N // P
HALF = 512
NH = N // HALF
TPH = HALF // P
HEADS, HD = 16, 16
GH = 4
GROUPS = HEADS // GH
SP_ = S + 1
E, RH = 3, 512
SW = SP_ + E
RM = E * RH // P
GM = D // P
FF = 4 * D
FM = FF // P
STACK = 64
MAXROW = 32
MASKROW = 33
PAIRS = HEADS // 2
NSEL = 2 * 2 * (PAIRS // KC)
SEL = {"q": 0, "k": NSEL // 2}
MASKED = -1.0e30
SCALE = HD ** -0.5

COLS = [("L0_ln_gamma", 2), ("L0_ln_beta", 2), ("L0_e_b1", RM), ("L0_gate_b1", GM),
        ("L1_ln1_g", 2), ("L1_ln1_b", 2), ("L1_ln3_g", 2), ("L1_ln3_b", 2), ("L1_ln2_g", 2), ("L1_ln2_b", 2),
        ("L1_sa_bq", 2), ("L1_sa_bk", 2), ("L1_sa_bv", 2), ("L1_ca_bq", 2), ("L1_ca_bk", 2), ("L1_ca_bv", 2),
        ("L1_b1", FM), ("L2_adaln_b", 12), ("L2_qkv_b", 6), ("L2_q_b", 2), ("L2_kv_b", 4), ("L2_fc1_b", FM),
        ("L3_bq", 2), ("L3_bkv", 4), ("L3_bss_q", 4), ("L3_bss_kv", 4), ("qs_rows", 1), ("ks_rows", 1)]
COL, NCOL = {}, 0
for _n, _c in COLS:
    COL[_n] = NCOL
    NCOL += _c
ROWS = ["out_b", "gate_b2", "sa_bo", "tp_b0", "tp_b1", "tp_b2", "ca_bo", "b2", "sa_proj_b", "g_sa", "g_ff",
        "ca_proj_b", "fc2_b", "bp", "router_b"]
ROW = {n: i for i, n in enumerate(ROWS)}
NROW = len(ROWS)


class Marks:

    def __init__(self, known=None):
        self.known, self.count, self.at, self.bank = known, {}, {}, {}
        self.start, self.total = {}, {}

    def add(self, sem, step=None, by=1):
        self.count[sem.name] = self.count.get(sem.name, 0) + by
        if step is not None:
            assert (sem.name, step) not in self.at, step
            self.at[sem.name, step] = self.count[sem.name]
        return by

    def open(self, loop):
        self.before = dict(self.count)
        for name, n in self.count.items():
            self.start.setdefault((loop, name), n)

    def close(self, loop):
        for name, n in self.count.items():
            body = n - self.before.get(name, 0)
            if body:
                self.total[loop, name] = body
                self.count[name] += (B - 1) * body

    def upto(self, loop, it, sem, steps):
        if self.known is None:
            return it + 1
        k = self.known
        n = max([k.at[sem.name, step] for step in steps] or [k.start[loop, sem.name]])
        total = k.total.get((loop, sem.name), 0)
        return it * total + n if total else n

    def put(self, step, bank):
        self.bank[step] = bank

    def where(self, step):
        return 0 if self.known is None else self.known.bank[step]


def attention_schedule(cross):
    def stack(g, n, k_by):
        out = []
        for pair in (2 * g, 2 * g + 1):
            out += [("K", "act", "q", pair, n)] + [("K", k_by, "k", pair, n)] * (not (cross and n))
        return out

    def project(*which):
        return [("P",) + w for w in which]

    if cross:
        first = project(("q", 0, 0), ("k", 0, 0), ("q", 1, 0), ("k", 1, 0), ("q", 0, 1), ("q", 1, 1)) + [("V", 0)] + stack(0, 0, "dve")
        beside = stack(1, 0, "dve") + stack(2, 0, "dve") + stack(3, 0, "dve")
        burst = [k for g in range(GROUPS) for k in stack(g, 1, "dve")]
        maxima = []
        for n in range(NH):
            maxima += [("A", g, n, t, 0) for g in range(GROUPS) for t in range(TPH)] + [("M", 0, n)]
        units = [(g, n, 0) for n in range(NH) for g in range(GROUPS)]
        ahead, rate, finish = GROUPS * TPH + 1, 6, 6
    else:
        first = project(("q", 0, 0), ("k", 0, 0), ("k", 0, 1), ("q", 0, 1)) + [k for n in range(NH) for k in stack(0, n, "dve") if k[2] == "k" or n == 0]
        beside = ([("K", "act", "q", pair, 1) for pair in (0, 1)]
                  + [k for n in range(NH) for k in stack(1, n, "act")] + project(*((w, 1, n) for n in range(NH) for w in "qk"))
                  + [k for g in (2, 3) for n in range(NH) for k in stack(g, n, "act")])
        burst = [("V", t2) for t2 in range(NT // 2)]
        maxima, turn = [], []
        for g in range(GROUPS):
            for n in range(NH):
                scores = [("A", g, n, t, j) for t in range(TPH) for j in range(GH)]
                maxima += scores[:2] + turn + scores[2:]
                turn = [("M", g, n)]
        maxima += turn
        units = [(g, n, kt) for g in range(GROUPS) for n in range(NH) for kt in range(NT)]
        ahead, rate, finish = GH * TPH + 8, (GH * TPH + 1) / NT, len(units) - NT + 3
    early = {finish: [("aT", 0, c) for c in range(KC)], finish + 1: [("o", 0)] + [("o", 1)] * cross, finish + 2: [("o", 1)] * (not cross)}
    lag = 1 if cross else 2
    steps = list(first)
    taken = 0

    def more(upto):
        nonlocal taken
        upto = min(int(upto), len(maxima))
        out = maxima[taken:upto]
        taken = max(taken, upto)
        return out

    lead = more(ahead)
    per = 2
    assert len(beside) <= per * len(lead)
    for i, step in enumerate(lead):
        steps += [step] + beside[i * per:(i + 1) * per]
    for i, step in enumerate(burst):
        steps.append(step)
        if not cross:
            steps += more(taken + 1)
    ahead = taken
    turn = None
    for u in range(len(units) + lag):
        if u < len(units):
            steps += more(ahead + rate * (u + 0.5)) + [("S",) + units[u] + (j,) for j in range(2)]
        if turn is not None:
            steps.append(("OT",) + turn)
            turn = None
        if u >= lag:
            unit = units[u - lag]
            steps.append(("PV",) + unit)
            if u - lag + 1 == len(units) or units[u - lag + 1][:2] != unit[:2]:
                steps.append(("O",) + unit[:2])
                turn = unit[:2]
        if u < len(units):
            steps += more(ahead + rate * (u + 1)) + [("S",) + units[u] + (j,) for j in range(2, GH)]
        steps += early.get(u, [])
    steps.append(("OT",) + turn)
    steps += [("aT", NH - 1, c) for c in range(KC)] + [("o", 2), ("o", 3)]
    return steps


SELF, CROSS = attention_schedule(False), attention_schedule(True)


def stacked(e, lo, hi):
    return slice(STACK * e + lo, STACK * e + hi)


def stacks_for(cross, engine, g, n):
    return [k for k in (CROSS if cross else SELF) if k[0] == "K" and k[1] == engine
            and k[3] * 2 // GH == g and (k[2] == "k" or k[4] == n)]


def constant_rows(row):
    import numpy as np

    out = np.zeros((P, 1), np.float32)
    out[[row, STACK + row]] = 1.0
    return out


def selections():
    import numpy as np

    out = np.zeros((P, NSEL + 1, P), np.float32)
    out[0, NSEL, [MASKROW, STACK + MASKROW]] = 1.0
    for which, places in (("q", ((0, 16), (48,))), ("k", ((0, 48), (16,)))):
        for part in range(2):
            for pp in range(PAIRS // KC):
                for e in range(2):
                    for row in places[part]:
                        for d in range(HD):
                            out[(2 * pp + e) * HD + d, SEL[which] + part * (PAIRS // KC) + pp, STACK * e + row + d] = 1.0
    return out


def build(nc, T, M):
    ctx = ExitStack()
    with ctx:
        at = [16512]

        def place(name, shape, dt=F32, offset=None):
            size = 4
            for d in shape[1:]:
                size *= d
            size = -(-size // 32) * 32
            if offset is None:
                offset = at[0]
                at[0] += size
            return nc.alloc_sbuf_tensor_at(name, shape, dt, offset=offset)

        def sem(name):
            return ctx.enter_context(nc.semaphore(name))

        r1 = at[0]
        qs = place("qs", [P, PAIRS, N], F32R)
        ks = place("ks", [P, PAIRS, N], F32R)
        kz = place("kz", [P, PAIRS, 2, SP_], F32R, offset=at[0] - 4 * PAIRS * N)
        r1_end, at[0] = at[0], r1
        ew1 = place("ew1", [P, 6, E, RH])
        ew2 = place("ew2", [P, RM, D])
        gw1 = place("gw1", [P, 6, D])
        gw2 = place("gw2", [P, KC, D])
        outw = place("outw", [P, KC, D])
        wqT = place("wqT", [P, KC, D])
        wk0 = place("wk0", [P, KC, D])
        wv0 = place("wv0", [P, KC, D])
        assert at[0] <= r1_end
        at[0] = r1_end
        r2 = at[0]
        probs = place("probs", [P, 4, GH, HALF])
        r2_end, at[0] = at[0], r2
        qh = place("qh", [P, KC, N], F32R)
        ql = place("ql", [P, KC, N], F32R)
        kh = place("kh", [P, KC, N], F32R)
        kl = place("kl", [P, KC, N], F32R)
        assert at[0] <= r2_end
        at[0] = r2
        hid = place("hid", [P, NH, FM, HALF])
        at[0] = r2
        hid0 = place("hid0", [P, RM + GM, HALF])
        at[0] = r2
        sel_in = place("sel_in", [P, NSEL + 1, P])
        at[0] = r2_end
        x = place("x", [P, NT, D])
        hT = place("hT", [P, KC, N])
        tok = place("tok", [P, NT, D])
        whole = place("whole", [P, 4, HALF], offset=at[0] - 4 * NT * D)
        pb = place("pb", [P, E, HALF], offset=at[0] - 4 * NT * D)
        v = place("v", [P, NT, HEADS, 32])
        ow = place("ow", [P, N])
        wT = place("wT", [P, N], offset=at[0] - 4 * N)
        rT = place("rT", [P, KC, HALF])
        mrow = place("mrow", [P, N], offset=at[0] - 4 * N)
        slot = [place(f"slot{i}", [P, 2048]) for i in range(4)]
        after_slots, at[0] = at[0], at[0] - 3 * 4 * 2048
        u0 = place("u0", [P, RM * P + D + E])
        pT = place("pT", [E, N])
        kv0T = place("kv0T", [P, 2 * KC, SP_])
        a0 = place("a0", [P, KC, SW])
        e1 = place("e1", [P, TPH, SP_])
        eb2 = place("eb2", [E, D])
        assert at[0] <= after_slots
        at[0] = after_slots
        adw = place("adw", [P, KC, 6 * D])
        xin = place("xin", [P, NT, D], offset=at[0] - 4 * KC * 6 * D)
        tpw = place("tpw", [P, KC, 3 * D], offset=at[0] - 4 * KC * 6 * D)
        ident = place("ident", [P, P])
        sel = place("sel", [P, NSEL + 1, P], F32R)
        cols = place("cols", [P, NCOL])
        rows = place("rows", [NROW, D])
        router = place("router", [P, 6, E])
        cond = place("cond", [P, KC])
        scond = place("scond", [P, KC])
        ctxT = place("ctxT", [P, KC, SP_])
        ctxk = place("ctxk", [S, D])
        kvT = place("kvT", [P, KC, SP_])
        e0 = place("e0", [P, TPH, SP_])
        e01 = (e0, e1)
        small = place("small", [P, 128])
        mi = place("mi", [1, SP_], I32)
        mic = place("mic", [S, 1], I32)
        mrowb, mcolb = place("mrowb", [1, SP_], F32R), place("mcolb", [S, 1])
        mx = place("mx", [P, 2, TPH, HEADS])
        grow = place("grow", [P, D])
        rrow = place("rrow", [P, D])
        sg = place("sg", [P, 2, 2, D], offset=r2_end - 4 * N)
        assert 4 * (RM + GM) * HALF + 4 * N <= r2_end - r2

        st = small[:, 0:6 * NT].rearrange("p (t k) -> p t k", k=6)
        mv = small[:, 48:48 + 2 * NT].rearrange("p (t k) -> p t k", k=2)
        ve, rstd, nhalf = small[:, 64:72], small[:, 72:80], small[:, 80:88]
        nmx, es, rc4 = small[:, 102:110], small[:, 110:118], small[:, 118:126]
        lg = place("lg", [P, NT, E])
        qs_rows, ks_rows = (cols[:, COL[n]:COL[n] + 1] for n in ("qs_rows", "ks_rows"))
        rc = place("rc", [P, TPH * GH])
        rmx, rs, rrs = place("rmx", [P, NT]), place("rs", [P, NT]), place("rrs", [P, NT])
        mod = place("mod", [P, 12])
        mod3 = place("mod3", [P, 8])
        stc, mvc = place("stc", [S, 6]), place("mvc", [S, 2])
        vec, rstdc = place("vec", [S, 1]), place("rstdc", [S, 1])
        assert at[0] <= 229368, at[0]

        ps = ctx.enter_context(nc.psum_tensor("ps", [P, 8, HALF], F32))

        def w256(i, k, n=D):
            return slot[i][:, 512 * k:512 * k + KC * n].rearrange("p (c n) -> p c n", c=KC)

        W1 = slot[2][:].rearrange("p (c n) -> p c n", c=KC)
        W2 = slot[3][:].rearrange("p (c n) -> p c n", c=FM)

        mm_done, act_done, dve_done, pool_done = sem("mm_done"), sem("act_done"), sem("dve_done"), sem("pool_done")
        constants_loaded = sem("constants_loaded")
        experts_loaded = {name: sem(f"experts_{name}_loaded") for name in ("kv", "q", "in", "out")}
        xin_loaded, residual_loaded, conditions_loaded = sem("xin_loaded"), sem("residual_loaded"), sem("conditions_loaded")
        x_loaded = [sem(f"x{t2}_loaded") for t2 in range(4)]
        slot_loaded = [sem(f"slot{i}_loaded") for i in range(5)]
        maxima_stacked = [[sem(f"maxima_{g}_{n}_stacked") for n in range(NH)] for g in range(GROUPS)]
        x_stored, out_stored = sem("x_stored"), [sem(f"out{t2}_stored") for t2 in range(4)]

        block = ctx.enter_context(nc.Block())

        def col(name, c):
            return cols[:, COL[name] + c:COL[name] + c + 1]

        ATT = {
            "L1sa": (False, w256(0, 0), w256(0, 1), w256(0, 2), w256(0, 3), ("L1_sa_bq", 0), ("L1_sa_bk", 0), ("L1_sa_bv", 0)),
            "L1ca": (True, w256(1, 0), w256(1, 1), w256(1, 2), w256(1, 3), ("L1_ca_bq", 0), ("L1_ca_bk", 0), ("L1_ca_bv", 0)),
            "L2sa": (False, w256(0, 0, 768)[:, :, 0:D], w256(0, 0, 768)[:, :, D:2 * D], w256(0, 0, 768)[:, :, 2 * D:],
                     w256(0, 3), ("L2_qkv_b", 0), ("L2_qkv_b", 2), ("L2_qkv_b", 4)),
            "L2ca": (True, w256(1, 0), w256(1, 1, 512)[:, :, 0:D], w256(1, 1, 512)[:, :, D:], w256(1, 3),
                     ("L2_q_b", 0), ("L2_kv_b", 0), ("L2_kv_b", 2)),
            "L3ca": (True, w256(2, 0), w256(2, 1, 512)[:, :, 0:D], w256(2, 1, 512)[:, :, D:], w256(2, 3),
                     ("L3_bq", 0), ("L3_bkv", 0), ("L3_bkv", 2)),
        }
        SLOT_OF = {"L1sa": slot_loaded[0], "L1ca": slot_loaded[1], "L2sa": slot_loaded[0], "L2ca": slot_loaded[1],
                   "L3ca": slot_loaded[2]}
        LN_OF = {"L1sa": "ln1", "L1ca": "ln3", "L2sa": "ln4", "L2ca": "ln5", "L3ca": "ln7"}
        XNEXT = {"ln3": "L1sa", "ln2": "L1ca", "ln4": "L1mlp", "ln5": "L2sa", "ln6": "L2ca", "ln7": "L2mlp"}
        LOADED = 16

        def wide(src):
            return src.rearrange("(c p) n -> p c n", p=P)

        def maxima_of(tag, g, n):
            return (n, HEADS, GH * g, ("M", 0, n)) if ATT[tag][0] else ((NH * g + n) % 2, GH, 0, ("M", g, n))

        @block.sync
        def _(sp):
            sp.dma_start(ident[:], T["ident"]).then_inc(constants_loaded, LOADED)
            sp.dma_start(router[:], wide(T["router_W"])).then_inc(constants_loaded, LOADED)
            sp.dma_start(cols[:], T["cols"]).then_inc(constants_loaded, LOADED)
            sp.dma_start(rows[:], T["rows"]).then_inc(constants_loaded, LOADED)
            sp.dma_start(eb2[:], T["e_b2"]).then_inc(constants_loaded, LOADED)
            sp.dma_start(sel_in[:], T["sel"]).then_inc(constants_loaded, LOADED)
            inner = [(ew1[:, c], T["L0_e_w1"][:, c * P:(c + 1) * P, :].rearrange("e p r -> p e r")) for c in (2, 3, 4, 5, 0, 1)]
            outer = [(ew2[:, e * 4:(e + 1) * 4], wide(T["L0_e_w2"][e])) for e in range(E)]
            for name, parts in (("kv", [(wk0[:], wide(T["L0_Wk"])), (wv0[:], wide(T["L0_Wv"]))]),
                                ("q", [(wqT[:], wide(T["L0_WqT"]))]),
                                ("in", inner + [(gw1[:], wide(T["L0_gate_w1"]))]),
                                ("out", outer + [(gw2[:], wide(T["L0_gate_w2"])), (outw[:], wide(T["L0_out_w"]))])):
                for i, (dst, src) in enumerate(parts):
                    sp.dma_start(dst, src).then_inc(experts_loaded[name], M.add(experts_loaded[name], i, LOADED))
            for k, n in enumerate(("wq", "wk", "wv", "wo")):
                sp.dma_start(w256(0, k), wide(T[f"L1_sa_{n}"])).then_inc(slot_loaded[0], M.add(slot_loaded[0], ("L1sa", k), LOADED))
            sp.wait_ge(xin_loaded, (B + 1) * LOADED)
            M.open("blocks")
            with sp.Fori(0, B) as it:
                def upto(sem, *steps):
                    return M.upto("blocks", it, sem, steps)

                sp.wait_ge(mm_done, upto(mm_done))
                sp.dma_start(tpw[:], wide(T["L1_tp_w"])).then_inc(slot_loaded[4], M.add(slot_loaded[4], "L1", LOADED))
                for k, n in enumerate(("wq", "wk", "wv", "wo")):
                    sp.dma_start(w256(1, k), wide(T[f"L1_ca_{n}"])).then_inc(slot_loaded[1], M.add(slot_loaded[1], ("L1ca", k), LOADED))
                sp.dma_start(W1, wide(T["L1_w1"])).then_inc(slot_loaded[2], M.add(slot_loaded[2], "L1mlp", LOADED))
                sp.dma_start(W2, wide(T["L1_w2"])).then_inc(slot_loaded[3], M.add(slot_loaded[3], "L1mlp", LOADED))

                def stack_maxima(tag):
                    if ATT[tag][0]:
                        order = [(g, n) for n in range(NH) for g in range(GROUPS)]
                    else:
                        order = [(g, n) for g in range(GROUPS) for n in range(NH)]
                    for g, n in order:
                        z, _, j0, step = maxima_of(tag, g, n)
                        sp.wait_ge(act_done, upto(act_done, (tag,) + step))
                        for j in range(GH):
                            h = GH * g + j
                            sp.dma_start(qs[stacked(h % 2, MAXROW, MAXROW + 1), h // 2, n * HALF:(n + 1) * HALF].bitcast(F32),
                                         mrow[j0 + j:j0 + j + 1, z * HALF:(z + 1) * HALF]
                                         ).then_inc(maxima_stacked[g][n], M.add(maxima_stacked[g][n], (tag, j), LOADED))

                stack_maxima("L1sa")
                sp.wait_ge(mm_done, upto(mm_done, ("L1sa", "o", 3)))
                sp.dma_start(w256(0, 0, 768), wide(T["L2_qkv_w"])).then_inc(slot_loaded[0], M.add(slot_loaded[0], ("L2sa", 0), LOADED))
                sp.dma_start(w256(0, 3), wide(T["L2_sa_proj_w"])).then_inc(slot_loaded[0], M.add(slot_loaded[0], ("L2sa", 3), LOADED))
                stack_maxima("L1ca")
                sp.wait_ge(mm_done, upto(mm_done, ("L1ca", "o", 3)))
                sp.dma_start(w256(1, 0), wide(T["L2_q_w"])).then_inc(slot_loaded[1], M.add(slot_loaded[1], ("L2ca", 0), LOADED))
                sp.dma_start(w256(1, 1, 512), wide(T["L2_kv_w"])).then_inc(slot_loaded[1], M.add(slot_loaded[1], ("L2ca", 1), LOADED))
                sp.dma_start(w256(1, 3), wide(T["L2_ca_proj_w"])).then_inc(slot_loaded[1], M.add(slot_loaded[1], ("L2ca", 3), LOADED))
                sp.wait_ge(mm_done, upto(mm_done, ("row", "L1mlp")))
                sp.dma_start(adw[:], wide(T["L2_adaln_w"])).then_inc(slot_loaded[4], M.add(slot_loaded[4], "L2", LOADED))
                sp.wait_ge(mm_done, upto(mm_done, ("L1mlp", "h", NH - 1, FM - 1)))
                sp.dma_start(W1, wide(T["L2_fc1_w"])).then_inc(slot_loaded[2], M.add(slot_loaded[2], "L2mlp", LOADED))
                sp.wait_ge(mm_done, upto(mm_done, ("L1mlp", "o", 3)))
                sp.dma_start(W2, wide(T["L2_fc2_w"])).then_inc(slot_loaded[3], M.add(slot_loaded[3], "L2mlp", LOADED))
                stack_maxima("L2sa")
                sp.wait_ge(mm_done, upto(mm_done, ("L2sa", "o", 3)))
                for k, n in enumerate(("wq", "wk", "wv", "wo")):
                    sp.dma_start(w256(0, k), wide(T[f"L1_sa_{n}"])).then_inc(slot_loaded[0], M.add(slot_loaded[0], None, LOADED))
                stack_maxima("L2ca")
                sp.wait_ge(mm_done, upto(mm_done, ("L2ca", "o", 3)))
                sp.dma_start(w256(1, 0, 512), wide(T["L3_Wss_q"])).then_inc(slot_loaded[1], M.add(slot_loaded[1], None, LOADED))
                sp.dma_start(w256(1, 2, 512), wide(T["L3_Wss_kv"])).then_inc(slot_loaded[1], M.add(slot_loaded[1], "L3ss", LOADED))
                sp.wait_ge(mm_done, upto(mm_done, ("L2mlp", "h", NH - 1, FM - 1)))
                sp.dma_start(w256(2, 0), wide(T["L3_Wq"])).then_inc(slot_loaded[2], M.add(slot_loaded[2], ("L3ca", 0), LOADED))
                sp.dma_start(w256(2, 1, 512), wide(T["L3_Wkv"])).then_inc(slot_loaded[2], M.add(slot_loaded[2], ("L3ca", 1), LOADED))
                sp.dma_start(w256(2, 3), wide(T["L3_Wp"])).then_inc(slot_loaded[2], M.add(slot_loaded[2], ("L3ca", 3), LOADED))
                stack_maxima("L3ca")
            M.close("blocks")

        @block.tensor
        def _(pe):
            owner = {}
            ring = [0]

            def mm(out, lhsT, rhs, start=True, stop=True):
                return pe.matmul(out, lhsT, rhs, start=start, stop=stop)

            def take(step, act=None, dve=None, banks=None):
                if banks is None:
                    banks = (ring[0] % 8,)
                    ring[0] += 1
                was = [owner[b] for b in banks if b in owner]
                for b in banks:
                    owner[b] = ("act", act) if act else ("dve", dve)
                M.put(step, banks[0])
                return banks[0], [s for e, s in was if e == "act"], [s for e, s in was if e == "dve"]

            def pick(name, n=P):
                r = ROW[name]
                return ident[0:NROW, r:r + 1].to_broadcast([NROW, n]), rows[:]

            def turn(upto, tag):
                for n in range(NH):
                    for c in range(KC):
                        b, act_was, dve_was = take((tag, "T", n, c), act=(tag, "hT", n, c))
                        pe.wait_ge(act_done, upto(act_done, *act_was))
                        for i in range(TPH):
                            t = TPH * n + i
                            pe.wait_ge(dve_done, upto(dve_done, (tag, "xh", t), *dve_was))
                            ins = pe.transpose(ps[:, b, i * P:(i + 1) * P], tok[:, t, c * P:(c + 1) * P], ident[:])
                        ins.then_inc(mm_done, M.add(mm_done, (tag, "T", n, c)))

            pe.wait_ge(constants_loaded, 6 * LOADED)
            pe.wait_ge(dve_done, 1)
            pe.transpose(ps[:, 0, 0:P], ident[:], ident[:]).then_inc(mm_done, M.add(mm_done))
            M.open("experts")
            with pe.Fori(0, B) as it:
                def upto(sem, *steps):
                    return M.upto("experts", it, sem, steps)

                b, act_was, dve_was = take(("L0", "kv"), act=("L0", "kv"))
                pe.wait_ge(act_done, upto(act_done))
                pe.wait_ge(dve_done, upto(dve_done))
                pe.wait_ge(conditions_loaded, upto(conditions_loaded, "first"))
                pe.wait_ge(experts_loaded["kv"], 2 * LOADED)
                for i, w in enumerate((wk0, wv0)):
                    for c in range(KC):
                        o = (i * KC + c) * SP_
                        for k in range(KC):
                            ins = mm(ps[:, b, o:o + SP_], w[:, k, c * P:(c + 1) * P], ctxT[:, k, :], k == 0, k == KC - 1)
                ins.then_inc(mm_done, M.add(mm_done, ("L0", "kv")))
                b, act_was, dve_was = take(("L0", "a"), act=("L0", "a"))
                pe.wait_ge(act_done, upto(act_done, ("L0", "kv")))
                pe.wait_ge(experts_loaded["q"], LOADED)
                for c in range(KC):
                    for k in range(KC):
                        ins = mm(ps[:, b, c * SP_:(c + 1) * SP_], wqT[:, k, c * P:(c + 1) * P], kv0T[:, k, :], k == 0, k == KC - 1)
                ins.then_inc(mm_done, M.add(mm_done, ("L0", "a")))
                for e in range(E + 1):
                    b, act_was, dve_was = take(("L0", "u", e), dve=("L0", "u", e))
                    pe.wait_ge(act_done, upto(act_done, *act_was))
                    pe.wait_ge(dve_done, upto(dve_done, *dve_was))
                    pe.wait_ge(experts_loaded["in"], 7 * LOADED)
                    all_keys = [cond[:, k:k + 1].to_broadcast([P, S]) for k in range(KC)]
                    for k in range(KC):
                        keys, inner, anchor = kv0T[:, KC + k, 0:S], KC + k, 2 * KC + k
                        if e < E:
                            mm(ps[0:S, b, :], keys, ew1[:, inner, e, :], k == 0, False)
                            ins = mm(ps[0:S, b, :], all_keys[k], ew1[:, anchor, e, :], False, k == KC - 1)
                        else:
                            mm(ps[0:S, b, 0:D], keys, gw1[:, inner, :], k == 0, False)
                            mm(ps[0:S, b, 0:D], all_keys[k], gw1[:, anchor, :], False, k == KC - 1)
                    if e == E:
                        lhs, rr = pick("router_b", S)
                        mm(ps[0:S, b, D:D + E], lhs, rr[:, 0:E], True, False)
                        for k in range(KC):
                            mm(ps[0:S, b, D:D + E], kv0T[:, KC + k, 0:S], router[:, KC + k, :], False, False)
                            ins = mm(ps[0:S, b, D:D + E], all_keys[k], router[:, 2 * KC + k, :], False, k == KC - 1)
                    ins.then_inc(mm_done, M.add(mm_done, ("L0", "u", e)))
                turn(upto, "ln0")
                for n in range(NH):
                    b, act_was, dve_was = take(("L0", "s", n), act=("L0", "e", n, TPH - 1))
                    pe.wait_ge(act_done, upto(act_done, ("L0", "a"), *(("ln0", "hT", n, c) for c in range(KC)), *act_was))
                    pe.wait_ge(dve_done, upto(dve_done, *dve_was))
                    for i in range(TPH):
                        t = TPH * n + i
                        for k in range(KC):
                            ins = mm(ps[:, b, i * SW:(i + 1) * SW], hT[:, k, t * P:(t + 1) * P], a0[:, k, :], k == 0, k == KC - 1)
                    ins.then_inc(mm_done, M.add(mm_done, ("L0", "s", n)))

                def hidden(n, m):
                    b, act_was, dve_was = take(("L0", "h", n, m), act=("L0", "h", n, m))
                    pe.wait_ge(act_done, upto(act_done, *act_was))
                    pe.wait_ge(dve_done, upto(dve_done, *dve_was))
                    for k in range(KC):
                        w = ew1[:, k, m // 4, (m % 4) * P:(m % 4 + 1) * P] if m < RM else gw1[:, k, (m - RM) * P:(m - RM + 1) * P]
                        mm(ps[:, b, :], w, hT[:, k, n * HALF:(n + 1) * HALF], k == 0, False)
                    return b

                def evidence(n, m, b):
                    mm(ps[:, b, :], u0[0:S, m * P:(m + 1) * P], wT[0:S, n * HALF:(n + 1) * HALF], False, True
                       ).then_inc(mm_done, M.add(mm_done, ("L0", "h", n, m)))

                def output(n):
                    for i2 in range(2):
                        t2 = 2 * n + i2
                        b, act_was, dve_was = take(("L0", "o", t2), dve=("L0", "sg", t2))
                        pe.wait_ge(act_done, upto(act_done, *(("L0", "rt", n, c) for c in range(KC)), *act_was))
                        pe.wait_ge(dve_done, upto(dve_done, *dve_was))
                        for i in range(2):
                            tt = slice((2 * i2 + i) * P, (2 * i2 + i + 1) * P)
                            mm(ps[:, b, i * D:(i + 1) * D], *pick("out_b"), True, False)
                            for k in range(KC):
                                ins = mm(ps[:, b, i * D:(i + 1) * D], rT[:, k, tt], outw[:, k, :], False, k == KC - 1)
                        ins.then_inc(mm_done, M.add(mm_done, ("L0", "o", t2)))

                early = [hidden(0, m) for m in range(4)]
                for n in range(NH):
                    b, act_was, dve_was = take(("L0", "wT", n), act=("L0", "wT", n))
                    pe.wait_ge(act_done, upto(act_done, *act_was))
                    pe.wait_ge(dve_done, upto(dve_done, ("L0", "w", n), *dve_was))
                    for i in range(TPH):
                        ins = pe.transpose(ps[0:S, b, i * P:(i + 1) * P], e01[n][:, i, 0:S], ident[:])
                    ins.then_inc(mm_done, M.add(mm_done, ("L0", "wT", n)))
                for n in range(NH):
                    b, act_was, dve_was = take(("L0", "r", n), dve=("L0", "lt", n))
                    pe.wait_ge(act_done, upto(act_done, ("L0", "wT", n), *act_was))
                    pe.wait_ge(dve_done, upto(dve_done, ("L0", "u", E), *dve_was))
                    for i in range(TPH):
                        t = TPH * n + i
                        ins = mm(ps[:, b, i * E:(i + 1) * E], wT[0:S, t * P:(t + 1) * P], u0[0:S, RM * P + D:])
                    ins.then_inc(mm_done, M.add(mm_done, ("L0", "r", n)))
                for n in range(NH):
                    half = slice(n * HALF, (n + 1) * HALF)
                    for m in range(RM + GM):
                        evidence(n, m, early[m] if n == 0 and m < len(early) else hidden(n, m))
                        if n and m == 2:
                            output(n - 1)
                        if m // 4 == 2 and m % 4 < E:
                            e = m % 4
                            b, act_was, dve_was = take(("L0", "pb", n, e), act=("L0", "pb", n, e))
                            pe.wait_ge(act_done, upto(act_done, *act_was))
                            pe.wait_ge(dve_done, upto(dve_done, ("L0", "p"), *dve_was))
                            for i in range(TPH):
                                ins = mm(ps[:, b, i * P:(i + 1) * P], lg[:, TPH * n + i, e:e + 1].to_broadcast([P, P]), ident[:])
                            ins.then_inc(mm_done, M.add(mm_done, ("L0", "pb", n, e)))
                    b, act_was, dve_was = take(("L0", "pT", n), act=("L0", "pT", n))
                    pe.wait_ge(act_done, upto(act_done, *act_was))
                    pe.wait_ge(dve_done, upto(dve_done, *dve_was))
                    for i in range(TPH):
                        ins = pe.transpose(ps[0:E, b, i * P:(i + 1) * P], lg[:, TPH * n + i, :], ident[:])
                    ins.then_inc(mm_done, M.add(mm_done, ("L0", "pT", n)))
                    for i2 in range(2):
                        t2 = 2 * n + i2
                        b, act_was, dve_was = take(("L0", "g", t2), act=("L0", "g", t2))
                        pe.wait_ge(act_done, upto(act_done, *(("L0", "h", n, RM + c) for c in range(KC)), *act_was))
                        pe.wait_ge(dve_done, upto(dve_done, *dve_was))
                        pe.wait_ge(experts_loaded["out"], 5 * LOADED)
                        for i in range(2):
                            tt = slice((2 * i2 + i) * P, (2 * i2 + i + 1) * P)
                            mm(ps[:, b, i * D:(i + 1) * D], *pick("gate_b2"), True, False)
                            for k in range(KC):
                                ins = mm(ps[:, b, i * D:(i + 1) * D], hid0[:, RM + k, tt], gw2[:, k, :], False, k == KC - 1)
                        ins.then_inc(mm_done, M.add(mm_done, ("L0", "g", t2)))
                    for c in range(KC):
                        b, act_was, dve_was = take(("L0", "rt", n, c), act=("L0", "rt", n, c))
                        pe.wait_ge(act_done, upto(act_done, ("L0", "pT", n), *act_was))
                        pe.wait_ge(dve_done, upto(dve_done, *dve_was))
                        mm(ps[:, b, :], eb2[:, c * P:(c + 1) * P], pT[:, half], True, False)
                        for m in range(RM):
                            if c == 0:
                                pe.wait_ge(dve_done, upto(dve_done, ("L0", "hp", n, m)))
                            ins = mm(ps[:, b, :], ew2[:, m, c * P:(c + 1) * P], hid0[:, m, :], False, m == RM - 1)
                        ins.then_inc(mm_done, M.add(mm_done, ("L0", "rt", n, c)))
                output(NH - 1)
            M.close("experts")

            owner.clear()
            M.open("blocks")
            with pe.Fori(0, B) as it:
                def upto(sem, *steps):
                    return M.upto("blocks", it, sem, steps)

                def row(tag, terms, reader):
                    b, act_was, dve_was = take(("row", tag), dve=reader)
                    pe.wait_ge(act_done, upto(act_done, "scond", *act_was))
                    pe.wait_ge(dve_done, upto(dve_done, *dve_was))
                    for i, (a, r) in enumerate(terms):
                        ins = mm(ps[:, b, 0:D], a, r, i == 0, i == len(terms) - 1)
                    ins.then_inc(mm_done, M.add(mm_done, ("row", tag)))

                def silu_cond(w):
                    return [(scond[:, c:c + 1].to_broadcast([P, P]), w[:, c, :]) for c in range(KC)]

                def attend(tag):
                    cross, wq, wk, wv, wo, *_ = ATT[tag]
                    ln = LN_OF[tag]
                    kw = S if cross else P
                    src = {"L3ca": kvT}.get(tag, ctxT if cross else hT)
                    pe.wait_ge(SLOT_OF[tag], upto(SLOT_OF[tag], (tag, 3)))
                    pairs, singles, unit = 0, 0, {}
                    for step in (CROSS if cross else SELF):
                        kind = step[0]
                        if kind == "P":
                            which, c, n = step[1:]
                            w, rows_in, kn = (wq, hT, HALF) if which == "q" else (wk, src, SP_ if cross else HALF)
                            b, act_was, dve_was = take((tag,) + step, act=(tag,) + step, banks=(4 + singles % 3,))
                            singles += 1
                            pe.wait_ge(act_done, upto(act_done, *((ln, "hT", n, k) for k in range(KC)), *act_was))
                            pe.wait_ge(dve_done, upto(dve_done, *dve_was))
                            for k in range(KC):
                                ins = mm(ps[:, b, 0:kn], w[:, k, c * P:(c + 1) * P], rows_in[:, k, n * HALF:n * HALF + kn], k == 0, k == KC - 1)
                        elif kind == "V":
                            t2 = step[1]
                            b, act_was, dve_was = take((tag,) + step, act=(tag,) + step, banks=(4 + singles % 3,))
                            singles += 1
                            pe.wait_ge(act_done, upto(act_done, *((ln, "hT", t2 // 2, k) for k in range(KC)), *act_was))
                            pe.wait_ge(dve_done, upto(dve_done, *dve_was))
                            for i in range(1 if cross else 2):
                                t = 2 * t2 + i
                                for k in range(KC):
                                    ins = mm(ps[0:kw, b, i * D:(i + 1) * D], src[:, k, t * P:t * P + kw], wv[:, k, :], k == 0, k == KC - 1)
                        elif kind == "K":
                            who, which, pair, n = step[1:]
                            hi, lo = (qh, ql) if which == "q" else (kh, kl)
                            c, pp = divmod(pair, PAIRS // KC)
                            kn = SP_ if cross and which == "k" else HALF
                            part = slice(n * HALF, n * HALF + kn)
                            name = (tag,) + step
                            b, act_was, dve_was = take(name, banks=(4 + singles % 3,), **{who: name})
                            singles += 1
                            pe.wait_ge(act_done, upto(act_done, *act_was))
                            pe.wait_ge(dve_done, upto(dve_done, *dve_was))
                            pe.wait_ge(pool_done, upto(pool_done, (tag, "P", which, c, n)))
                            s = SEL[which] + pp
                            mm(ps[:, b, 0:kn], sel[:, s, :], hi[:, c, part], True, False)
                            masked = tag == "L1ca" and which == "k"
                            ins = mm(ps[:, b, 0:kn], sel[:, s + PAIRS // KC, :], lo[:, c, part], False, not masked)
                            if masked:
                                pe.wait_ge(dve_done, upto(dve_done, "mrowb"))
                                ins = mm(ps[:, b, 0:kn], sel[0:1, NSEL, :], mrowb[:], False, True)
                        elif kind == "A":
                            g, n, t, j = step[1:]
                            a = 2 * (pairs % 2)
                            pairs += 1
                            _, act_was, dve_was = take((tag,) + step, dve=(tag,) + step, banks=(a, a + 1))
                            pe.wait_ge(act_done, upto(act_done, *((tag,) + k for k in stacks_for(cross, "act", g, n)), *act_was))
                            pe.wait_ge(dve_done, upto(dve_done, *((tag,) + k for k in stacks_for(cross, "dve", g, n)), *dve_was))
                            tt = slice((TPH * n + t) * P, (TPH * n + t + 1) * P)
                            if cross:
                                for pair in (2 * g, 2 * g + 1):
                                    o = pair % 2 * 2 * SP_
                                    ins = mm(ps[:, a, o:o + 2 * SP_], qs[:, pair, tt], kz[:, pair])
                            else:
                                h = GH * g + j
                                r = stacked(h % 2, 0, STACK)
                                for i in range(2):
                                    ins = mm(ps[:, a + i, :], qs[r, h // 2, tt], ks[r, h // 2, i * HALF:(i + 1) * HALF])
                        elif kind == "M":
                            g, n = step[1:]
                            z, w, _, _ = maxima_of(tag, g, n)
                            a = 2 * (pairs % 2)
                            pairs += 1
                            _, act_was, dve_was = take((tag,) + step, act=(tag,) + step, banks=(a, a + 1))
                            pe.wait_ge(act_done, upto(act_done, *act_was))
                            last = ("A", GROUPS - 1, n, TPH - 1, 0) if cross else ("A", g, n, TPH - 1, GH - 1)
                            pe.wait_ge(dve_done, upto(dve_done, (tag,) + last, *dve_was))
                            for t in range(TPH):
                                ins = pe.transpose(ps[0:w, a, t * P:(t + 1) * P], mx[:, z, t, 0:w], ident[:])
                        elif kind == "S":
                            g, n, kt, j = step[1:]
                            if (kt, j) == (0, 0):
                                pe.wait_ge(maxima_stacked[g][n], upto(maxima_stacked[g][n], (tag, GH - 1)))
                            b, act_was, dve_was = take((tag,) + step, act=(tag,) + step, banks=(4 + singles % 3,))
                            singles += 1
                            pe.wait_ge(act_done, upto(act_done, *act_was))
                            pe.wait_ge(dve_done, upto(dve_done, *dve_was))
                            h = GH * g + j
                            if cross:
                                ins = mm(ps[0:kw, b, :], kz[:, h // 2, h % 2, 0:kw], qs[:, h // 2, n * HALF:(n + 1) * HALF])
                            else:
                                r = stacked(h % 2, 0, STACK)
                                ins = mm(ps[:, b, :], ks[r, h // 2, kt * P:(kt + 1) * P], qs[r, h // 2, n * HALF:(n + 1) * HALF])
                        elif kind == "PV":
                            g, n, kt = step[1:]
                            u = unit.setdefault((g, n, kt), len(unit)) % 4
                            act_was = []
                            if kt == 0:
                                _, act_was, dve_was = take((tag,) + step, act=(tag, "O", g, n), banks=(7,))
                                pe.wait_ge(dve_done, upto(dve_done, *dve_was))
                            pe.wait_ge(act_done, upto(act_done, (tag, "S", g, n, kt, GH - 1), (tag, "V", 0 if cross else kt // 2), *act_was))
                            for j in range(GH):
                                ins = mm(ps[32 * j:32 * j + 32, 7, :], v[0:kw, kt, GH * g + j, :],
                                         probs[0:kw, u, j, :], kt == 0, cross or kt == NT - 1)
                        elif kind == "OT":
                            g, n = step[1:]
                            a = 2 * (pairs % 2)
                            pairs += 1
                            _, act_was, dve_was = take((tag,) + step, dve=(tag, "tok", g, n), banks=(a, a + 1))
                            pe.wait_ge(act_done, upto(act_done, (tag, "O", g, n), *act_was))
                            pe.wait_ge(dve_done, upto(dve_done, *dve_was))
                            for i in range(TPH):
                                o = n * HALF + i * P
                                ins = pe.transpose(ps[:, a, i * P:(i + 1) * P], ow[:, o:o + P], ident[:])
                        elif kind == "aT":
                            n, c = step[1:]
                            a = 2 * (pairs % 2)
                            pairs += 1
                            _, act_was, dve_was = take((tag,) + step, act=(tag,) + step, banks=(a, a + 1))
                            pe.wait_ge(act_done, upto(act_done, *act_was))
                            pe.wait_ge(dve_done, upto(dve_done, *((tag, "tok", g, n) for g in range(GROUPS)), *dve_was))
                            for i in range(TPH):
                                ins = pe.transpose(ps[:, a, i * P:(i + 1) * P], tok[:, TPH * n + i, c * P:(c + 1) * P], ident[:])
                        elif kind == "o":
                            t2 = step[1]
                            a = 2 * (pairs % 2)
                            pairs += 1
                            _, act_was, dve_was = take((tag,) + step, dve=(tag, "x", t2), banks=(a, a + 1))
                            pe.wait_ge(act_done, upto(act_done, *((tag, "aT", t2 // 2, c) for c in range(KC)), *act_was))
                            pe.wait_ge(dve_done, upto(dve_done, *dve_was))
                            for i in range(2):
                                t = 2 * t2 + i
                                for k in range(KC):
                                    ins = mm(ps[:, a, i * D:(i + 1) * D], hT[:, k, t * P:(t + 1) * P], wo[:, k, :], k == 0, k == KC - 1)
                        if kind != "O":
                            ins.then_inc(mm_done, M.add(mm_done, (tag,) + step))

                def mlp(tag, ln):
                    def up(n, m):
                        b, act_was, dve_was = take((tag, "h", n, m), act=(tag, "h", n, m))
                        pe.wait_ge(act_done, upto(act_done, *((ln, "hT", n, c) for c in range(KC)), *act_was))
                        pe.wait_ge(dve_done, upto(dve_done, *dve_was))
                        for k in range(KC):
                            ins = mm(ps[:, b, :], W1[:, k, m * P:(m + 1) * P], hT[:, k, n * HALF:(n + 1) * HALF], k == 0, k == KC - 1)
                        ins.then_inc(mm_done, M.add(mm_done, (tag, "h", n, m)))

                    def down(t2):
                        b, act_was, dve_was = take((tag, "o", t2), dve=(tag, "x", t2))
                        pe.wait_ge(act_done, upto(act_done, (tag, "h", t2 // 2, FM - 1), *act_was))
                        pe.wait_ge(dve_done, upto(dve_done, *dve_was))
                        for i in range(2):
                            o = ((2 * t2 + i) % TPH) * P
                            for m in range(FM):
                                ins = mm(ps[:, b, i * D:(i + 1) * D], hid[:, t2 // 2, m, o:o + P], W2[:, m, :], m == 0, m == FM - 1)
                        ins.then_inc(mm_done, M.add(mm_done, (tag, "o", t2)))

                    pe.wait_ge(slot_loaded[2], upto(slot_loaded[2], tag))
                    for m in range(FM):
                        up(0, m)
                    up(1, 0)
                    up(1, 1)
                    pe.wait_ge(slot_loaded[3], upto(slot_loaded[3], tag))
                    down(0)
                    down(1)
                    for m in range(2, FM):
                        up(1, m)
                    down(2)
                    down(3)

                tp = [tpw[:, :, i * D:(i + 1) * D] for i in range(3)]
                turn(upto, "ln1")
                pe.wait_ge(slot_loaded[4], upto(slot_loaded[4], "L1"))
                row("L1sa", silu_cond(tp[0]) + [pick("tp_b0"), pick("sa_bo")], ("row", "L1sa"))
                attend("L1sa")
                row("L1ca", silu_cond(tp[1]) + [pick("tp_b1"), pick("ca_bo")], ("row", "L1ca"))
                turn(upto, "ln3")
                attend("L1ca")
                row("L1mlp", silu_cond(tp[2]) + [pick("tp_b2"), pick("b2")], ("row", "L1mlp"))
                turn(upto, "ln2")
                mlp("L1mlp", "ln2")
                b, act_was, dve_was = take("mod", dve="mod")
                pe.wait_ge(act_done, upto(act_done, "scond", *act_was))
                pe.wait_ge(dve_done, upto(dve_done, *dve_was))
                pe.wait_ge(slot_loaded[4], upto(slot_loaded[4], "L2"))
                for m in (0, 1, 2, 3, 6, 7, 8, 9):
                    for k in range(KC):
                        ins = mm(ps[:, b, m:m + 1], adw[:, k, m * P:(m + 1) * P], scond[:, k:k + 1], k == 0, k == KC - 1)
                ins.then_inc(mm_done, M.add(mm_done, "mod"))
                row("L2sa_g", silu_cond(adw[:, :, 2 * D:3 * D]) + [pick("g_sa")], ("grow", "L2sa"))
                row("L2sa", [pick("sa_proj_b")], ("row", "L2sa"))
                turn(upto, "ln4")
                attend("L2sa")
                row("L2ca", [pick("ca_proj_b")], ("row", "L2ca"))
                turn(upto, "ln5")
                attend("L2ca")
                row("L2mlp_g", silu_cond(adw[:, :, 5 * D:6 * D]) + [pick("g_ff")], ("grow", "L2mlp"))
                row("L2mlp", [pick("fc2_b")], ("row", "L2mlp"))
                turn(upto, "ln6")
                mlp("L2mlp", "ln6")
                b, act_was, dve_was = take("mod3", dve="mod3")
                pe.wait_ge(act_done, upto(act_done, *act_was))
                pe.wait_ge(dve_done, upto(dve_done, *dve_was))
                pe.wait_ge(slot_loaded[1], upto(slot_loaded[1], "L3ss"))
                for i in range(2):
                    for m in range(4):
                        for k in range(KC):
                            ins = mm(ps[:, b, 4 * i + m:4 * i + m + 1], w256(1, 2 * i, 512)[:, k, m * P:(m + 1) * P],
                                     scond[:, k:k + 1], k == 0, k == KC - 1)
                ins.then_inc(mm_done, M.add(mm_done, "mod3"))
                b, act_was, dve_was = take("cT", act="kvT")
                pe.wait_ge(act_done, upto(act_done, *act_was))
                pe.wait_ge(dve_done, upto(dve_done, "ctxn", *dve_was))
                for c in range(KC):
                    ins = pe.transpose(ps[:, b, c * S:(c + 1) * S], ctxk[:, c * P:(c + 1) * P], ident[0:S, 0:S])
                ins.then_inc(mm_done, M.add(mm_done, "cT"))
                row("L3ca", [pick("bp")], ("row", "L3ca"))
                turn(upto, "ln7")
                attend("L3ca")
            M.close("blocks")

        @block.scalar
        def _(act):
            def load_tokens(it):
                act.dma_start(xin[:], T["x"][it].rearrange("(t p) d -> p t d", p=P)).then_inc(xin_loaded, M.add(xin_loaded, None, LOADED))

            def load_conditions(it, loop):
                act.dma_start(ctxT[:], T["ctxT"][it].rearrange("(c p) s -> p c s", p=P)
                              ).then_inc(conditions_loaded, M.add(conditions_loaded, None, LOADED))
                act.dma_start(cond[:], T["condT"][it]).then_inc(conditions_loaded, M.add(conditions_loaded, loop, LOADED))

            def affine(upto, tag, gain, shift):
                for n in range(NH):
                    for c in range(KC):
                        act.wait_ge(mm_done, upto(mm_done, (tag, "T", n, c)))
                        src, dst = ps[:, M.where((tag, "T", n, c)), :], hT[:, c, n * HALF:(n + 1) * HALF]
                        if gain is None:
                            ins = act.activation(dst, src, ACT.Copy)
                        else:
                            ins = act.activation(dst, src, ACT.Identity, bias=shift(c), scale=gain(c))
                        ins.then_inc(act_done, M.add(act_done, (tag, "hT", n, c)))

            act.wait_ge(constants_loaded, 6 * LOADED)
            load_tokens(0)
            load_conditions(0, "first")
            act.activation(small[:, 127:128], cols[:, 0:1], ACT.Copy).then_inc(act_done, M.add(act_done))
            M.open("experts")
            with act.Fori(0, B) as it:
                def upto(sem, *steps):
                    return M.upto("experts", it, sem, steps)

                act.dma_start(x[:], T["x"][it].rearrange("(t p) d -> p t d", p=P)).then_inc(residual_loaded, M.add(residual_loaded, "x", LOADED))
                act.wait_ge(mm_done, upto(mm_done, ("L0", "kv")))
                b = M.where(("L0", "kv"))
                act.activation(kv0T[:], ps[:, b, 0:2 * KC * SP_].rearrange("p (c s) -> p c s", s=SP_), ACT.Copy
                               ).then_inc(act_done, M.add(act_done, ("L0", "kv")))
                act.wait_ge(mm_done, upto(mm_done, ("L0", "a")))
                b = M.where(("L0", "a"))
                act.activation(a0[:, :, 0:SP_], ps[:, b, 0:KC * SP_].rearrange("p (c s) -> p c s", s=SP_), ACT.Copy, scale=D ** -0.5
                               ).then_inc(act_done, M.add(act_done, ("L0", "a")))
                affine(upto, "ln0", lambda c: col("L0_ln_gamma", c), lambda c: col("L0_ln_beta", c))
                for n in range(NH):
                    b = M.where(("L0", "s", n))
                    act.wait_ge(dve_done, upto(dve_done, ("L0", "nmx", n)))
                    for i in range(TPH):
                        t = TPH * n + i
                        act.activation(e01[n][:, i, 0:S], ps[:, b, i * SW:i * SW + S], ACT.Exp, bias=nmx[:, t:t + 1],
                                       accum_out=es[:, t:t + 1]).then_inc(act_done, M.add(act_done, ("L0", "e", n, i)))
                for n in range(NH):
                    act.wait_ge(mm_done, upto(mm_done, ("L0", "wT", n)))
                    act.activation(wT[0:S, n * HALF:(n + 1) * HALF], ps[0:S, M.where(("L0", "wT", n)), :], ACT.Copy
                                   ).then_inc(act_done, M.add(act_done, ("L0", "wT", n)))
                act.wait_ge(dve_done, upto(dve_done, ("L0", "lg", NH - 1)))
                act.activation(lg[:], lg[:], ACT.Exp).then_inc(act_done, M.add(act_done, ("L0", "le")))
                for n in range(NH):
                    half = slice(n * HALF, (n + 1) * HALF)
                    for m in range(RM + GM):
                        act.wait_ge(mm_done, upto(mm_done, ("L0", "h", n, m)))
                        act.activation(hid0[:, m, :], ps[:, M.where(("L0", "h", n, m)), :], ACT.Silu, bias=col("L0_e_b1", m)
                                       ).then_inc(act_done, M.add(act_done, ("L0", "h", n, m)))
                        if m // 4 == 2 and m % 4 < E:
                            e = m % 4
                            act.wait_ge(mm_done, upto(mm_done, ("L0", "pb", n, e)))
                            if n:
                                act.wait_ge(dve_done, upto(dve_done, ("L0", "hp", n - 1, RM - 1)))
                            act.activation(pb[:, e, :], ps[:, M.where(("L0", "pb", n, e)), :], ACT.Copy
                                           ).then_inc(act_done, M.add(act_done, ("L0", "pb", n, e)))
                    act.wait_ge(mm_done, upto(mm_done, ("L0", "pT", n)))
                    act.activation(pT[:, half], ps[0:E, M.where(("L0", "pT", n)), :], ACT.Copy
                                   ).then_inc(act_done, M.add(act_done, ("L0", "pT", n)))
                    for i2 in range(2):
                        t2 = 2 * n + i2
                        act.wait_ge(mm_done, upto(mm_done, ("L0", "g", t2)))
                        if n:
                            act.wait_ge(dve_done, upto(dve_done, ("L0", "x", t2 - 2)))
                        act.activation(sg[:, i2], ps[:, M.where(("L0", "g", t2)), :].rearrange("p (i d) -> p i d", i=2),
                                       ACT.Tanh, scale=0.5).then_inc(act_done, M.add(act_done, ("L0", "g", t2)))
                    if n == 0:
                        act.wait_ge(dve_done, upto(dve_done, ("ln0", "xh", NT - 1)))
                        load_tokens(it + 1)
                        load_conditions(it + 1, "experts")
                    for c in range(KC):
                        act.wait_ge(mm_done, upto(mm_done, ("L0", "rt", n, c)))
                        act.activation(rT[:, c, :], ps[:, M.where(("L0", "rt", n, c)), :], ACT.Copy
                                       ).then_inc(act_done, M.add(act_done, ("L0", "rt", n, c)))
                for t2 in range(4):
                    act.wait_ge(dve_done, upto(dve_done, ("L0", "x", t2)))
                    act.dma_start(T["x0"][it].rearrange("(t p) d -> p t d", p=P)[:, 2 * t2:2 * t2 + 2, :],
                                  x[:, 2 * t2:2 * t2 + 2, :]).then_inc(x_stored, M.add(x_stored, t2, LOADED))
                act.wait_ge(x_stored, upto(x_stored, 3))
            M.close("experts")

            act.dma_start(T["x0"][B].rearrange("(t p) d -> p t d", p=P), x[:]).then_inc(x_stored, M.add(x_stored, None, LOADED))
            act.wait_ge(x_stored, (4 * B + 1) * LOADED)
            for t2 in range(4):
                act.dma_start(x[:, 2 * t2:2 * t2 + 2, :], T["x0"][0].rearrange("(t p) d -> p t d", p=P)[:, 2 * t2:2 * t2 + 2, :]
                              ).then_inc(x_loaded[t2], M.add(x_loaded[t2], "first", LOADED))
            M.open("blocks")
            with act.Fori(0, B) as it:
                def upto(sem, *steps):
                    return M.upto("blocks", it, sem, steps)

                def attend(tag):
                    cross = ATT[tag][0]
                    bq, bk, bv = ATT[tag][5:]
                    kw = S if cross else P
                    unit, projected = {}, []
                    for step in (CROSS if cross else SELF):
                        kind, name = step[0], (tag,) + step
                        if kind == "P":
                            which, c, n = step[1:]
                            hi, bias, kn = (qh, bq, HALF) if which == "q" else (kh, bk, SP_ if cross else HALF)
                            act.wait_ge(mm_done, upto(mm_done, name))
                            act.activation(hi[:, c, n * HALF:n * HALF + kn], ps[:, M.where(name), 0:kn], ACT.Identity, bias=col(bias[0], bias[1] + c))
                            if len(projected) >= 4:
                                act.wait_ge(pool_done, upto(pool_done, projected[-4]))
                            act.activation(whole[:, len(projected) % 4, 0:kn], ps[:, M.where(name), 0:kn], ACT.Identity,
                                           bias=col(bias[0], bias[1] + c)).then_inc(act_done, M.add(act_done, name))
                            projected.append(name)
                        elif kind == "V":
                            t2, i = step[1], 1 if cross else 2
                            src = ps[0:kw, M.where(name), 0:i * D].rearrange("p (i h d) -> p i h d", i=i, d=HD)
                            act.wait_ge(mm_done, upto(mm_done, name))
                            act.activation(v[0:kw, 2 * t2:2 * t2 + i, :, 0:HD], src, ACT.Copy).then_inc(act_done, M.add(act_done, name))
                        elif kind == "K" and step[1] == "act":
                            which, pair, n = step[2:]
                            act.wait_ge(mm_done, upto(mm_done, name))
                            if which == "q":
                                act.activation(qs[:, pair, n * HALF:(n + 1) * HALF], ps[:, M.where(name), :], ACT.Identity,
                                               bias=qs_rows).then_inc(act_done, M.add(act_done, name))
                            else:
                                act.activation(ks[:, pair, n * HALF:(n + 1) * HALF], ps[:, M.where(name), :], ACT.Identity,
                                               bias=ks_rows).then_inc(act_done, M.add(act_done, name))
                        elif kind == "M":
                            g, n = step[1:]
                            z, w, _, _ = maxima_of(tag, g, n)
                            act.wait_ge(mm_done, upto(mm_done, name))
                            if not cross and NH * g + n >= 2:
                                act.wait_ge(maxima_stacked[g - 1][n], upto(maxima_stacked[g - 1][n], (tag, GH - 1)))
                            act.activation(mrow[0:w, z * HALF:(z + 1) * HALF], ps[0:w, M.where(name), :], ACT.Copy
                                           ).then_inc(act_done, M.add(act_done, name))
                        elif kind == "S":
                            g, n, kt, j = step[1:]
                            u = unit.setdefault((g, n, kt), len(unit))
                            act.wait_ge(mm_done, upto(mm_done, name, *[(tag, "PV") + k for k in list(unit)[u - 4:u - 3] if u >= 4]))
                            src, dst = ps[0:kw, M.where(name), :], probs[0:kw, u % 4, j, :]
                            if tag == "L1ca":
                                if (u, j) == (0, 0):
                                    act.wait_ge(dve_done, upto(dve_done, "mcolb"))
                                ins = act.activation(dst, src, ACT.Exp, bias=mcolb[:], scale=SCALE)
                            else:
                                ins = act.activation(dst, src, ACT.Exp, scale=SCALE)
                            ins.then_inc(act_done, M.add(act_done, name))
                        elif kind == "O":
                            g, n = step[1:]
                            act.wait_ge(mm_done, upto(mm_done, (tag, "PV", g, n, 0 if cross else NT - 1), *[(tag, "OT", g - 1, n)] * (g > 0)))
                            act.activation(ow[:, n * HALF:(n + 1) * HALF], ps[:, 7, :], ACT.Copy).then_inc(act_done, M.add(act_done, name))
                        elif kind == "aT":
                            n, c = step[1:]
                            act.wait_ge(mm_done, upto(mm_done, name))
                            act.activation(hT[:, c, n * HALF:(n + 1) * HALF], ps[:, M.where(name), :], ACT.Identity,
                                           bias=col(bv[0], bv[1] + c)).then_inc(act_done, M.add(act_done, name))

                def mlp(tag, func, bias):
                    for n in range(NH):
                        for m in range(FM):
                            act.wait_ge(mm_done, upto(mm_done, (tag, "h", n, m)))
                            act.activation(hid[:, n, m, :], ps[:, M.where((tag, "h", n, m)), :], func, bias=col(bias, m)
                                           ).then_inc(act_done, M.add(act_done, (tag, "h", n, m)))

                load_conditions(it, "blocks")
                act.dma_start(mi[:], T["mask"][it]).then_inc(conditions_loaded, M.add(conditions_loaded, None, LOADED))
                act.dma_start(mic[:], T["maskT"][it]).then_inc(conditions_loaded, M.add(conditions_loaded, None, LOADED))
                act.dma_start(ctxk[:], T["ctx"][it]).then_inc(conditions_loaded, M.add(conditions_loaded, "all", LOADED))
                act.wait_ge(conditions_loaded, upto(conditions_loaded, "all"))
                act.activation(scond[:], cond[:], ACT.Silu).then_inc(act_done, M.add(act_done, "scond"))
                affine(upto, "ln1", lambda c: col("L1_ln1_g", c), lambda c: col("L1_ln1_b", c))
                attend("L1sa")
                affine(upto, "ln3", lambda c: col("L1_ln3_g", c), lambda c: col("L1_ln3_b", c))
                attend("L1ca")
                affine(upto, "ln2", lambda c: col("L1_ln2_g", c), lambda c: col("L1_ln2_b", c))
                mlp("L1mlp", ACT.Gelu, "L1_b1")
                act.wait_ge(dve_done, upto(dve_done, "mod"))
                affine(upto, "ln4", lambda c: mod[:, 2 + c:3 + c], lambda c: mod[:, c:c + 1])
                attend("L2sa")
                affine(upto, "ln5", None, None)
                attend("L2ca")
                affine(upto, "ln6", lambda c: mod[:, 8 + c:9 + c], lambda c: mod[:, 6 + c:7 + c])
                mlp("L2mlp", ACT.Gelu_apprx_tanh, "L2_fc1_b")
                act.wait_ge(mm_done, upto(mm_done, "cT"))
                act.wait_ge(dve_done, upto(dve_done, "mod3"))
                b = M.where("cT")
                for c in range(KC):
                    act.activation(kvT[:, c, 0:S], ps[:, b, c * S:(c + 1) * S], ACT.Identity, bias=mod3[:, 6 + c:7 + c],
                                   scale=mod3[:, 4 + c:5 + c]).then_inc(act_done, M.add(act_done, ("kvT", c)))
                    act.activation(kvT[:, c, S:SP_], ps[:, b, (c + 1) * S - 1:(c + 1) * S], ACT.Identity, bias=mod3[:, 6 + c:7 + c],
                                   scale=mod3[:, 4 + c:5 + c]).then_inc(act_done, M.add(act_done, "kvT" if c == KC - 1 else ("kvT2", c)))
                affine(upto, "ln7", lambda c: mod3[:, c:c + 1], lambda c: mod3[:, 2 + c:3 + c])
                attend("L3ca")
                for t2 in range(4):
                    act.wait_ge(dve_done, upto(dve_done, ("L3ca", "x", t2)))
                    act.dma_start(T["out"][it].rearrange("(t p) d -> p t d", p=P)[:, 2 * t2:2 * t2 + 2, :],
                                  x[:, 2 * t2:2 * t2 + 2, :]).then_inc(out_stored[t2], M.add(out_stored[t2], "out", LOADED))
                for t2 in range(4):
                    act.wait_ge(out_stored[t2], upto(out_stored[t2], "out"))
                    act.dma_start(x[:, 2 * t2:2 * t2 + 2, :], T["x0"][it + 1].rearrange("(t p) d -> p t d", p=P)[:, 2 * t2:2 * t2 + 2, :]
                                  ).then_inc(x_loaded[t2], M.add(x_loaded[t2], None, LOADED))
            M.close("blocks")
            for t2 in range(4):
                act.wait_ge(x_loaded[t2], (B + 1) * LOADED)

        @block.vector
        def _(dve):
            def stats(upto, tag, t, src):
                dve.bn_stats(st[:, t, :], src[:, t, :]).then_inc(dve_done, M.add(dve_done, (tag, "st", t)))

            def spread(upto, tag, h, eps):
                tt = slice(TPH * h, TPH * h + TPH)
                dve.wait_ge(dve_done, upto(dve_done, (tag, "st", TPH * h + TPH - 1)))
                dve.memset(ve[:, tt], 0.0)
                for t in range(TPH * h, TPH * h + TPH):
                    dve.bn_aggr(mv[:, t, :], st[:, t, :]).then_inc(dve_done, M.add(dve_done, (tag, "ag", t)))
                dve.wait_ge(dve_done, upto(dve_done, (tag, "ag", TPH * h + TPH - 1)))
                dve.tensor_scalar(ve[:, tt], mv[:, tt, 1], eps, None, ALU.add).then_inc(dve_done, M.add(dve_done, (tag, "ve", h)))

            def normalise(upto, tag, h, src):
                dve.wait_ge(pool_done, upto(pool_done, (tag, "rstd", h)))
                for t in range(TPH * h, TPH * h + TPH):
                    dve.tensor_scalar(tok[:, t, :], src[:, t, :], mv[:, t, 0:1], rstd[:, t:t + 1], ALU.subtract, ALU.mult
                                      ).then_inc(dve_done, M.add(dve_done, (tag, "xh", t)))

            dve.memset(nhalf, -0.5)
            dve.memset(v[:], 1.0)
            dve.wait_ge(constants_loaded, 6 * LOADED)
            dve.tensor_copy(a0[:, :, SP_:], router[:, 0:KC, :])
            dve.tensor_copy(sel[:], sel_in[:]).then_inc(dve_done, M.add(dve_done))
            dve.wait_ge(dve_done, 1)
            M.open("experts")
            with dve.Fori(0, B) as it:
                def upto(sem, *steps):
                    return M.upto("experts", it, sem, steps)

                dve.wait_ge(xin_loaded, upto(xin_loaded))
                for h in range(NH):
                    for t in range(TPH * h, TPH * h + TPH):
                        stats(upto, "ln0", t, xin)
                    spread(upto, "ln0", h, 1e-5)
                for h in range(NH):
                    normalise(upto, "ln0", h, xin)
                for e in range(E + 1):
                    w = RH if e < E else D + E
                    dve.wait_ge(mm_done, upto(mm_done, ("L0", "u", e)))
                    dve.tensor_copy(u0[0:S, e * RH:e * RH + w], ps[0:S, M.where(("L0", "u", e)), 0:w]
                                    ).then_inc(dve_done, M.add(dve_done, ("L0", "u", e)))
                for n in range(NH):
                    tt = slice(TPH * n, TPH * n + TPH)
                    both = ps[:, M.where(("L0", "s", n)), 0:TPH * SW].rearrange("p (t s) -> p t s", s=SW)
                    dve.wait_ge(mm_done, upto(mm_done, ("L0", "s", n)))
                    dve.tensor_copy(lg[:, tt], both[:, :, SP_:]).then_inc(dve_done, M.add(dve_done, ("L0", "lt0", n)))
                    dve.tensor_reduce(nmx[:, tt], both[:, :, 0:S], AX.X, ALU.max, negate=True).then_inc(dve_done, M.add(dve_done, ("L0", "nmx", n)))
                for n in range(NH):
                    tt = slice(TPH * n, TPH * n + TPH)
                    dve.wait_ge(act_done, upto(act_done, ("L0", "e", n, TPH - 1)))
                    dve.reciprocal(rc4[:, tt], es[:, tt]).then_inc(dve_done, M.add(dve_done, ("L0", "rc4", n)))
                    dve.wait_ge(dve_done, upto(dve_done, ("L0", "rc4", n)))
                    dve.tensor_tensor(e01[n][:, :, 0:S], e01[n][:, :, 0:S], rc4[:, tt].unsqueeze(2).to_broadcast([P, TPH, S]), ALU.mult
                                      ).then_inc(dve_done, M.add(dve_done, ("L0", "w", n)))
                for n in range(NH):
                    tt = slice(TPH * n, TPH * n + TPH)
                    src = ps[:, M.where(("L0", "r", n)), 0:TPH * E].rearrange("p (t e) -> p t e", e=E)
                    dve.wait_ge(mm_done, upto(mm_done, ("L0", "r", n)))
                    dve.tensor_tensor(lg[:, tt], lg[:, tt], src, ALU.add).then_inc(dve_done, M.add(dve_done, ("L0", "lt", n)))
                    dve.wait_ge(dve_done, upto(dve_done, ("L0", "lt", n)))
                    dve.tensor_reduce(rmx[:, tt], lg[:, tt], AX.X, ALU.max, negate=True).then_inc(dve_done, M.add(dve_done, ("L0", "rmx", n)))
                    dve.wait_ge(dve_done, upto(dve_done, ("L0", "rmx", n)))
                    dve.tensor_tensor(lg[:, tt], lg[:, tt], rmx[:, tt].unsqueeze(2).to_broadcast([P, TPH, E]), ALU.add
                                      ).then_inc(dve_done, M.add(dve_done, ("L0", "lg", n)))
                dve.wait_ge(act_done, upto(act_done, ("L0", "le")))
                dve.tensor_reduce(rs[:], lg[:], AX.X, ALU.add).then_inc(dve_done, M.add(dve_done, ("L0", "rs")))
                dve.wait_ge(dve_done, upto(dve_done, ("L0", "rs")))
                dve.reciprocal(rrs[:], rs[:]).then_inc(dve_done, M.add(dve_done, ("L0", "rrs")))
                dve.wait_ge(dve_done, upto(dve_done, ("L0", "rrs")))
                dve.tensor_tensor(lg[:], lg[:], rrs[:].unsqueeze(2).to_broadcast([P, NT, E]), ALU.mult
                                  ).then_inc(dve_done, M.add(dve_done, ("L0", "p")))
                for n in range(NH):
                    for m in range(RM):
                        dve.wait_ge(act_done, upto(act_done, ("L0", "pb", n, m // 4), ("L0", "h", n, m)))
                        dve.tensor_tensor(hid0[:, m, :], hid0[:, m, :], pb[:, m // 4, :], ALU.mult
                                          ).then_inc(dve_done, M.add(dve_done, ("L0", "hp", n, m)))
                    for i2 in range(2):
                        t2 = 2 * n + i2
                        xx = x[:, 2 * t2:2 * t2 + 2, :]
                        o = ps[:, M.where(("L0", "o", t2)), :].rearrange("p (i d) -> p i d", i=2)
                        dve.wait_ge(mm_done, upto(mm_done, ("L0", "o", t2)))
                        dve.wait_ge(act_done, upto(act_done, ("L0", "g", t2)))
                        dve.scalar_tensor_tensor(sg[:, i2], sg[:, i2], 1.0, o, ALU.add, ALU.mult
                                                 ).then_inc(dve_done, M.add(dve_done, ("L0", "sg", t2)))
                        dve.wait_ge(dve_done, upto(dve_done, ("L0", "sg", t2)))
                        if t2 == 0:
                            dve.wait_ge(residual_loaded, upto(residual_loaded, "x"))
                        dve.scalar_tensor_tensor(xx, sg[:, i2], 0.5, xx, ALU.mult, ALU.add
                                                 ).then_inc(dve_done, M.add(dve_done, ("L0", "x", t2)))
            M.close("experts")

            M.open("blocks")
            with dve.Fori(0, B) as it:
                def upto(sem, *steps):
                    return M.upto("blocks", it, sem, steps)

                def take_row(tag):
                    dve.wait_ge(mm_done, upto(mm_done, ("row", tag)))
                    dve.tensor_copy(rrow[:], ps[:, M.where(("row", tag)), 0:D]).then_inc(dve_done, M.add(dve_done, ("row", tag)))

                def take_gated_row(tag):
                    dve.wait_ge(mm_done, upto(mm_done, ("row", tag + "_g")))
                    dve.tensor_copy(grow[:], ps[:, M.where(("row", tag + "_g")), 0:D]).then_inc(dve_done, M.add(dve_done, ("grow", tag)))
                    dve.wait_ge(mm_done, upto(mm_done, ("row", tag)))
                    dve.wait_ge(dve_done, upto(dve_done, ("grow", tag)))
                    dve.tensor_tensor(rrow[:], grow[:], ps[:, M.where(("row", tag)), 0:D], ALU.mult
                                      ).then_inc(dve_done, M.add(dve_done, ("row", tag)))

                def residual(tag, t2, gated, ln=None, eps=None):
                    if ln and t2 == 2:
                        normalise(upto, ln, 0, x)
                    src = ps[:, M.where((tag, "o", t2)), :].rearrange("p (i d) -> p i d", i=2)
                    xx = x[:, 2 * t2:2 * t2 + 2, :]
                    dve.wait_ge(mm_done, upto(mm_done, (tag, "o", t2)))
                    if gated:
                        tmp = tok[:, 2 * t2:2 * t2 + 2, :]
                        dve.tensor_tensor(tmp, src, grow[:].unsqueeze(1).to_broadcast([P, 2, D]), ALU.mult
                                          ).then_inc(dve_done, M.add(dve_done, (tag, "gx", t2)))
                        dve.wait_ge(dve_done, upto(dve_done, (tag, "gx", t2)))
                        src = tmp
                    dve.wait_ge(pool_done, upto(pool_done, ("row", tag)))
                    dve.tensor_tensor(xx, xx, src, ALU.add).then_inc(dve_done, M.add(dve_done, (tag, "x", t2)))
                    if ln:
                        dve.wait_ge(dve_done, upto(dve_done, (tag, "x", t2)))
                        stats(upto, ln, 2 * t2, x)
                        stats(upto, ln, 2 * t2 + 1, x)
                        if t2 % 2:
                            spread(upto, ln, t2 // 2, eps)
                        if t2 == 3:
                            normalise(upto, ln, 1, x)

                def attend(tag, gated=False, ln=None, eps=None):
                    cross = ATT[tag][0]
                    if cross:
                        dve.wait_ge(dve_done, upto(dve_done, (LN_OF[tag], "xh", NT - 1)))
                        dve.memset(kz[:].bitcast(F32), 0.0).then_inc(dve_done, M.add(dve_done, (tag, "zero")))
                        dve.wait_ge(dve_done, upto(dve_done, (tag, "zero")))
                    turned = []
                    for step in (CROSS if cross else SELF):
                        kind, name = step[0], (tag,) + step
                        if kind == "o":
                            residual(tag, step[1], gated, ln, eps)
                        elif kind == "K" and step[1] == "dve":
                            pair, n = step[3:]
                            dve.wait_ge(mm_done, upto(mm_done, name))
                            if cross:
                                for e in range(2):
                                    r = stacked(e, 0, STACK)
                                    ins = dve.tensor_scalar(kz[r, pair, e, :], ps[r, M.where(name), 0:SP_], ks_rows[r], None, ALU.add)
                                ins.then_inc(dve_done, M.add(dve_done, name))
                            else:
                                dve.tensor_scalar(ks[:, pair, n * HALF:(n + 1) * HALF], ps[:, M.where(name), :], ks_rows, None, ALU.add
                                                  ).then_inc(dve_done, M.add(dve_done, name))
                        elif kind == "A":
                            g, n, t, j = step[1:]
                            z, w, j0, turn_step = maxima_of(tag, g, n)
                            a = M.where(name)
                            if not cross and NH * g + n >= 2:
                                dve.wait_ge(mm_done, upto(mm_done, name, (tag, "M", g - 1, n)))
                            else:
                                dve.wait_ge(mm_done, upto(mm_done, name))
                            if cross:
                                dve.tensor_reduce(mx[:, z, t, j0:j0 + GH], ps[:, a, 0:GH * SP_].rearrange("p (j s) -> p j s", s=SP_), AX.X, ALU.max,
                                                  negate=True).then_inc(dve_done, M.add(dve_done, name))
                            else:
                                dve.tensor_reduce(mx[:, z, t, j:j + 1], ps[:, a:a + 2, :], AX.XY, ALU.max, negate=True
                                                  ).then_inc(dve_done, M.add(dve_done, name))
                        elif kind == "OT":
                            g, n = step[1:]
                            o = ps[:, M.where(name), :].rearrange("p (t j d) -> p t j d", t=TPH, j=GH)
                            rcv = rc[:].rearrange("p (t j) -> p t j", j=GH)
                            dst = tok[:, TPH * n:TPH * n + TPH, GH * HD * g:GH * HD * (g + 1)].rearrange("p t (j d) -> p t j d", d=HD)
                            dve.wait_ge(mm_done, upto(mm_done, name))
                            if turned:
                                dve.wait_ge(dve_done, upto(dve_done, (tag, "tok") + turned[-1]))
                            dve.reciprocal(rcv, o[:, :, :, HD]).then_inc(dve_done, M.add(dve_done, (tag, "rc", g, n)))
                            dve.wait_ge(dve_done, upto(dve_done, (tag, "rc", g, n)))
                            dve.tensor_tensor(dst, o[:, :, :, 0:HD], rcv.unsqueeze(3).to_broadcast([P, TPH, GH, HD]), ALU.mult
                                              ).then_inc(dve_done, M.add(dve_done, (tag, "tok", g, n)))
                            turned.append((g, n))

                for h in range(NH):
                    for t in range(TPH * h, TPH * h + TPH):
                        if t % 2 == 0:
                            dve.wait_ge(x_loaded[t // 2], upto(x_loaded[t // 2], "first"))
                        stats(upto, "ln1", t, x)
                    spread(upto, "ln1", h, 1e-5)
                for h in range(NH):
                    normalise(upto, "ln1", h, x)
                dve.wait_ge(conditions_loaded, upto(conditions_loaded, "all"))
                dve.tensor_scalar(mrowb[:], mi[:], 0.0, MASKED, ALU.is_equal, ALU.mult).then_inc(dve_done, M.add(dve_done, "mrowb"))
                dve.tensor_scalar(mcolb[:], mic[:], 0.0, MASKED, ALU.is_equal, ALU.mult).then_inc(dve_done, M.add(dve_done, "mcolb"))
                take_row("L1sa")
                attend("L1sa", False, "ln3", 1e-5)
                take_row("L1ca")
                attend("L1ca", False, "ln2", 1e-5)
                take_row("L1mlp")
                for t2 in range(4):
                    residual("L1mlp", t2, False, "ln4", 1e-6)
                dve.wait_ge(mm_done, upto(mm_done, "mod"))
                b = M.where("mod")
                ab = COL["L2_adaln_b"]
                for i in (0, 6):
                    dve.tensor_tensor(mod[:, i:i + 2], ps[:, b, i:i + 2], cols[:, ab + i:ab + i + 2], ALU.add
                                      ).then_inc(dve_done, M.add(dve_done, ("shift", i)))
                    dve.scalar_tensor_tensor(mod[:, i + 2:i + 4], ps[:, b, i + 2:i + 4], 1.0, cols[:, ab + i + 2:ab + i + 4], ALU.add, ALU.add
                                             ).then_inc(dve_done, M.add(dve_done, "mod" if i else ("scale", i)))
                take_gated_row("L2sa")
                attend("L2sa", True, "ln5", 1e-6)
                take_row("L2ca")
                attend("L2ca", False, "ln6", 1e-6)
                take_gated_row("L2mlp")
                dve.bn_stats(stc[:], ctxk[:]).then_inc(dve_done, M.add(dve_done, "stc"))
                dve.wait_ge(dve_done, upto(dve_done, "stc"))
                dve.memset(vec[:], 0.0)
                dve.bn_aggr(mvc[:], stc[:]).then_inc(dve_done, M.add(dve_done, "agc"))
                dve.wait_ge(dve_done, upto(dve_done, "agc"))
                dve.tensor_scalar(vec[:], mvc[:, 1:2], 1e-5, None, ALU.add).then_inc(dve_done, M.add(dve_done, "vec"))
                dve.wait_ge(pool_done, upto(pool_done, "rstdc"))
                dve.tensor_scalar(ctxk[:], ctxk[:], mvc[:, 0:1], rstdc[:], ALU.subtract, ALU.mult).then_inc(dve_done, M.add(dve_done, "ctxn"))
                for t2 in range(4):
                    residual("L2mlp", t2, True, "ln7", 1e-5)
                dve.wait_ge(mm_done, upto(mm_done, "mod3"))
                b = M.where("mod3")
                for i, name in ((0, "L3_bss_q"), (4, "L3_bss_kv")):
                    cb = COL[name]
                    dve.scalar_tensor_tensor(mod3[:, i:i + 2], ps[:, b, i:i + 2], 1.0, cols[:, cb:cb + 2], ALU.add, ALU.add
                                             ).then_inc(dve_done, M.add(dve_done, ("scale3", i)))
                    dve.tensor_tensor(mod3[:, i + 2:i + 4], ps[:, b, i + 2:i + 4], cols[:, cb + 2:cb + 4], ALU.add
                                      ).then_inc(dve_done, M.add(dve_done, "mod3" if i else ("shift3", i)))
                take_row("L3ca")
                attend("L3ca")
            M.close("blocks")

        @block.gpsimd
        def _(pool):
            def rsqrt(upto, tag, h):
                tt = slice(TPH * h, TPH * h + TPH)
                pool.wait_ge(dve_done, upto(dve_done, (tag, "ve", h)))
                pool.tensor_tensor(rstd[:, tt], ve[:, tt], nhalf[:, tt], ALU.pow).then_inc(pool_done, M.add(pool_done, (tag, "rstd", h)))

            pool.wait_ge(dve_done, 1)
            M.open("experts")
            with pool.Fori(0, B) as it:
                def upto(sem, *steps):
                    return M.upto("experts", it, sem, steps)

                rsqrt(upto, "ln0", 0)
                rsqrt(upto, "ln0", 1)
            M.close("experts")
            M.open("blocks")
            with pool.Fori(0, B) as it:
                def upto(sem, *steps):
                    return M.upto("blocks", it, sem, steps)

                def add_row(tag, ln):
                    pool.wait_ge(dve_done, upto(dve_done, ("row", tag), (ln, "xh", NT - 1)))
                    pool.tensor_tensor(x[:], x[:], rrow[:].unsqueeze(1).to_broadcast([P, NT, D]), ALU.add
                                       ).then_inc(pool_done, M.add(pool_done, ("row", tag)))

                def split(tag):
                    cross, count = ATT[tag][0], 0
                    for step in (CROSS if cross else SELF):
                        if step[0] == "P":
                            which, c, n = step[1:]
                            hi, lo, kn = (qh, ql, HALF) if which == "q" else (kh, kl, SP_ if cross else HALF)
                            part = slice(n * HALF, n * HALF + kn)
                            pool.wait_ge(act_done, upto(act_done, (tag,) + step))
                            pool.tensor_tensor(lo[:, c, part], whole[:, count % 4, 0:kn], hi[:, c, part].bitcast(F32), ALU.subtract
                                               ).then_inc(pool_done, M.add(pool_done, (tag,) + step))
                            count += 1

                for ln, tag in (("ln1", "L1sa"), ("ln3", "L1ca"), ("ln2", "L1mlp"), ("ln4", "L2sa"), ("ln5", "L2ca"), ("ln6", "L2mlp")):
                    rsqrt(upto, ln, 0)
                    rsqrt(upto, ln, 1)
                    if tag in ATT:
                        split(tag)
                    add_row(tag, ln)
                pool.wait_ge(dve_done, upto(dve_done, "vec"))
                pool.tensor_tensor(rstdc[:], vec[:], nhalf[0:S, 0:1], ALU.pow).then_inc(pool_done, M.add(pool_done, "rstdc"))
                rsqrt(upto, "ln7", 0)
                rsqrt(upto, "ln7", 1)
                split("L3ca")
                add_row("L3ca", "ln7")
            M.close("blocks")


_OUT = (B, N, D)


def kernel(**inputs):
    import numpy as np
    import concourse.bacc as bacc
    from concourse.bass_utils import run_bass_kernel_spmd

    def given(name):
        for full in (name, name.replace("_", "_xcond_", 1)):
            if full in inputs:
                return np.asarray(inputs[full])
        raise KeyError(name)

    def again(a):
        return np.concatenate([a, a[B - 1:B]])

    fixed = {"qs_rows": constant_rows(MASKROW), "ks_rows": constant_rows(MAXROW)}
    cols = np.concatenate([fixed[n].T if n in fixed else given(n).reshape(-1, P) for n, _ in COLS]).T
    tp_b, ada = given("L1_tp_b").reshape(3, D), given("L2_adaln_b").reshape(6, D)
    router_b = np.zeros((D,), np.float32)
    router_b[0:E] = given("L0_router_b")
    rows = np.stack([given("L0_out_b"), given("L0_gate_b2"), given("L1_sa_bo"), tp_b[0], tp_b[1], tp_b[2], given("L1_ca_bo"),
                     given("L1_b2"), given("L2_sa_proj_b"), ada[2], ada[5], given("L2_ca_proj_b"), given("L2_fc2_b"),
                     given("L3_bp"), router_b])
    ctx, cond, mask = given("ctx_1024"), given("cond_1024"), given("mask_BxS2_ik0")
    twice = np.concatenate([ctx, ctx[:, S - 1:S]], axis=1)
    arrays = {
        "x": again(given("x")), "ctx": ctx, "ctxT": again(twice.transpose(0, 2, 1)), "condT": again(cond.reshape(B, KC, P).transpose(0, 2, 1)),
        "mask": np.concatenate([mask, mask[:, S - 1:S]], axis=1).reshape(B, 1, SP_), "maskT": mask.reshape(B, S, 1),
        "cols": cols, "rows": rows, "ident": np.eye(P, dtype=np.float32), "sel": selections(),
        "e_b2": given("L0_e_b2"), "router_W": given("L0_router_W"), "L0_WqT": given("L0_Wq").T,
    }
    for n in ("L0_Wk", "L0_Wv", "L0_e_w1", "L0_e_w2", "L0_gate_w1", "L0_gate_w2", "L0_out_w", "L1_sa_wq", "L1_sa_wk", "L1_sa_wv",
              "L1_sa_wo", "L1_ca_wq", "L1_ca_wk", "L1_ca_wv", "L1_ca_wo", "L1_tp_w", "L1_w1", "L1_w2", "L2_adaln_w", "L2_qkv_w",
              "L2_sa_proj_w", "L2_q_w", "L2_kv_w", "L2_ca_proj_w", "L2_fc1_w", "L2_fc2_w", "L3_Wq", "L3_Wkv", "L3_Wp",
              "L3_Wss_q", "L3_Wss_kv"):
        arrays[n] = given(n)
    arrays = {n: np.ascontiguousarray(a) for n, a in arrays.items()}

    def program(marks):
        nc = bacc.Bacc("TRN2", target_bir_lowering=False, num_devices=1)
        T = {n: nc.dram_tensor(f"in_{n}", a.shape, mybir.dt.from_np(a.dtype), kind="ExternalInput").ap() for n, a in arrays.items()}
        T["x0"] = nc.dram_tensor("x_after_block0", (B + 1, N, D), F32, kind="Internal").ap()
        T["out"] = nc.dram_tensor("out", _OUT, F32, kind="ExternalOutput").ap()
        build(nc, T, marks)
        return nc

    counted = Marks()
    program(counted)
    nc = program(Marks(counted))
    r = run_bass_kernel_spmd(nc, [{f"in_{n}": a for n, a in arrays.items()}], core_ids=[0])
    return r.results[0]["out"]
```

```python
from contextlib import ExitStack

import concourse.bass as bass
from concourse import mybir

F32 = mybir.dt.float32
F32R = mybir.dt.float32r
I32 = mybir.dt.int32
ACT = mybir.ActivationFunctionType
ALU = mybir.AluOpType
AX = mybir.AxisListType

P = 128
B, N, D, S = 4, 1024, 256, 77
KC = D // P
NT = N // P
HALF = 512
NH = N // HALF
TPH = HALF // P
HEADS, HD = 16, 16
GH = 4
GROUPS = HEADS // GH
SP_ = S + 1
E, RH = 3, 512
SW = SP_ + E
RM = E * RH // P
GM = D // P
FF = 4 * D
FM = FF // P
STACK = 64
MAXROW = 32
MASKROW = 33
PAIRS = HEADS // 2
NSEL = 2 * 2 * (PAIRS // KC)
SEL = {"q": 0, "k": NSEL // 2}
MASKED = -1.0e30
SCALE = HD ** -0.5

COLS = [("L0_ln_gamma", 2), ("L0_ln_beta", 2), ("L0_e_b1", RM), ("L0_gate_b1", GM),
        ("L1_ln1_g", 2), ("L1_ln1_b", 2), ("L1_ln3_g", 2), ("L1_ln3_b", 2), ("L1_ln2_g", 2), ("L1_ln2_b", 2),
        ("L1_sa_bq", 2), ("L1_sa_bk", 2), ("L1_sa_bv", 2), ("L1_ca_bq", 2), ("L1_ca_bk", 2), ("L1_ca_bv", 2),
        ("L1_b1", FM), ("L2_adaln_b", 12), ("L2_qkv_b", 6), ("L2_q_b", 2), ("L2_kv_b", 4), ("L2_fc1_b", FM),
        ("L3_bq", 2), ("L3_bkv", 4), ("L3_bss_q", 4), ("L3_bss_kv", 4), ("qs_rows", 1), ("ks_rows", 1)]
COL, NCOL = {}, 0
for _n, _c in COLS:
    COL[_n] = NCOL
    NCOL += _c
ROWS = ["out_b", "gate_b2", "sa_bo", "tp_b0", "tp_b1", "tp_b2", "ca_bo", "b2", "sa_proj_b", "g_sa", "g_ff",
        "ca_proj_b", "fc2_b", "bp", "router_b"]
ROW = {n: i for i, n in enumerate(ROWS)}
NROW = len(ROWS)


class Marks:

    def __init__(self, known=None):
        self.known, self.count, self.at, self.bank = known, {}, {}, {}
        self.start, self.total = {}, {}

    def add(self, sem, step=None, by=1):
        self.count[sem.name] = self.count.get(sem.name, 0) + by
        if step is not None:
            assert (sem.name, step) not in self.at, step
            self.at[sem.name, step] = self.count[sem.name]
        return by

    def open(self, loop):
        self.before = dict(self.count)
        for name, n in self.count.items():
            self.start.setdefault((loop, name), n)

    def close(self, loop):
        for name, n in self.count.items():
            body = n - self.before.get(name, 0)
            if body:
                self.total[loop, name] = body
                self.count[name] += (B - 1) * body

    def upto(self, loop, it, sem, steps):
        if self.known is None:
            return it + 1
        k = self.known
        n = max([k.at[sem.name, step] for step in steps] or [k.start[loop, sem.name]])
        total = k.total.get((loop, sem.name), 0)
        return it * total + n if total else n

    def put(self, step, bank):
        self.bank[step] = bank

    def where(self, step):
        return 0 if self.known is None else self.known.bank[step]


MODULES = [("L1sa", "self"), ("L1ca", "cross"), ("L1mlp", "mlp"), ("L2sa", "self"), ("L2ca", "cross"), ("L2mlp", "mlp"),
           ("L3ca", "cross")]
KIND = dict(MODULES)


def pass_schedule():
    steps = []

    def put(tag, *which):
        steps.extend((tag,) + w for w in which)

    def stack(g, n, k_by):
        return [k for pair in (2 * g, 2 * g + 1) for k in (("K", "act", "q", pair, n), ("K", k_by, "k", pair, n))]

    def head(kind):
        if kind == "mlp":
            up = [("up", 0, m) for m in range(FM)]
            return up[:2], up[2:4], up[4:]
        first, later = [("P", "q", c, 0) for c in range(KC)], [("P", "k", c, 0) for c in range(KC)]
        if kind == "cross":
            queries = [("K", "act", "q", pair, 0) for pair in range(PAIRS)]
            return first, later, queries[:4] + [("K", "dve", "k", pair, 0) for pair in range(PAIRS)] + queries[4:] + [("V", 0)]
        return first, later, stack(0, 0, "act") + [("V", 0)]

    def self_attention(tag, follow):
        put(tag, ("P", "k", 0, 1), ("P", "q", 0, 1), ("V", 1), ("K", "dve", "k", 0, 1), ("K", "dve", "k", 1, 1))
        maxima, turn = [], []
        for g in range(GROUPS):
            for n in range(NH):
                scores = [("A", g, n, t, j) for t in range(TPH) for j in range(GH)]
                maxima += scores[:2] + turn + scores[2:]
                turn = [("M", g, n)]
        maxima += turn
        beside = ([("K", "act", "q", pair, 1) for pair in (0, 1)] + stack(1, 0, "act") + stack(1, 1, "act")
                  + [("P", w, 1, 1) for w in "qk"] + [k for g in (2, 3) for n in range(NH) for k in stack(g, n, "act")])
        taken = 0

        def more(upto):
            nonlocal taken
            upto = min(int(upto), len(maxima))
            put(tag, *maxima[taken:upto])
            taken = max(taken, upto)

        first_slot = GH * TPH + 3
        for i in range(first_slot):
            more(i + 1)
            put(tag, *beside[i:i + 1])
        rest = beside[first_slot:]
        for i in range(6):
            put(tag, *rest[2 * i:2 * i + 2])
            more(taken + 1)
        assert len(rest) <= 12
        put(tag, ("add",))
        ahead, rate, lag = taken, (GH * TPH + 1) / NT, 2
        units = [(g, n, kt) for g in range(GROUPS) for n in range(NH) for kt in range(NT)]
        end = len(units)
        turn = None
        for u in range(end + lag):
            if u < end:
                more(ahead + rate * (u + 0.5))
                put(tag, *[("S",) + units[u] + (j,) for j in range(2)])
            if u < 2:
                put(tag, ("V", 2 + u))
            if turn is not None:
                put(tag, ("OT",) + turn)
                turn = None
            if u >= lag:
                unit = units[u - lag]
                put(tag, ("PV",) + unit)
                if unit[2] == NT - 1:
                    put(tag, ("O",) + unit[:2])
                    turn = unit[:2]
            if u < end:
                more(ahead + rate * (u + 1))
                put(tag, *[("S",) + units[u] + (j,) for j in range(2, GH)])
            if u == end - 5:
                put(tag, *[("aT", 0, c) for c in range(KC)])
            elif u in (end - 4, end - 3):
                put(tag, ("o", u - end + 4))
            elif u == end - 1:
                put(follow, ("N", 0))

    def cross_attention(tag, follow):
        put(tag, *[("P", "q", c, 1) for c in range(KC)], ("add",))
        beside = [("K", "act", "q", pair, 1) for pair in range(PAIRS)]
        maxima = [("A", i // TPH, n, i % TPH, 0) for n in range(NH) for i in range(GROUPS * TPH)]
        for i, step in enumerate(maxima[:GROUPS * TPH]):
            put(tag, step, *(beside[i // 2:i // 2 + 1] if i % 2 else []))
        put(tag, ("M", 0, 0), *maxima[GROUPS * TPH:-6])
        last = maxima[-6:] + [("M", 0, 1)]
        units = [(g, n, 0) for n in range(NH) for g in range(GROUPS)]
        if follow:
            put(follow, ("split", "W1"), *[("split", "W2")] * (follow == "L2mlp"))
        lag = 2
        for u in range(len(units) + lag):
            if u < len(units):
                put(tag, ("S",) + units[u] + (0,), *last[4 * u:4 * u + 2])
            if u > lag:
                put(tag, ("OT",) + units[u - lag - 1][:2])
            if u >= lag:
                put(tag, ("PV",) + units[u - lag], ("O",) + units[u - lag][:2])
            if u < len(units):
                put(tag, ("S",) + units[u] + (2,), *last[4 * u + 2:4 * u + 4])
            if u == GROUPS + lag + 1:
                put(tag, *[("aT", 0, c) for c in range(KC)])
            elif u == GROUPS + lag + 2:
                put(tag, ("o", 0))

    def after_attention(tag, follow):
        put(tag, ("OT", GROUPS - 1, NH - 1), *[("o", 1)] * (KIND[tag] == "cross"))
        first, later, rest = head(KIND[follow]) if follow else ([], [], [])
        if not follow:
            put(tag, *[("aT", NH - 1, c) for c in range(KC)], ("out", 0), ("out", 1), ("o", 2), ("o", 3), ("out", 2), ("out", 3))
            return
        if KIND[follow] == "cross":
            put(follow, ("zero",), ("T", 0))
            put(tag, *[("aT", NH - 1, c) for c in range(KC)])
            put(follow, *first[:1])
            put(tag, ("o", 2), ("o", 3))
        else:
            put(tag, *[("aT", NH - 1, c) for c in range(KC)])
            put(follow, ("N", 0))
            put(tag, ("o", 2), ("o", 3))
            put(follow, ("T", 0), ("R",), ("N", 1), ("T", 1), *first, *later, *rest)
            return
        put(follow, ("R",), *first[1:], *later)
        second_half(follow, rest)

    def second_half(tag, rest):
        if KIND[tag] == "cross":
            put(tag, *rest[:4], ("N", 1), *rest[4:4 + PAIRS], ("T", 1), *rest[4 + PAIRS:])
        else:
            put(tag, *rest, ("N", 1), ("T", 1))

    def mlp(tag, follow):
        put(follow, *[("context",)] * (follow == "L3ca"))
        put(tag, ("add",))
        first, later, rest = head(KIND[follow])
        put(tag, ("up", 1, 0), ("up", 1, 1), *[("split", "W2")] * (tag == "L1mlp"), *[("up", 1, m) for m in range(2, 5)])
        put(follow, ("mod",), *[("zero",)] * (follow == "L3ca"))
        put(tag, *[("up", 1, m) for m in range(5, FM)], ("o", 0))
        put(follow, *[("cT",)] * (follow == "L3ca"))
        put(tag, ("o", 1))
        put(follow, ("N", 0))
        put(tag, ("o", 2), ("o", 3))
        put(follow, ("T", 0), *first)
        put(follow, ("R",), *later)
        second_half(follow, rest)

    tag = MODULES[0][0]
    first, later, rest = head(KIND[tag])
    put(tag, ("begin", 0), ("begin", 1), ("N", 0), ("T", 0), ("N", 1), *first, *later, ("T", 1), *rest, ("R",))
    for i, (tag, kind) in enumerate(MODULES):
        follow = MODULES[i + 1][0] if i + 1 < len(MODULES) else None
        if kind == "mlp":
            mlp(tag, follow)
        else:
            (self_attention if kind == "self" else cross_attention)(tag, follow)
            after_attention(tag, follow)
    return steps


PASS = pass_schedule()


def stacked(e, lo, hi):
    return slice(STACK * e + lo, STACK * e + hi)


def stacks_for(tag, engine, g, n):
    return [k for k in PASS if k[:3] == (tag, "K", engine) and k[4] * 2 // GH == g and (k[3] == "k" or k[5] == n)]


def constant_rows(row):
    import numpy as np

    out = np.zeros((P, 1), np.float32)
    out[[row, STACK + row]] = 1.0
    return out


def selections():
    import numpy as np

    out = np.zeros((P, NSEL + 1, P), np.float32)
    out[0, NSEL, [MASKROW, STACK + MASKROW]] = 1.0
    for which, places in (("q", ((0, 16), (48,))), ("k", ((0, 48), (16,)))):
        for part in range(2):
            for pp in range(PAIRS // KC):
                for e in range(2):
                    for row in places[part]:
                        for d in range(HD):
                            out[(2 * pp + e) * HD + d, SEL[which] + part * (PAIRS // KC) + pp, STACK * e + row + d] = 1.0
    return out


def build(nc, T, M):
    ctx = ExitStack()
    with ctx:
        at = [16512]

        def place(name, shape, dt=F32, offset=None):
            size = 4
            for d in shape[1:]:
                size *= d
            size = -(-size // 32) * 32
            if offset is None:
                offset = at[0]
                at[0] += size
            return nc.alloc_sbuf_tensor_at(name, shape, dt, offset=offset)

        def sem(name):
            return ctx.enter_context(nc.semaphore(name))

        r1 = at[0]
        qs = place("qs", [P, PAIRS, N], F32R)
        ks = place("ks", [P, PAIRS, N], F32R)
        kz = place("kz", [P, PAIRS, 2, SP_], F32R, offset=at[0] - 4 * PAIRS * N)
        behind = at[0] - 4 * PAIRS * N + 4 * PAIRS * 2 * SP_ + 4 * 32
        W1h = place("W1h", [P, KC, FF], F32R, offset=behind)
        W2h = place("W2h", [P, FM, D], F32R, offset=behind + 4 * KC * FF)
        hTl = place("hTl", [P, KC, N], F32R, offset=behind + 4 * KC * FF + 4 * FM * D)
        assert behind + 4 * KC * FF + 4 * FM * D + 4 * KC * N <= at[0]
        hidh = place("hidh", [P, NH, FM, HALF], F32R, offset=r1)
        r1_end, at[0] = at[0], r1
        ew1l = place("ew1l", [P, KC, E, RH], F32R, offset=at[0])
        ew1 = place("ew1", [P, 6, E, RH])
        ew2 = place("ew2", [P, RM, D])
        gw1l = place("gw1l", [P, KC, D], F32R, offset=at[0])
        gw1 = place("gw1", [P, 6, D])
        gw2 = place("gw2", [P, KC, D])
        outw = place("outw", [P, KC, D])
        wqT = place("wqT", [P, KC, D])
        wk0 = place("wk0", [P, KC, D])
        wv0 = place("wv0", [P, KC, D])
        assert at[0] <= r1_end
        at[0] = r1_end
        r2 = at[0]
        probs = place("probs", [P, 4, GH, HALF])
        r2_end, at[0] = at[0], r2
        qh = place("qh", [P, KC, N], F32R)
        ql = place("ql", [P, KC, N], F32R)
        kh = place("kh", [P, KC, N], F32R)
        kl = place("kl", [P, KC, N], F32R)
        assert at[0] <= r2_end
        at[0] = r2
        hidl = place("hidl", [P, NH, FM, HALF], F32R, offset=r2)
        hid = place("hid", [P, NH, FM, HALF])
        at[0] = r2
        hid0 = place("hid0", [P, RM + GM, HALF])
        at[0] = r2
        sel_in = place("sel_in", [P, NSEL + 1, P])
        at[0] = r2_end
        x = place("x", [P, NT, D])
        hTh = place("hTh", [P, KC, N], F32R, offset=at[0])
        hT = place("hT", [P, KC, N])
        tok = place("tok", [P, NT, D])
        whole = place("whole", [P, 4, HALF], offset=at[0] - 4 * NT * D)
        pb = place("pb", [P, E, HALF], offset=at[0] - 4 * NT * D)
        ew1h = place("ew1h", [P, KC, E, RH], F32R, offset=at[0])
        gw1h = place("gw1h", [P, KC, D], F32R, offset=at[0] + 4 * KC * E * RH)
        assert KC * (E * RH + D) <= NT * HEADS * 32
        v = place("v", [P, NT, HEADS, 32])
        ow = place("ow", [P, N])
        wT = place("wT", [P, N], offset=at[0] - 4 * N)
        rT = place("rT", [P, KC, HALF])
        mrow = place("mrow", [P, N], offset=at[0] - 4 * N)
        W1l = place("W1l", [P, KC, FF], F32R, offset=at[0] + 2 * 4 * 2048)
        W2l = place("W2l", [P, FM, D], F32R, offset=at[0] + 3 * 4 * 2048)
        hTl0 = place("hTl0", [P, KC, N], F32R, offset=at[0])
        slot = [place(f"slot{i}", [P, 2048]) for i in range(4)]
        after_slots, at[0] = at[0], at[0] - 3 * 4 * 2048
        u0 = place("u0", [P, RM * P + D + E])
        pT = place("pT", [E, N])
        kv0T = place("kv0T", [P, 2 * KC, SP_])
        a0 = place("a0", [P, KC, SW])
        e1 = place("e1", [P, TPH, SP_])
        eb2 = place("eb2", [E, D])
        assert at[0] <= after_slots
        at[0] = after_slots
        adw = place("adw", [P, KC, 6 * D])
        xin = place("xin", [P, NT, D], offset=at[0] - 4 * KC * 6 * D)
        ident = place("ident", [P, P])
        sel = place("sel", [P, NSEL + 1, P], F32R)
        cols = place("cols", [P, NCOL])
        rows = place("rows", [NROW, D])
        router = place("router", [P, 6, E])
        cond = place("cond", [P, KC])
        scond = place("scond", [P, KC])
        ctxT = place("ctxT", [P, KC, SP_])
        ctxk = place("ctxk", [S, D])
        kvT = place("kvT", [P, KC, SP_])
        e0 = place("e0", [P, TPH, SP_])
        e01 = (e0, e1)
        small = place("small", [P, 128])
        mi = place("mi", [1, SP_], I32)
        mic = place("mic", [S, 1], I32)
        mrowb, mcolb = place("mrowb", [1, SP_], F32R), place("mcolb", [S, 1])
        mx = place("mx", [P, 2, TPH, HEADS])
        grow = place("grow", [P, D])
        rrow = place("rrow", [P, D])
        sg = place("sg", [P, 2, 2, D], offset=r2_end - 4 * N)
        assert 4 * (RM + GM) * HALF + 4 * N <= r2_end - r2

        st = small[:, 0:6 * NT].rearrange("p (t k) -> p t k", k=6)
        mv = small[:, 48:48 + 2 * NT].rearrange("p (t k) -> p t k", k=2)
        ve, rstd, nhalf = small[:, 64:72], small[:, 72:80], small[:, 80:88]
        zero = small[:, 88:89]
        nmx, es, rc4 = small[:, 102:110], small[:, 110:118], small[:, 118:126]
        lg = place("lg", [P, NT, E])
        qs_rows, ks_rows = (cols[:, COL[n]:COL[n] + 1] for n in ("qs_rows", "ks_rows"))
        rc = place("rc", [P, TPH * GH])
        rmx, rs, rrs = place("rmx", [P, NT]), place("rs", [P, NT]), place("rrs", [P, NT])
        mod = place("mod", [P, 12])
        mod3 = place("mod3", [P, 8])
        stc, mvc = place("stc", [S, 6]), place("mvc", [S, 2])
        vec, rstdc = place("vec", [S, 1]), place("rstdc", [S, 1])
        assert at[0] <= 229368, at[0]

        ps = ctx.enter_context(nc.psum_tensor("ps", [P, 8, HALF], F32))

        def w256(i, k, n=D):
            return slot[i][:, 512 * k:512 * k + KC * n].rearrange("p (c n) -> p c n", c=KC)

        W1 = slot[2][:].rearrange("p (c n) -> p c n", c=KC)
        W2 = slot[3][:].rearrange("p (c n) -> p c n", c=FM)
        tpw = slot[3][:, 0:KC * 3 * D].rearrange("p (c n) -> p c n", c=KC)

        mm_done, act_done, dve_done, pool_done = sem("mm_done"), sem("act_done"), sem("dve_done"), sem("pool_done")
        constants_loaded = sem("constants_loaded")
        experts_loaded = {name: sem(f"experts_{name}_loaded") for name in ("kv", "q", "tokens", "in", "out")}
        xin_loaded, residual_loaded, conditions_loaded = sem("xin_loaded"), sem("residual_loaded"), sem("conditions_loaded")
        slot_loaded = [sem(f"slot{i}_loaded") for i in range(5)]
        maxima_stacked = [[sem(f"maxima_{g}_{n}_stacked") for n in range(NH)] for g in range(GROUPS)]
        x_stored, out_stored = sem("x_stored"), [sem(f"out{t2}_stored") for t2 in range(4)]

        block = ctx.enter_context(nc.Block())

        def col(name, c):
            return cols[:, COL[name] + c:COL[name] + c + 1]

        ATT = {
            "L1sa": (False, w256(0, 0), w256(0, 1), w256(0, 2), w256(0, 3), ("L1_sa_bq", 0), ("L1_sa_bk", 0), ("L1_sa_bv", 0)),
            "L1ca": (True, w256(1, 0), w256(1, 1), w256(1, 2), w256(1, 3), ("L1_ca_bq", 0), ("L1_ca_bk", 0), ("L1_ca_bv", 0)),
            "L2sa": (False, w256(0, 0, 768)[:, :, 0:D], w256(0, 0, 768)[:, :, D:2 * D], w256(0, 0, 768)[:, :, 2 * D:],
                     w256(0, 3), ("L2_qkv_b", 0), ("L2_qkv_b", 2), ("L2_qkv_b", 4)),
            "L2ca": (True, w256(1, 0), w256(1, 1, 512)[:, :, 0:D], w256(1, 1, 512)[:, :, D:], w256(1, 3),
                     ("L2_q_b", 0), ("L2_kv_b", 0), ("L2_kv_b", 2)),
            "L3ca": (True, w256(2, 0), w256(2, 1, 512)[:, :, 0:D], w256(2, 1, 512)[:, :, D:], w256(2, 3),
                     ("L3_bq", 0), ("L3_bkv", 0), ("L3_bkv", 2)),
        }
        SLOT_OF = {"L1sa": slot_loaded[0], "L1ca": slot_loaded[1], "L2sa": slot_loaded[0], "L2ca": slot_loaded[1],
                   "L3ca": slot_loaded[2]}
        SLOT_OF.update(L1mlp=slot_loaded[2], L2mlp=slot_loaded[2])
        LAST_LOAD = {tag: tag if KIND[tag] == "mlp" else (tag, 3) for tag in KIND}
        LN_OF = {"L1sa": "ln1", "L1ca": "ln3", "L1mlp": "ln2", "L2sa": "ln4", "L2ca": "ln5", "L2mlp": "ln6", "L3ca": "ln7"}
        EPS = {"ln1": 1e-5, "ln3": 1e-5, "ln2": 1e-5, "ln4": 1e-6, "ln5": 1e-6, "ln6": 1e-6, "ln7": 1e-5}
        NEXT_LN = {tag: LN_OF[follow] for (tag, _), (follow, _) in zip(MODULES, MODULES[1:])}
        GATED = ("L2sa", "L2mlp")
        LOADED = 16

        def wide(src):
            return src.rearrange("(c p) n -> p c n", p=P)

        UNITS = {tag: [k for k in PASS if k[:2] == (tag, "PV")] for tag in ATT}

        def buffer_of(name):
            tag, _, g, n, kt = name[:5]
            return UNITS[tag].index((tag, "PV", g, n, kt)) % 4

        def whole_of(name):
            same_half = [k for k in PASS if k[:2] == name[:2] and k[4] == name[4]]
            i = same_half.index(name)
            return 2 * name[4] + i % 2, same_half[i - 2] if i >= 2 else None

        def maxima_of(tag, g, n):
            return (n, HEADS, GH * g, ("M", 0, n)) if KIND[tag] == "cross" else ((NH * g + n) % 2, GH, 0, ("M", g, n))

        @block.sync
        def _(sp):
            sp.dma_start(ident[:], T["ident"]).then_inc(constants_loaded, LOADED)
            sp.dma_start(router[:], wide(T["router_W"])).then_inc(constants_loaded, LOADED)
            sp.dma_start(cols[:], T["cols"]).then_inc(constants_loaded, LOADED)
            sp.dma_start(rows[:], T["rows"]).then_inc(constants_loaded, LOADED)
            sp.dma_start(eb2[:], T["e_b2"]).then_inc(constants_loaded, LOADED)
            sp.dma_start(sel_in[:], T["sel"]).then_inc(constants_loaded, LOADED)
            inner = [(ew1[:, c], T["L0_e_w1"][:, c * P:(c + 1) * P, :].rearrange("e p r -> p e r")) for c in range(6)]
            outer = [(ew2[:, e * 4:(e + 1) * 4], wide(T["L0_e_w2"][e])) for e in range(E)]
            for name, parts in (("kv", [(wk0[:], wide(T["L0_Wk"])), (wv0[:], wide(T["L0_Wv"]))]),
                                ("q", [(wqT[:], wide(T["L0_WqT"]))]),
                                ("tokens", inner[:KC] + [(gw1[:], wide(T["L0_gate_w1"]))]),
                                ("in", inner[KC:]),
                                ("out", outer + [(gw2[:], wide(T["L0_gate_w2"])), (outw[:], wide(T["L0_out_w"]))])):
                for i, (dst, src) in enumerate(parts):
                    sp.dma_start(dst, src).then_inc(experts_loaded[name], M.add(experts_loaded[name], i, LOADED))
            sp.wait_ge(mm_done, M.upto("blocks", 0, mm_done, ()))
            for k, n in enumerate(("wq", "wk", "wv", "wo")):
                sp.dma_start(w256(0, k), wide(T[f"L1_sa_{n}"])).then_inc(slot_loaded[0], M.add(slot_loaded[0], ("L1sa", k), LOADED))
            M.open("blocks")
            with sp.Fori(0, B) as it:
                def upto(sem, *steps):
                    return M.upto("blocks", it, sem, steps)

                sp.wait_ge(mm_done, upto(mm_done))
                sp.dma_start(tpw, wide(T["L1_tp_w"])).then_inc(slot_loaded[3], M.add(slot_loaded[3], "tp", LOADED))
                for k, n in enumerate(("wq", "wk", "wv", "wo")):
                    sp.dma_start(w256(1, k), wide(T[f"L1_ca_{n}"])).then_inc(slot_loaded[1], M.add(slot_loaded[1], ("L1ca", k), LOADED))
                sp.dma_start(W1, wide(T["L1_w1"])).then_inc(slot_loaded[2], M.add(slot_loaded[2], "L1mlp", LOADED))

                def stack_maxima(tag):
                    if ATT[tag][0]:
                        order = [(g, n) for n in range(NH) for g in range(GROUPS)]
                    else:
                        order = [(g, n) for g in range(GROUPS) for n in range(NH)]
                    for g, n in order:
                        z, _, j0, step = maxima_of(tag, g, n)
                        sp.wait_ge(act_done, upto(act_done, (tag,) + step))
                        for j in range(GH):
                            h = GH * g + j
                            sp.dma_start(qs[stacked(h % 2, MAXROW, MAXROW + 1), h // 2, n * HALF:(n + 1) * HALF].bitcast(F32),
                                         mrow[j0 + j:j0 + j + 1, z * HALF:(z + 1) * HALF]
                                         ).then_inc(maxima_stacked[g][n], M.add(maxima_stacked[g][n], (tag, j), LOADED))

                stack_maxima("L1sa")
                sp.wait_ge(pool_done, upto(pool_done, ("row", "L1sa")))
                sp.dma_start(adw[:], wide(T["L2_adaln_w"])).then_inc(slot_loaded[4], M.add(slot_loaded[4], "L2", LOADED))
                sp.wait_ge(mm_done, upto(mm_done, ("L1sa", "o", 3)))
                sp.dma_start(w256(0, 0, 768), wide(T["L2_qkv_w"])).then_inc(slot_loaded[0], M.add(slot_loaded[0], ("L2sa", 0), LOADED))
                sp.dma_start(w256(0, 3), wide(T["L2_sa_proj_w"])).then_inc(slot_loaded[0], M.add(slot_loaded[0], ("L2sa", 3), LOADED))
                stack_maxima("L1ca")
                sp.wait_ge(mm_done, upto(mm_done, ("row", "L1mlp")))
                sp.dma_start(W2, wide(T["L1_w2"])).then_inc(slot_loaded[3], M.add(slot_loaded[3], "L1mlp", LOADED))
                sp.wait_ge(mm_done, upto(mm_done, ("L1ca", "o", 3)))
                sp.dma_start(w256(1, 0), wide(T["L2_q_w"])).then_inc(slot_loaded[1], M.add(slot_loaded[1], ("L2ca", 0), LOADED))
                sp.dma_start(w256(1, 1, 512), wide(T["L2_kv_w"])).then_inc(slot_loaded[1], M.add(slot_loaded[1], ("L2ca", 1), LOADED))
                sp.dma_start(w256(1, 3), wide(T["L2_ca_proj_w"])).then_inc(slot_loaded[1], M.add(slot_loaded[1], ("L2ca", 3), LOADED))
                sp.wait_ge(mm_done, upto(mm_done, ("L1mlp", "up", NH - 1, FM - 1)))
                sp.dma_start(W1, wide(T["L2_fc1_w"])).then_inc(slot_loaded[2], M.add(slot_loaded[2], "L2mlp", LOADED))
                sp.wait_ge(mm_done, upto(mm_done, ("L1mlp", "o", 3)))
                sp.dma_start(W2, wide(T["L2_fc2_w"])).then_inc(slot_loaded[3], M.add(slot_loaded[3], "L2mlp", LOADED))
                stack_maxima("L2sa")
                sp.wait_ge(mm_done, upto(mm_done, ("L2sa", "o", 3)))
                for k, n in enumerate(("wq", "wk", "wv", "wo")):
                    sp.dma_start(w256(0, k), wide(T[f"L1_sa_{n}"])).then_inc(slot_loaded[0], M.add(slot_loaded[0], None, LOADED))
                stack_maxima("L2ca")
                sp.wait_ge(mm_done, upto(mm_done, ("L2ca", "o", 3)))
                sp.dma_start(w256(1, 0, 512), wide(T["L3_Wss_q"])).then_inc(slot_loaded[1], M.add(slot_loaded[1], None, LOADED))
                sp.dma_start(w256(1, 2, 512), wide(T["L3_Wss_kv"])).then_inc(slot_loaded[1], M.add(slot_loaded[1], "L3ss", LOADED))
                sp.wait_ge(mm_done, upto(mm_done, ("L2mlp", "up", NH - 1, FM - 1)))
                sp.dma_start(w256(2, 0), wide(T["L3_Wq"])).then_inc(slot_loaded[2], M.add(slot_loaded[2], ("L3ca", 0), LOADED))
                sp.dma_start(w256(2, 1, 512), wide(T["L3_Wkv"])).then_inc(slot_loaded[2], M.add(slot_loaded[2], ("L3ca", 1), LOADED))
                sp.dma_start(w256(2, 3), wide(T["L3_Wp"])).then_inc(slot_loaded[2], M.add(slot_loaded[2], ("L3ca", 3), LOADED))
                stack_maxima("L3ca")
            M.close("blocks")

        @block.tensor
        def _(pe):
            owner = {}
            ring = [0]

            def mm(out, lhsT, rhs, start=True, stop=True):
                return pe.matmul(out, lhsT, rhs, start=start, stop=stop)

            def take(step, act=None, dve=None, banks=None):
                if banks is None:
                    banks = (ring[0] % 8,)
                    ring[0] += 1
                was = [owner[b] for b in banks if b in owner]
                for b in banks:
                    owner[b] = ("act", act) if act else ("dve", dve)
                M.put(step, banks[0])
                return banks[0], [s for e, s in was if e == "act"], [s for e, s in was if e == "dve"]

            def pick(name, n=P):
                r = ROW[name]
                return ident[0:NROW, r:r + 1].to_broadcast([NROW, n]), rows[:]

            def turn(upto, tag):
                for n in range(NH):
                    for c in range(KC):
                        b, act_was, dve_was = take((tag, "T", n, c), act=(tag, "hT", n, c))
                        pe.wait_ge(act_done, upto(act_done, *act_was))
                        for i in range(TPH):
                            t = TPH * n + i
                            pe.wait_ge(dve_done, upto(dve_done, (tag, "xh", t), *dve_was))
                            ins = pe.transpose(ps[:, b, i * P:(i + 1) * P], tok[:, t, c * P:(c + 1) * P], ident[:])
                        ins.then_inc(mm_done, M.add(mm_done, (tag, "T", n, c)))

            pe.wait_ge(constants_loaded, 6 * LOADED)
            pe.wait_ge(dve_done, 1)
            pe.transpose(ps[:, 0, 0:P], ident[:], ident[:]).then_inc(mm_done, M.add(mm_done))
            M.open("experts")
            with pe.Fori(0, B) as it:
                def upto(sem, *steps):
                    return M.upto("experts", it, sem, steps)

                b, act_was, dve_was = take(("L0", "kv"), act=("L0", "kv"))
                pe.wait_ge(act_done, upto(act_done))
                pe.wait_ge(dve_done, upto(dve_done))
                pe.wait_ge(conditions_loaded, upto(conditions_loaded, "first"))
                pe.wait_ge(experts_loaded["kv"], 2 * LOADED)
                for i, w in enumerate((wk0, wv0)):
                    for c in range(KC):
                        o = (i * KC + c) * SP_
                        for k in range(KC):
                            ins = mm(ps[:, b, o:o + SP_], w[:, k, c * P:(c + 1) * P], ctxT[:, k, :], k == 0, k == KC - 1)
                ins.then_inc(mm_done, M.add(mm_done, ("L0", "kv")))
                b, act_was, dve_was = take(("L0", "a"), act=("L0", "a"))
                pe.wait_ge(act_done, upto(act_done, ("L0", "kv")))
                pe.wait_ge(experts_loaded["q"], LOADED)
                for c in range(KC):
                    for k in range(KC):
                        ins = mm(ps[:, b, c * SP_:(c + 1) * SP_], wqT[:, k, c * P:(c + 1) * P], kv0T[:, k, :], k == 0, k == KC - 1)
                ins.then_inc(mm_done, M.add(mm_done, ("L0", "a")))
                turn(upto, "ln0")
                for n in range(NH):
                    b, act_was, dve_was = take(("L0", "s", n), act=("L0", "e", n, TPH - 1))
                    pe.wait_ge(act_done, upto(act_done, ("L0", "a"), *(("ln0", "hT", n, c) for c in range(KC)), *act_was))
                    pe.wait_ge(dve_done, upto(dve_done, *dve_was))
                    for i in range(TPH):
                        t = TPH * n + i
                        for k in range(KC):
                            ins = mm(ps[:, b, i * SW:(i + 1) * SW], whole[:, KC * n + k, i * P:(i + 1) * P], a0[:, k, :], k == 0, k == KC - 1)
                    ins.then_inc(mm_done, M.add(mm_done, ("L0", "s", n)))
                for e in range(E + 1):
                    b, act_was, dve_was = take(("L0", "u", e), dve=("L0", "u", e))
                    pe.wait_ge(act_done, upto(act_done, *act_was))
                    pe.wait_ge(dve_done, upto(dve_done, *dve_was))
                    pe.wait_ge(experts_loaded["tokens"], 3 * LOADED)
                    pe.wait_ge(experts_loaded["in"], 4 * LOADED)
                    all_keys = [cond[:, k:k + 1].to_broadcast([P, S]) for k in range(KC)]
                    for k in range(KC):
                        keys, inner, anchor = kv0T[:, KC + k, 0:S], KC + k, 2 * KC + k
                        if e < E:
                            mm(ps[0:S, b, :], keys, ew1[:, inner, e, :], k == 0, False)
                            ins = mm(ps[0:S, b, :], all_keys[k], ew1[:, anchor, e, :], False, k == KC - 1)
                        else:
                            mm(ps[0:S, b, 0:D], keys, gw1[:, inner, :], k == 0, False)
                            mm(ps[0:S, b, 0:D], all_keys[k], gw1[:, anchor, :], False, k == KC - 1)
                    if e == E:
                        lhs, rr = pick("router_b", S)
                        mm(ps[0:S, b, D:D + E], lhs, rr[:, 0:E], True, False)
                        for k in range(KC):
                            mm(ps[0:S, b, D:D + E], kv0T[:, KC + k, 0:S], router[:, KC + k, :], False, False)
                            ins = mm(ps[0:S, b, D:D + E], all_keys[k], router[:, 2 * KC + k, :], False, k == KC - 1)
                    ins.then_inc(mm_done, M.add(mm_done, ("L0", "u", e)))

                def hidden(n, m):
                    b, act_was, dve_was = take(("L0", "h", n, m), act=("L0", "h", n, m))
                    pe.wait_ge(act_done, upto(act_done, *act_was))
                    pe.wait_ge(dve_done, upto(dve_done, *dve_was))
                    pe.wait_ge(pool_done, upto(pool_done, *(("ln0", "lo", n, c) for c in range(KC))))
                    half = slice(n * HALF, (n + 1) * HALF)
                    for k in range(KC):
                        if m < RM:
                            wh, wl = (w[:, k, m // 4, (m % 4) * P:(m % 4 + 1) * P] for w in (ew1h, ew1l))
                        else:
                            wh, wl = (w[:, k, (m - RM) * P:(m - RM + 1) * P] for w in (gw1h, gw1l))
                        for w, h in ((wh, hTh), (wh, hTl0), (wl, hTh)):
                            mm(ps[:, b, :], w, h[:, k, half], (k, w is wh, h is hTh) == (0, True, True), False)
                    return b

                def evidence(n, m, b):
                    mm(ps[:, b, :], u0[0:S, m * P:(m + 1) * P], wT[0:S, n * HALF:(n + 1) * HALF], False, True
                       ).then_inc(mm_done, M.add(mm_done, ("L0", "h", n, m)))

                def output(n):
                    for i2 in range(2):
                        t2 = 2 * n + i2
                        b, act_was, dve_was = take(("L0", "o", t2), dve=("L0", "sg", t2))
                        pe.wait_ge(act_done, upto(act_done, *(("L0", "rt", n, c) for c in range(KC)), *act_was))
                        pe.wait_ge(dve_done, upto(dve_done, *dve_was))
                        for i in range(2):
                            tt = slice((2 * i2 + i) * P, (2 * i2 + i + 1) * P)
                            mm(ps[:, b, i * D:(i + 1) * D], *pick("out_b"), True, False)
                            for k in range(KC):
                                ins = mm(ps[:, b, i * D:(i + 1) * D], rT[:, k, tt], outw[:, k, :], False, k == KC - 1)
                        ins.then_inc(mm_done, M.add(mm_done, ("L0", "o", t2)))

                early = [hidden(0, m) for m in range(4)]
                for n in range(NH):
                    b, act_was, dve_was = take(("L0", "wT", n), act=("L0", "wT", n))
                    pe.wait_ge(act_done, upto(act_done, *act_was))
                    pe.wait_ge(dve_done, upto(dve_done, ("L0", "w", n), *dve_was))
                    for i in range(TPH):
                        ins = pe.transpose(ps[0:S, b, i * P:(i + 1) * P], e01[n][:, i, 0:S], ident[:])
                    ins.then_inc(mm_done, M.add(mm_done, ("L0", "wT", n)))
                for n in range(NH):
                    b, act_was, dve_was = take(("L0", "r", n), dve=("L0", "lt", n))
                    pe.wait_ge(act_done, upto(act_done, ("L0", "wT", n), *act_was))
                    pe.wait_ge(dve_done, upto(dve_done, ("L0", "u", E), *dve_was))
                    for i in range(TPH):
                        t = TPH * n + i
                        ins = mm(ps[:, b, i * E:(i + 1) * E], wT[0:S, t * P:(t + 1) * P], u0[0:S, RM * P + D:])
                    ins.then_inc(mm_done, M.add(mm_done, ("L0", "r", n)))
                for n in range(NH):
                    half = slice(n * HALF, (n + 1) * HALF)
                    for m in range(RM + GM):
                        evidence(n, m, early[m] if n == 0 and m < len(early) else hidden(n, m))
                        if n and m == 2:
                            output(n - 1)
                        if m // 4 == 2 and m % 4 < E:
                            e = m % 4
                            b, act_was, dve_was = take(("L0", "pb", n, e), act=("L0", "pb", n, e))
                            pe.wait_ge(act_done, upto(act_done, *act_was))
                            pe.wait_ge(dve_done, upto(dve_done, ("L0", "p"), *dve_was))
                            for i in range(TPH):
                                ins = mm(ps[:, b, i * P:(i + 1) * P], lg[:, TPH * n + i, e:e + 1].to_broadcast([P, P]), ident[:])
                            ins.then_inc(mm_done, M.add(mm_done, ("L0", "pb", n, e)))
                    b, act_was, dve_was = take(("L0", "pT", n), act=("L0", "pT", n))
                    pe.wait_ge(act_done, upto(act_done, *act_was))
                    pe.wait_ge(dve_done, upto(dve_done, *dve_was))
                    for i in range(TPH):
                        ins = pe.transpose(ps[0:E, b, i * P:(i + 1) * P], lg[:, TPH * n + i, :], ident[:])
                    ins.then_inc(mm_done, M.add(mm_done, ("L0", "pT", n)))
                    for i2 in range(2):
                        t2 = 2 * n + i2
                        b, act_was, dve_was = take(("L0", "g", t2), act=("L0", "g", t2))
                        pe.wait_ge(act_done, upto(act_done, *(("L0", "h", n, RM + c) for c in range(KC)), *act_was))
                        pe.wait_ge(dve_done, upto(dve_done, *dve_was))
                        pe.wait_ge(experts_loaded["out"], 5 * LOADED)
                        for i in range(2):
                            tt = slice((2 * i2 + i) * P, (2 * i2 + i + 1) * P)
                            mm(ps[:, b, i * D:(i + 1) * D], *pick("gate_b2"), True, False)
                            for k in range(KC):
                                ins = mm(ps[:, b, i * D:(i + 1) * D], hid0[:, RM + k, tt], gw2[:, k, :], False, k == KC - 1)
                        ins.then_inc(mm_done, M.add(mm_done, ("L0", "g", t2)))
                    for c in range(KC):
                        b, act_was, dve_was = take(("L0", "rt", n, c), act=("L0", "rt", n, c))
                        pe.wait_ge(act_done, upto(act_done, ("L0", "pT", n), *act_was))
                        pe.wait_ge(dve_done, upto(dve_done, *dve_was))
                        mm(ps[:, b, :], eb2[:, c * P:(c + 1) * P], pT[:, half], True, False)
                        for m in range(RM):
                            if c == 0:
                                pe.wait_ge(dve_done, upto(dve_done, ("L0", "hp", n, m)))
                            ins = mm(ps[:, b, :], ew2[:, m, c * P:(c + 1) * P], hid0[:, m, :], False, m == RM - 1)
                        ins.then_inc(mm_done, M.add(mm_done, ("L0", "rt", n, c)))
                output(NH - 1)
            M.close("experts")

            owner.clear()
            tp = [tpw[:, :, i * D:(i + 1) * D] for i in range(3)]
            silu_cond = [scond[:, c:c + 1].to_broadcast([P, P]) for c in range(KC)]

            def silu_of(w):
                return [(silu_cond[c], w[:, c, :]) for c in range(KC)]

            ROWS_OF = {
                "L1sa": [("L1sa", silu_of(tp[0]) + [pick("tp_b0"), pick("sa_bo")])],
                "L1ca": [("L1ca", silu_of(tp[1]) + [pick("tp_b1"), pick("ca_bo")])],
                "L1mlp": [("L1mlp", silu_of(tp[2]) + [pick("tp_b2"), pick("b2")])],
                "L2sa": [("L2sa_g", silu_of(adw[:, :, 2 * D:3 * D]) + [pick("g_sa")]), ("L2sa", [pick("sa_proj_b")])],
                "L2ca": [("L2ca", [pick("ca_proj_b")])],
                "L2mlp": [("L2mlp_g", silu_of(adw[:, :, 5 * D:6 * D]) + [pick("g_ff")]), ("L2mlp", [pick("fc2_b")])],
                "L3ca": [("L3ca", [pick("bp")])],
            }
            rings = {"small": 0, "single": 0, "wide": 0}
            M.open("blocks")
            with pe.Fori(0, B) as it:
                def upto(sem, *steps):
                    return M.upto("blocks", it, sem, steps)

                weights_used = set()
                for name in PASS:
                    tag, step = name[0], name[1:]
                    kind, cross, ln = step[0], KIND[tag] == "cross", LN_OF[tag]
                    kw = S if cross else P
                    if tag in ATT:
                        _, wq, wk, wv, wo, *_ = ATT[tag]
                        src = {"L3ca": kvT}.get(tag, ctxT if cross else hT)
                    alone = KIND[tag] != "self"

                    def small():
                        rings["small"] += 1
                        if not alone and kind not in ("T", "R", "mod"):
                            b = 2 * (rings["small"] % 2)
                            return b, (b, b + 1) if kind == "A" else (b,)
                        many = kind == "A" or KIND[tag] == "mlp" and kind == "o"
                        b = (0, 1, 6, 7)[rings["small"] % 4] if many else rings["small"] % 2
                        return b, (b,)

                    def single():
                        rings["single"] += 1
                        if alone:
                            return (2 + rings["single"] % 4,)
                        maxima_done = kind == "S" and PASS.index((tag, "M", GROUPS - 1, NH - 1)) < PASS.index(name)
                        return ((4, 5, 6, 1, 3)[rings["single"] % 5] if maxima_done else 4 + rings["single"] % 3,)

                    if kind in ("P", "V") and tag not in weights_used:
                        weights_used.add(tag)
                        pe.wait_ge(SLOT_OF[tag], upto(SLOT_OF[tag], LAST_LOAD[tag]))
                    if kind in ("begin", "N", "add", "O", "zero", "context", "out", "split"):
                        continue
                    if kind == "T":
                        n = step[1]
                        for c in range(KC):
                            b, banks = small()
                            _, act_was, dve_was = take((ln, "T", n, c), act=(ln, "hT", n, c), banks=banks)
                            pe.wait_ge(act_done, upto(act_done, *act_was))
                            for i in range(TPH):
                                t = TPH * n + i
                                pe.wait_ge(dve_done, upto(dve_done, (ln, "xh", t), *dve_was))
                                ins = pe.transpose(ps[:, b, i * P:(i + 1) * P], tok[:, t, c * P:(c + 1) * P], ident[:])
                            ins.then_inc(mm_done, M.add(mm_done, (ln, "T", n, c)))
                        continue
                    if kind == "R":
                        if tag == "L1sa":
                            pe.wait_ge(slot_loaded[3], upto(slot_loaded[3], "tp"))
                        for row, terms in ROWS_OF[tag]:
                            b, banks = small()
                            _, act_was, dve_was = take(("row", row), dve=("grow", tag) if row != tag else ("row", row), banks=banks)
                            pe.wait_ge(act_done, upto(act_done, "scond", *act_was))
                            pe.wait_ge(dve_done, upto(dve_done, *dve_was))
                            for i, (a, r) in enumerate(terms):
                                ins = mm(ps[:, b, 0:D], a, r, i == 0, i == len(terms) - 1)
                            ins.then_inc(mm_done, M.add(mm_done, ("row", row)))
                        continue
                    if kind == "mod" and tag == "L2sa":
                        b, banks = small()
                        _, act_was, dve_was = take(name, dve=name, banks=banks)
                        pe.wait_ge(act_done, upto(act_done, "scond", *act_was))
                        pe.wait_ge(dve_done, upto(dve_done, *dve_was))
                        pe.wait_ge(slot_loaded[4], upto(slot_loaded[4], "L2"))
                        for m in (0, 1, 2, 3, 6, 7, 8, 9):
                            for k in range(KC):
                                ins = mm(ps[:, b, m:m + 1], adw[:, k, m * P:(m + 1) * P], scond[:, k:k + 1], k == 0, k == KC - 1)
                    elif kind == "mod":
                        b, banks = small()
                        _, act_was, dve_was = take(name, dve=name, banks=banks)
                        pe.wait_ge(act_done, upto(act_done, *act_was))
                        pe.wait_ge(dve_done, upto(dve_done, *dve_was))
                        pe.wait_ge(slot_loaded[1], upto(slot_loaded[1], "L3ss"))
                        for i in range(2):
                            for m in range(4):
                                for k in range(KC):
                                    ins = mm(ps[:, b, 4 * i + m:4 * i + m + 1], w256(1, 2 * i, 512)[:, k, m * P:(m + 1) * P],
                                             scond[:, k:k + 1], k == 0, k == KC - 1)
                    elif kind == "cT":
                        b, banks = small()
                        _, act_was, dve_was = take(name, act="kvT", banks=banks)
                        pe.wait_ge(act_done, upto(act_done, *act_was))
                        pe.wait_ge(dve_done, upto(dve_done, "ctxn", *dve_was))
                        for c in range(KC):
                            ins = pe.transpose(ps[:, b, c * S:(c + 1) * S], ctxk[:, c * P:(c + 1) * P], ident[0:S, 0:S])
                    elif kind == "P":
                        which, c, n = step[1:]
                        w, rows_in, kn = (wq, hT, HALF) if which == "q" else (wk, src, SP_ if cross else HALF)
                        b, act_was, dve_was = take(name, act=name, banks=single())
                        needed = [(ln, "hT", n, k) for k in range(KC)] if which == "q" or not cross else ["kvT"] * (tag == "L3ca")
                        pe.wait_ge(act_done, upto(act_done, *needed, *act_was))
                        pe.wait_ge(dve_done, upto(dve_done, *dve_was))
                        for k in range(KC):
                            ins = mm(ps[:, b, 0:kn], w[:, k, c * P:(c + 1) * P], rows_in[:, k, n * HALF:n * HALF + kn], k == 0, k == KC - 1)
                    elif kind == "V":
                        t2 = step[1]
                        b, act_was, dve_was = take(name, act=name, banks=single())
                        pe.wait_ge(act_done, upto(act_done, *((ln, "hT", t2 // 2, k) for k in range(KC)), *act_was))
                        pe.wait_ge(dve_done, upto(dve_done, *dve_was))
                        for i in range(1 if cross else 2):
                            t = 2 * t2 + i
                            for k in range(KC):
                                ins = mm(ps[0:kw, b, i * D:(i + 1) * D], src[:, k, t * P:t * P + kw], wv[:, k, :], k == 0, k == KC - 1)
                    elif kind == "K":
                        who, which, pair, n = step[1:]
                        hi, lo = (qh, ql) if which == "q" else (kh, kl)
                        c, pp = divmod(pair, PAIRS // KC)
                        kn = SP_ if cross and which == "k" else HALF
                        part = slice(n * HALF, n * HALF + kn)
                        b, act_was, dve_was = take(name, banks=single(), **{who: name})
                        pe.wait_ge(act_done, upto(act_done, *act_was))
                        pe.wait_ge(dve_done, upto(dve_done, *dve_was))
                        pe.wait_ge(pool_done, upto(pool_done, (tag, "P", which, c, n)))
                        s = SEL[which] + pp
                        mm(ps[:, b, 0:kn], sel[:, s, :], hi[:, c, part], True, False)
                        masked = tag == "L1ca" and which == "k"
                        ins = mm(ps[:, b, 0:kn], sel[:, s + PAIRS // KC, :], lo[:, c, part], False, not masked)
                        if masked:
                            pe.wait_ge(dve_done, upto(dve_done, "mrowb"))
                            ins = mm(ps[:, b, 0:kn], sel[0:1, NSEL, :], mrowb[:], False, True)
                    elif kind == "A":
                        g, n, t, j = step[1:]
                        a, banks = small()
                        _, act_was, dve_was = take(name, dve=name, banks=banks)
                        pe.wait_ge(act_done, upto(act_done, *stacks_for(tag, "act", g, n), *act_was))
                        pe.wait_ge(dve_done, upto(dve_done, *stacks_for(tag, "dve", g, n), *dve_was))
                        tt = slice((TPH * n + t) * P, (TPH * n + t + 1) * P)
                        if cross:
                            for pair in (2 * g, 2 * g + 1):
                                o = pair % 2 * 2 * SP_
                                ins = mm(ps[:, a, o:o + 2 * SP_], qs[:, pair, tt], kz[:, pair])
                        else:
                            h = GH * g + j
                            r = stacked(h % 2, 0, STACK)
                            for i in range(2):
                                ins = mm(ps[:, a + i, :], qs[r, h // 2, tt], ks[r, h // 2, i * HALF:(i + 1) * HALF])
                    elif kind == "M":
                        g, n = step[1:]
                        z, w, _, _ = maxima_of(tag, g, n)
                        a, banks = small()
                        _, act_was, dve_was = take(name, act=name, banks=banks)
                        pe.wait_ge(act_done, upto(act_done, *act_was))
                        last = ("A", GROUPS - 1, n, TPH - 1, 0) if cross else ("A", g, n, TPH - 1, GH - 1)
                        pe.wait_ge(dve_done, upto(dve_done, (tag,) + last, *dve_was))
                        for t in range(TPH):
                            ins = pe.transpose(ps[0:w, a, t * P:(t + 1) * P], mx[:, z, t, 0:w], ident[:])
                    elif kind == "S":
                        g, n, kt, j = step[1:]
                        if (kt, j) == (0, 0):
                            pe.wait_ge(maxima_stacked[g][n], upto(maxima_stacked[g][n], (tag, GH - 1)))
                        if cross:
                            b = 2 + 2 * (rings["wide"] % 2)
                            rings["wide"] += 1
                            _, act_was, dve_was = take(name, act=name, banks=(b, b + 1))
                        else:
                            b, act_was, dve_was = take(name, act=name, banks=single())
                        pe.wait_ge(act_done, upto(act_done, *act_was))
                        pe.wait_ge(dve_done, upto(dve_done, *dve_was))
                        h = GH * g + j
                        half = slice(n * HALF, (n + 1) * HALF)
                        if cross:
                            for e in range(2):
                                ins = mm(ps[0:kw, b + e, :], kz[:, h // 2, e, 0:kw], qs[:, h // 2, half])
                        else:
                            r = stacked(h % 2, 0, STACK)
                            ins = mm(ps[:, b, :], ks[r, h // 2, kt * P:(kt + 1) * P], qs[r, h // 2, half])
                    elif kind == "PV":
                        g, n, kt = step[1:]
                        u = buffer_of(name)
                        b, act_was = 7, []
                        if cross:
                            b, act_was, dve_was = take(name, dve=(tag, "O", g, n), banks=(6 + u % 2,))
                            pe.wait_ge(dve_done, upto(dve_done, *dve_was))
                        elif kt == 0:
                            _, act_was, dve_was = take(name, act=(tag, "O", g, n), banks=(7,))
                            pe.wait_ge(dve_done, upto(dve_done, *dve_was))
                        pe.wait_ge(act_done, upto(act_done, (tag, "S", g, n, kt, GH - (2 if cross else 1)), (tag, "V", 0 if cross else kt // 2), *act_was))
                        for j in range(GH):
                            ins = mm(ps[32 * j:32 * j + 32, b, :], v[0:kw, kt, GH * g + j, :],
                                     probs[0:kw, u, j, :], kt == 0, cross or kt == NT - 1)
                    elif kind == "OT":
                        g, n = step[1:]
                        a, banks = small()
                        _, act_was, dve_was = take(name, dve=(tag, "tok", g, n), banks=banks)
                        pe.wait_ge(act_done, upto(act_done, *[(tag, "O", g, n)] * (not cross), *act_was))
                        pe.wait_ge(dve_done, upto(dve_done, *[(tag, "O", g, n)] * cross, *dve_was))
                        for i in range(TPH):
                            o = (g % 2 if cross else n) * HALF + i * P
                            ins = pe.transpose(ps[:, a, i * P:(i + 1) * P], ow[:, o:o + P], ident[:])
                    elif kind == "aT":
                        n, c = step[1:]
                        a, banks = small()
                        _, act_was, dve_was = take(name, act=name, banks=banks)
                        pe.wait_ge(act_done, upto(act_done, *act_was))
                        pe.wait_ge(dve_done, upto(dve_done, *((tag, "tok", g, n) for g in range(GROUPS)), *dve_was))
                        for i in range(TPH):
                            ins = pe.transpose(ps[:, a, i * P:(i + 1) * P], tok[:, TPH * n + i, c * P:(c + 1) * P], ident[:])
                    elif kind == "up":
                        n, m = step[1:]
                        b, act_was, dve_was = take(name, act=name, banks=single())
                        pe.wait_ge(act_done, upto(act_done, *((ln, "hT", n, c) for c in range(KC)), *act_was))
                        pe.wait_ge(dve_done, upto(dve_done, *dve_was))
                        pe.wait_ge(pool_done, upto(pool_done, (tag, "split", "W1"), *((ln, "lo", n, c) for c in range(KC))))
                        products = [(w[:, k, m * P:(m + 1) * P], h[:, k, n * HALF:(n + 1) * HALF])
                                    for k in range(KC) for w, h in ((W1h, hTh), (W1h, hTl), (W1l, hTh))]
                        for i, (w, h) in enumerate(products):
                            ins = mm(ps[:, b, :], w, h, i == 0, i == len(products) - 1)
                    elif kind == "o":
                        t2 = step[1]
                        a, banks = small()
                        _, act_was, dve_was = take(name, dve=(tag, "x", t2), banks=banks)
                        if KIND[tag] == "mlp":
                            pe.wait_ge(act_done, upto(act_done, *act_was))
                            pe.wait_ge(pool_done, upto(pool_done, (tag, "split", "W2"), (tag, "up", t2 // 2, FM - 1)))
                        else:
                            pe.wait_ge(act_done, upto(act_done, *((tag, "aT", t2 // 2, c) for c in range(KC)), *act_was))
                        pe.wait_ge(dve_done, upto(dve_done, *dve_was))
                        for i in range(2):
                            t = 2 * t2 + i
                            o = (t % TPH) * P
                            if KIND[tag] == "mlp":
                                products = [(h[:, t2 // 2, m, o:o + P], w[:, m, :])
                                            for m in range(FM) for h, w in ((hidh, W2h), (hidl, W2h), (hidh, W2l))]
                                for m, (h, w) in enumerate(products):
                                    ins = mm(ps[:, a, i * D:(i + 1) * D], h, w, m == 0, m == len(products) - 1)
                            else:
                                for k in range(KC):
                                    ins = mm(ps[:, a, i * D:(i + 1) * D], hT[:, k, t * P:(t + 1) * P], wo[:, k, :], k == 0, k == KC - 1)
                    ins.then_inc(mm_done, M.add(mm_done, name))
            M.close("blocks")

        @block.scalar
        def _(act):
            def load_tokens(it):
                act.dma_start(xin[:], T["x"][it].rearrange("(t p) d -> p t d", p=P)).then_inc(xin_loaded, M.add(xin_loaded, None, LOADED))

            def load_conditions(it, loop):
                act.dma_start(ctxT[:], T["ctxT"][it].rearrange("(c p) s -> p c s", p=P)
                              ).then_inc(conditions_loaded, M.add(conditions_loaded, None, LOADED))
                act.dma_start(cond[:], T["condT"][it]).then_inc(conditions_loaded, M.add(conditions_loaded, loop, LOADED))

            def affine(upto, tag, gain, shift, n):
                for c in range(KC):
                    act.wait_ge(mm_done, upto(mm_done, (tag, "T", n, c)))
                    src, dst = ps[:, M.where((tag, "T", n, c)), :], hT[:, c, n * HALF:(n + 1) * HALF]
                    if gain is None:
                        ins = act.activation(dst, src, ACT.Copy)
                    else:
                        ins = act.activation(dst, src, ACT.Identity, bias=shift(c), scale=gain(c))
                    ins.then_inc(act_done, M.add(act_done, (tag, "hT", n, c)))

            def affine_split(upto, tag, gain, shift, n):
                half = slice(n * HALF, (n + 1) * HALF)
                for c in range(KC):
                    act.wait_ge(mm_done, upto(mm_done, (tag, "T", n, c)))
                    act.activation(hTh[:, c, half], ps[:, M.where((tag, "T", n, c)), :], ACT.Identity, bias=shift(c), scale=gain(c))
                for c in range(KC):
                    act.activation(whole[:, KC * n + c, :], ps[:, M.where((tag, "T", n, c)), :], ACT.Identity, bias=shift(c),
                                   scale=gain(c)).then_inc(act_done, M.add(act_done, (tag, "hT", n, c)))

            load_tokens(0)
            load_conditions(0, "first")
            act.wait_ge(constants_loaded, 6 * LOADED)
            act.activation(small[:, 127:128], cols[:, 0:1], ACT.Copy).then_inc(act_done, M.add(act_done))
            M.open("experts")
            with act.Fori(0, B) as it:
                def upto(sem, *steps):
                    return M.upto("experts", it, sem, steps)

                act.dma_start(x[:], T["x"][it].rearrange("(t p) d -> p t d", p=P)).then_inc(residual_loaded, M.add(residual_loaded, "x", LOADED))
                act.wait_ge(mm_done, upto(mm_done, ("L0", "kv")))
                b = M.where(("L0", "kv"))
                act.activation(kv0T[:], ps[:, b, 0:2 * KC * SP_].rearrange("p (c s) -> p c s", s=SP_), ACT.Copy
                               ).then_inc(act_done, M.add(act_done, ("L0", "kv")))
                act.wait_ge(mm_done, upto(mm_done, ("L0", "a")))
                b = M.where(("L0", "a"))
                act.activation(a0[:, :, 0:SP_], ps[:, b, 0:KC * SP_].rearrange("p (c s) -> p c s", s=SP_), ACT.Copy, scale=D ** -0.5
                               ).then_inc(act_done, M.add(act_done, ("L0", "a")))
                for n in range(NH):
                    affine_split(upto, "ln0", lambda c: col("L0_ln_gamma", c), lambda c: col("L0_ln_beta", c), n)
                for n in range(NH):
                    b = M.where(("L0", "s", n))
                    act.wait_ge(dve_done, upto(dve_done, ("L0", "nmx", n)))
                    for i in range(TPH):
                        t = TPH * n + i
                        act.activation(e01[n][:, i, 0:S], ps[:, b, i * SW:i * SW + S], ACT.Exp, bias=nmx[:, t:t + 1],
                                       accum_out=es[:, t:t + 1]).then_inc(act_done, M.add(act_done, ("L0", "e", n, i)))
                for n in range(NH):
                    act.wait_ge(mm_done, upto(mm_done, ("L0", "wT", n)))
                    act.activation(wT[0:S, n * HALF:(n + 1) * HALF], ps[0:S, M.where(("L0", "wT", n)), :], ACT.Copy
                                   ).then_inc(act_done, M.add(act_done, ("L0", "wT", n)))
                act.wait_ge(dve_done, upto(dve_done, ("L0", "lg", NH - 1)))
                act.activation(lg[:], lg[:], ACT.Exp).then_inc(act_done, M.add(act_done, ("L0", "le")))
                for n in range(NH):
                    half = slice(n * HALF, (n + 1) * HALF)
                    for m in range(RM + GM):
                        act.wait_ge(mm_done, upto(mm_done, ("L0", "h", n, m)))
                        act.activation(hid0[:, m, :], ps[:, M.where(("L0", "h", n, m)), :], ACT.Silu, bias=col("L0_e_b1", m)
                                       ).then_inc(act_done, M.add(act_done, ("L0", "h", n, m)))
                        if m // 4 == 2 and m % 4 < E:
                            e = m % 4
                            act.wait_ge(mm_done, upto(mm_done, ("L0", "pb", n, e)))
                            if n:
                                act.wait_ge(dve_done, upto(dve_done, ("L0", "hp", n - 1, RM - 1)))
                            else:
                                act.wait_ge(pool_done, upto(pool_done, ("ln0", "lo", NH - 1, KC - 1)))
                            act.activation(pb[:, e, :], ps[:, M.where(("L0", "pb", n, e)), :], ACT.Copy
                                           ).then_inc(act_done, M.add(act_done, ("L0", "pb", n, e)))
                    act.wait_ge(mm_done, upto(mm_done, ("L0", "pT", n)))
                    act.activation(pT[:, half], ps[0:E, M.where(("L0", "pT", n)), :], ACT.Copy
                                   ).then_inc(act_done, M.add(act_done, ("L0", "pT", n)))
                    for i2 in range(2):
                        t2 = 2 * n + i2
                        act.wait_ge(mm_done, upto(mm_done, ("L0", "g", t2)))
                        if n:
                            act.wait_ge(dve_done, upto(dve_done, ("L0", "x", t2 - 2)))
                        act.activation(sg[:, i2], ps[:, M.where(("L0", "g", t2)), :].rearrange("p (i d) -> p i d", i=2),
                                       ACT.Tanh, scale=0.5).then_inc(act_done, M.add(act_done, ("L0", "g", t2)))
                    if n == 0:
                        act.wait_ge(dve_done, upto(dve_done, ("ln0", "xh", NT - 1)))
                        load_tokens(it + 1)
                        load_conditions(it + 1, "experts")
                    for c in range(KC):
                        act.wait_ge(mm_done, upto(mm_done, ("L0", "rt", n, c)))
                        act.activation(rT[:, c, :], ps[:, M.where(("L0", "rt", n, c)), :], ACT.Copy
                                       ).then_inc(act_done, M.add(act_done, ("L0", "rt", n, c)))
                for t2 in range(4):
                    act.wait_ge(dve_done, upto(dve_done, ("L0", "x", t2)))
                    act.dma_start(T["x0"][it].rearrange("(t p) d -> p t d", p=P)[:, 2 * t2:2 * t2 + 2, :],
                                  x[:, 2 * t2:2 * t2 + 2, :]).then_inc(x_stored, M.add(x_stored, t2, LOADED))
                act.wait_ge(x_stored, upto(x_stored, 3))
            M.close("experts")

            act.wait_ge(x_stored, 4 * LOADED)
            act.wait_ge(xin_loaded, (B + 1) * LOADED)
            act.dma_start(xin[:], T["x0"][0].rearrange("(t p) d -> p t d", p=P)).then_inc(xin_loaded, M.add(xin_loaded, None, LOADED))
            for t2 in range(4):
                act.dma_start(T["x0"][B].rearrange("(t p) d -> p t d", p=P)[:, 2 * t2:2 * t2 + 2, :],
                              x[:, 2 * t2:2 * t2 + 2, :]).then_inc(out_stored[t2], M.add(out_stored[t2], None, LOADED))
            for t2 in range(4):
                act.wait_ge(out_stored[t2], LOADED)
            GAIN = {"ln1": lambda c: col("L1_ln1_g", c), "ln3": lambda c: col("L1_ln3_g", c), "ln2": lambda c: col("L1_ln2_g", c),
                    "ln4": lambda c: mod[:, 2 + c:3 + c], "ln5": None, "ln6": lambda c: mod[:, 8 + c:9 + c],
                    "ln7": lambda c: mod3[:, c:c + 1]}
            SHIFT = {"ln1": lambda c: col("L1_ln1_b", c), "ln3": lambda c: col("L1_ln3_b", c), "ln2": lambda c: col("L1_ln2_b", c),
                     "ln4": lambda c: mod[:, c:c + 1], "ln5": None, "ln6": lambda c: mod[:, 6 + c:7 + c],
                     "ln7": lambda c: mod3[:, 2 + c:3 + c]}
            GELU = {"L1mlp": (ACT.Gelu, "L1_b1"), "L2mlp": (ACT.Gelu_apprx_tanh, "L2_fc1_b")}
            M.open("blocks")
            with act.Fori(0, B) as it:
                def upto(sem, *steps):
                    return M.upto("blocks", it, sem, steps)

                for name in PASS:
                    tag, step = name[0], name[1:]
                    kind, cross, ln = step[0], KIND[tag] == "cross", LN_OF[tag]
                    kw = S if cross else P
                    if tag in ATT:
                        bq, bk, bv = ATT[tag][5:]
                    if kind == "begin" and step[1] == 0:
                        load_conditions(it, "blocks")
                        act.dma_start(mi[:], T["mask"][it]).then_inc(conditions_loaded, M.add(conditions_loaded, None, LOADED))
                        act.dma_start(mic[:], T["maskT"][it]).then_inc(conditions_loaded, M.add(conditions_loaded, None, LOADED))
                        act.dma_start(ctxk[:], T["ctx"][it]).then_inc(conditions_loaded, M.add(conditions_loaded, "all", LOADED))
                    elif kind == "T":
                        if step[1] == 0 and ln in ("ln4", "ln7"):
                            act.wait_ge(dve_done, upto(dve_done, (tag, "mod")))
                        if KIND[tag] == "mlp":
                            affine_split(upto, ln, GAIN[ln], SHIFT[ln], step[1])
                        else:
                            affine(upto, ln, GAIN[ln], SHIFT[ln], step[1])
                        if (tag, step[1]) == ("L2mlp", 1):
                            act.wait_ge(mm_done, upto(mm_done, ("row", "L2mlp_g")))
                            act.dma_start(xin[:], T["x0"][it + 1].rearrange("(t p) d -> p t d", p=P)
                                          ).then_inc(xin_loaded, M.add(xin_loaded, "next", LOADED))
                    elif kind == "R" and tag == "L1sa":
                        act.wait_ge(conditions_loaded, upto(conditions_loaded, "all"))
                        act.activation(scond[:], cond[:], ACT.Silu).then_inc(act_done, M.add(act_done, "scond"))
                    elif kind == "cT":
                        act.wait_ge(mm_done, upto(mm_done, name))
                        act.wait_ge(dve_done, upto(dve_done, (tag, "mod")))
                        b = M.where(name)
                        for c in range(KC):
                            act.activation(kvT[:, c, 0:S], ps[:, b, c * S:(c + 1) * S], ACT.Identity, bias=mod3[:, 6 + c:7 + c],
                                           scale=mod3[:, 4 + c:5 + c]).then_inc(act_done, M.add(act_done, ("kvT", c)))
                            act.activation(kvT[:, c, S:SP_], ps[:, b, (c + 1) * S - 1:(c + 1) * S], ACT.Identity, bias=mod3[:, 6 + c:7 + c],
                                           scale=mod3[:, 4 + c:5 + c]).then_inc(act_done, M.add(act_done, "kvT" if c == KC - 1 else ("kvT2", c)))
                    elif kind == "P":
                        which, c, n = step[1:]
                        hi, bias, kn = (qh, bq, HALF) if which == "q" else (kh, bk, SP_ if cross else HALF)
                        w, used = whole_of(name)
                        act.wait_ge(mm_done, upto(mm_done, name))
                        act.activation(hi[:, c, n * HALF:n * HALF + kn], ps[:, M.where(name), 0:kn], ACT.Identity, bias=col(bias[0], bias[1] + c))
                        if used:
                            act.wait_ge(pool_done, upto(pool_done, used))
                        act.activation(whole[:, w, 0:kn], ps[:, M.where(name), 0:kn], ACT.Identity,
                                       bias=col(bias[0], bias[1] + c)).then_inc(act_done, M.add(act_done, name))
                    elif kind == "V":
                        t2, i = step[1], 1 if cross else 2
                        src = ps[0:kw, M.where(name), 0:i * D].rearrange("p (i h d) -> p i h d", i=i, d=HD)
                        act.wait_ge(mm_done, upto(mm_done, name))
                        act.activation(v[0:kw, 2 * t2:2 * t2 + i, :, 0:HD], src, ACT.Copy).then_inc(act_done, M.add(act_done, name))
                    elif kind == "K" and step[1] == "act":
                        which, pair, n = step[2:]
                        act.wait_ge(mm_done, upto(mm_done, name))
                        if which == "q":
                            act.activation(qs[:, pair, n * HALF:(n + 1) * HALF], ps[:, M.where(name), :], ACT.Identity,
                                           bias=qs_rows).then_inc(act_done, M.add(act_done, name))
                        else:
                            act.activation(ks[:, pair, n * HALF:(n + 1) * HALF], ps[:, M.where(name), :], ACT.Identity,
                                           bias=ks_rows).then_inc(act_done, M.add(act_done, name))
                    elif kind == "M":
                        g, n = step[1:]
                        z, w, _, _ = maxima_of(tag, g, n)
                        act.wait_ge(mm_done, upto(mm_done, name))
                        if not cross and NH * g + n >= 2:
                            act.wait_ge(maxima_stacked[g - 1][n], upto(maxima_stacked[g - 1][n], (tag, GH - 1)))
                        act.activation(mrow[0:w, z * HALF:(z + 1) * HALF], ps[0:w, M.where(name), :], ACT.Copy
                                       ).then_inc(act_done, M.add(act_done, name))
                    elif kind == "S":
                        g, n, kt, j = step[1:]
                        u = UNITS[tag].index((tag, "PV", g, n, kt))
                        act.wait_ge(mm_done, upto(mm_done, name, *UNITS[tag][max(u - 4, 0):max(u - 3, 0)]))
                        if cross:
                            src, dst = ps[0:kw, M.where(name):M.where(name) + 2, :], probs[0:kw, u % 4, j:j + 2, :]
                        else:
                            src, dst = ps[:, M.where(name), :], probs[:, u % 4, j, :]
                        if tag == "L1ca":
                            if (u, j) == (0, 0):
                                act.wait_ge(dve_done, upto(dve_done, "mcolb"))
                            ins = act.activation(dst, src, ACT.Exp, bias=mcolb[:], scale=SCALE)
                        else:
                            ins = act.activation(dst, src, ACT.Exp, scale=SCALE)
                        ins.then_inc(act_done, M.add(act_done, name))
                    elif kind == "O" and not cross:
                        g, n = step[1:]
                        act.wait_ge(mm_done, upto(mm_done, (tag, "PV", g, n, NT - 1), *[(tag, "OT", g - 1, n)] * (g > 0)))
                        act.activation(ow[:, n * HALF:(n + 1) * HALF], ps[:, 7, :], ACT.Copy).then_inc(act_done, M.add(act_done, name))
                    elif kind == "aT":
                        n, c = step[1:]
                        act.wait_ge(mm_done, upto(mm_done, name))
                        act.activation(hT[:, c, n * HALF:(n + 1) * HALF], ps[:, M.where(name), :], ACT.Identity,
                                       bias=col(bv[0], bv[1] + c)).then_inc(act_done, M.add(act_done, name))
                    elif kind == "up":
                        n, m = step[1:]
                        func, bias = GELU[tag]
                        act.wait_ge(mm_done, upto(mm_done, name))
                        act.activation(hidh[:, n, m, :], ps[:, M.where(name), :], func, bias=col(bias, m))
                        act.activation(hid[:, n, m, :], ps[:, M.where(name), :], func, bias=col(bias, m)
                                       ).then_inc(act_done, M.add(act_done, name))
                    elif kind == "out":
                        t2 = step[1]
                        act.wait_ge(dve_done, upto(dve_done, (tag, "x", t2)))
                        act.dma_start(T["out"][it].rearrange("(t p) d -> p t d", p=P)[:, 2 * t2:2 * t2 + 2, :],
                                      x[:, 2 * t2:2 * t2 + 2, :]).then_inc(out_stored[t2], M.add(out_stored[t2], "out", LOADED))
            M.close("blocks")
            for t2 in range(4):
                act.wait_ge(out_stored[t2], (B + 1) * LOADED)
            act.wait_ge(xin_loaded, (2 * B + 2) * LOADED)

        @block.vector
        def _(dve):
            def stats(upto, tag, t, src):
                dve.bn_stats(st[:, t, :], src[:, t, :]).then_inc(dve_done, M.add(dve_done, (tag, "st", t)))

            def spread(upto, tag, h, eps):
                tt = slice(TPH * h, TPH * h + TPH)
                dve.wait_ge(dve_done, upto(dve_done, (tag, "st", TPH * h + TPH - 1)))
                dve.memset(ve[:, tt], 0.0)
                for t in range(TPH * h, TPH * h + TPH):
                    dve.bn_aggr(mv[:, t, :], st[:, t, :]).then_inc(dve_done, M.add(dve_done, (tag, "ag", t)))
                dve.wait_ge(dve_done, upto(dve_done, (tag, "ag", TPH * h + TPH - 1)))
                dve.tensor_scalar(ve[:, tt], mv[:, tt, 1], eps, None, ALU.add).then_inc(dve_done, M.add(dve_done, (tag, "ve", h)))

            def normalise(upto, tag, h, src):
                dve.wait_ge(pool_done, upto(pool_done, (tag, "rstd", h)))
                for t in range(TPH * h, TPH * h + TPH):
                    dve.tensor_scalar(tok[:, t, :], src[:, t, :], mv[:, t, 0:1], rstd[:, t:t + 1], ALU.subtract, ALU.mult
                                      ).then_inc(dve_done, M.add(dve_done, (tag, "xh", t)))

            dve.memset(nhalf, -0.5)
            dve.memset(zero, 0.0)
            dve.wait_ge(constants_loaded, 6 * LOADED)
            dve.tensor_copy(a0[:, :, SP_:], router[:, 0:KC, :])
            dve.tensor_copy(sel[:], sel_in[:]).then_inc(dve_done, M.add(dve_done))
            dve.wait_ge(dve_done, 1)
            M.open("experts")
            with dve.Fori(0, B) as it:
                def upto(sem, *steps):
                    return M.upto("experts", it, sem, steps)

                dve.wait_ge(xin_loaded, upto(xin_loaded))
                for h in range(NH):
                    for t in range(TPH * h, TPH * h + TPH):
                        stats(upto, "ln0", t, xin)
                    spread(upto, "ln0", h, 1e-5)
                for h in range(NH):
                    normalise(upto, "ln0", h, xin)
                for n in range(NH):
                    tt = slice(TPH * n, TPH * n + TPH)
                    both = ps[:, M.where(("L0", "s", n)), 0:TPH * SW].rearrange("p (t s) -> p t s", s=SW)
                    dve.wait_ge(mm_done, upto(mm_done, ("L0", "s", n)))
                    dve.tensor_copy(lg[:, tt], both[:, :, SP_:]).then_inc(dve_done, M.add(dve_done, ("L0", "lt0", n)))
                    dve.tensor_reduce(nmx[:, tt], both[:, :, 0:S], AX.X, ALU.max, negate=True).then_inc(dve_done, M.add(dve_done, ("L0", "nmx", n)))
                for n in range(NH):
                    tt = slice(TPH * n, TPH * n + TPH)
                    dve.wait_ge(act_done, upto(act_done, ("L0", "e", n, TPH - 1)))
                    dve.reciprocal(rc4[:, tt], es[:, tt]).then_inc(dve_done, M.add(dve_done, ("L0", "rc4", n)))
                    dve.wait_ge(dve_done, upto(dve_done, ("L0", "rc4", n)))
                    dve.tensor_tensor(e01[n][:, :, 0:S], e01[n][:, :, 0:S], rc4[:, tt].unsqueeze(2).to_broadcast([P, TPH, S]), ALU.mult
                                      ).then_inc(dve_done, M.add(dve_done, ("L0", "w", n)))
                for e in range(E + 1):
                    w = RH if e < E else D + E
                    dve.wait_ge(mm_done, upto(mm_done, ("L0", "u", e)))
                    dve.tensor_copy(u0[0:S, e * RH:e * RH + w], ps[0:S, M.where(("L0", "u", e)), 0:w]
                                    ).then_inc(dve_done, M.add(dve_done, ("L0", "u", e)))
                for n in range(NH):
                    tt = slice(TPH * n, TPH * n + TPH)
                    src = ps[:, M.where(("L0", "r", n)), 0:TPH * E].rearrange("p (t e) -> p t e", e=E)
                    dve.wait_ge(mm_done, upto(mm_done, ("L0", "r", n)))
                    dve.tensor_tensor(lg[:, tt], lg[:, tt], src, ALU.add).then_inc(dve_done, M.add(dve_done, ("L0", "lt", n)))
                    dve.wait_ge(dve_done, upto(dve_done, ("L0", "lt", n)))
                    dve.tensor_reduce(rmx[:, tt], lg[:, tt], AX.X, ALU.max, negate=True).then_inc(dve_done, M.add(dve_done, ("L0", "rmx", n)))
                    dve.wait_ge(dve_done, upto(dve_done, ("L0", "rmx", n)))
                    dve.tensor_tensor(lg[:, tt], lg[:, tt], rmx[:, tt].unsqueeze(2).to_broadcast([P, TPH, E]), ALU.add
                                      ).then_inc(dve_done, M.add(dve_done, ("L0", "lg", n)))
                dve.wait_ge(act_done, upto(act_done, ("L0", "le")))
                dve.tensor_reduce(rs[:], lg[:], AX.X, ALU.add).then_inc(dve_done, M.add(dve_done, ("L0", "rs")))
                dve.wait_ge(dve_done, upto(dve_done, ("L0", "rs")))
                dve.reciprocal(rrs[:], rs[:]).then_inc(dve_done, M.add(dve_done, ("L0", "rrs")))
                dve.wait_ge(dve_done, upto(dve_done, ("L0", "rrs")))
                dve.tensor_tensor(lg[:], lg[:], rrs[:].unsqueeze(2).to_broadcast([P, NT, E]), ALU.mult
                                  ).then_inc(dve_done, M.add(dve_done, ("L0", "p")))
                for n in range(NH):
                    for m in range(RM):
                        dve.wait_ge(act_done, upto(act_done, ("L0", "pb", n, m // 4), ("L0", "h", n, m)))
                        dve.tensor_tensor(hid0[:, m, :], hid0[:, m, :], pb[:, m // 4, :], ALU.mult
                                          ).then_inc(dve_done, M.add(dve_done, ("L0", "hp", n, m)))
                    for i2 in range(2):
                        t2 = 2 * n + i2
                        xx = x[:, 2 * t2:2 * t2 + 2, :]
                        o = ps[:, M.where(("L0", "o", t2)), :].rearrange("p (i d) -> p i d", i=2)
                        dve.wait_ge(mm_done, upto(mm_done, ("L0", "o", t2)))
                        dve.wait_ge(act_done, upto(act_done, ("L0", "g", t2)))
                        dve.scalar_tensor_tensor(sg[:, i2], sg[:, i2], 1.0, o, ALU.add, ALU.mult
                                                 ).then_inc(dve_done, M.add(dve_done, ("L0", "sg", t2)))
                        dve.wait_ge(dve_done, upto(dve_done, ("L0", "sg", t2)))
                        if t2 == 0:
                            dve.wait_ge(residual_loaded, upto(residual_loaded, "x"))
                        dve.scalar_tensor_tensor(xx, sg[:, i2], 0.5, xx, ALU.mult, ALU.add
                                                 ).then_inc(dve_done, M.add(dve_done, ("L0", "x", t2)))
            M.close("experts")

            dve.memset(v[:], 1.0)
            M.open("blocks")
            with dve.Fori(0, B) as it:
                def upto(sem, *steps):
                    return M.upto("blocks", it, sem, steps)

                turned = []
                for name in PASS:
                    tag, step = name[0], name[1:]
                    kind, cross, ln = step[0], KIND[tag] == "cross", LN_OF[tag]
                    if kind == "begin":
                        n = step[1]
                        if n == 0:
                            dve.wait_ge(xin_loaded, upto(xin_loaded))
                        for t in range(TPH * n, TPH * n + TPH):
                            stats(upto, ln, t, xin)
                        spread(upto, ln, n, EPS[ln])
                    elif kind == "N":
                        normalise(upto, ln, step[1], xin if tag == "L1sa" else x)
                    elif kind == "R":
                        if tag in GATED:
                            dve.wait_ge(mm_done, upto(mm_done, ("row", tag + "_g")))
                            dve.tensor_copy(grow[:], ps[:, M.where(("row", tag + "_g")), 0:D]).then_inc(dve_done, M.add(dve_done, ("grow", tag)))
                            dve.wait_ge(mm_done, upto(mm_done, ("row", tag)))
                            dve.wait_ge(dve_done, upto(dve_done, ("grow", tag)))
                            dve.tensor_tensor(rrow[:], grow[:], ps[:, M.where(("row", tag)), 0:D], ALU.mult
                                              ).then_inc(dve_done, M.add(dve_done, ("row", tag)))
                        else:
                            dve.wait_ge(mm_done, upto(mm_done, ("row", tag)))
                            dve.tensor_copy(rrow[:], ps[:, M.where(("row", tag)), 0:D]).then_inc(dve_done, M.add(dve_done, ("row", tag)))
                        if tag == "L1sa":
                            dve.wait_ge(conditions_loaded, upto(conditions_loaded, "all"))
                            dve.tensor_scalar(mrowb[:], mi[:], 0.0, MASKED, ALU.is_equal, ALU.mult).then_inc(dve_done, M.add(dve_done, "mrowb"))
                            dve.tensor_scalar(mcolb[:], mic[:], 0.0, MASKED, ALU.is_equal, ALU.mult).then_inc(dve_done, M.add(dve_done, "mcolb"))
                    elif kind == "zero":
                        dve.memset(kz[:].bitcast(F32), 0.0).then_inc(dve_done, M.add(dve_done, name))
                    elif kind == "mod" and tag == "L2sa":
                        dve.wait_ge(mm_done, upto(mm_done, name))
                        b = M.where(name)
                        ab = COL["L2_adaln_b"]
                        for i in (0, 6):
                            dve.tensor_tensor(mod[:, i:i + 2], ps[:, b, i:i + 2], cols[:, ab + i:ab + i + 2], ALU.add
                                              ).then_inc(dve_done, M.add(dve_done, ("shift", i)))
                            dve.scalar_tensor_tensor(mod[:, i + 2:i + 4], ps[:, b, i + 2:i + 4], 1.0, cols[:, ab + i + 2:ab + i + 4], ALU.add, ALU.add
                                                     ).then_inc(dve_done, M.add(dve_done, name if i else ("scale", i)))
                    elif kind == "mod":
                        dve.wait_ge(mm_done, upto(mm_done, name))
                        b = M.where(name)
                        for i, bias in ((0, "L3_bss_q"), (4, "L3_bss_kv")):
                            cb = COL[bias]
                            dve.scalar_tensor_tensor(mod3[:, i:i + 2], ps[:, b, i:i + 2], 1.0, cols[:, cb:cb + 2], ALU.add, ALU.add
                                                     ).then_inc(dve_done, M.add(dve_done, ("scale3", i)))
                            dve.tensor_tensor(mod3[:, i + 2:i + 4], ps[:, b, i + 2:i + 4], cols[:, cb + 2:cb + 4], ALU.add
                                              ).then_inc(dve_done, M.add(dve_done, name if i else ("shift3", i)))
                    elif kind == "context":
                        dve.bn_stats(stc[:], ctxk[:]).then_inc(dve_done, M.add(dve_done, "stc"))
                        dve.wait_ge(dve_done, upto(dve_done, "stc"))
                        dve.memset(vec[:], 0.0)
                        dve.bn_aggr(mvc[:], stc[:]).then_inc(dve_done, M.add(dve_done, "agc"))
                        dve.wait_ge(dve_done, upto(dve_done, "agc"))
                        dve.tensor_scalar(vec[:], mvc[:, 1:2], 1e-5, None, ALU.add).then_inc(dve_done, M.add(dve_done, "vec"))
                        dve.wait_ge(pool_done, upto(pool_done, "rstdc"))
                        dve.tensor_scalar(ctxk[:], ctxk[:], mvc[:, 0:1], rstdc[:], ALU.subtract, ALU.mult).then_inc(dve_done, M.add(dve_done, "ctxn"))
                    elif kind == "o":
                        t2, follow = step[1], NEXT_LN.get(tag)
                        src = ps[:, M.where(name), :].rearrange("p (i d) -> p i d", i=2)
                        xx = x[:, 2 * t2:2 * t2 + 2, :]
                        dve.wait_ge(mm_done, upto(mm_done, name))
                        if tag in GATED:
                            tmp = tok[:, 2 * t2:2 * t2 + 2, :]
                            dve.tensor_tensor(tmp, src, grow[:].unsqueeze(1).to_broadcast([P, 2, D]), ALU.mult
                                              ).then_inc(dve_done, M.add(dve_done, (tag, "gx", t2)))
                            dve.wait_ge(dve_done, upto(dve_done, (tag, "gx", t2)))
                            src = tmp
                        dve.wait_ge(pool_done, upto(pool_done, ("row", tag)))
                        dve.tensor_tensor(xx, xx, src, ALU.add).then_inc(dve_done, M.add(dve_done, (tag, "x", t2)))
                        if follow:
                            dve.wait_ge(dve_done, upto(dve_done, (tag, "x", t2)))
                            stats(upto, follow, 2 * t2, x)
                            stats(upto, follow, 2 * t2 + 1, x)
                            if t2 % 2:
                                spread(upto, follow, t2 // 2, EPS[follow])
                    elif kind == "K" and step[1] == "dve":
                        pair, n = step[3:]
                        dve.wait_ge(mm_done, upto(mm_done, name))
                        if cross:
                            dve.wait_ge(dve_done, upto(dve_done, (tag, "zero")))
                            for e in range(2):
                                r = stacked(e, 0, STACK)
                                ins = dve.tensor_scalar(kz[r, pair, e, :], ps[r, M.where(name), 0:SP_], ks_rows[r], None, ALU.add)
                            ins.then_inc(dve_done, M.add(dve_done, name))
                        else:
                            dve.tensor_scalar(ks[:, pair, n * HALF:(n + 1) * HALF], ps[:, M.where(name), :], ks_rows, None, ALU.add
                                              ).then_inc(dve_done, M.add(dve_done, name))
                    elif kind == "A":
                        g, n, t, j = step[1:]
                        z, w, j0, turn_step = maxima_of(tag, g, n)
                        a = M.where(name)
                        if not cross and NH * g + n >= 2:
                            dve.wait_ge(mm_done, upto(mm_done, name, (tag, "M", g - 1, n)))
                        else:
                            dve.wait_ge(mm_done, upto(mm_done, name))
                        if cross:
                            dve.tensor_reduce(mx[:, z, t, j0:j0 + GH], ps[:, a, 0:GH * SP_].rearrange("p (j s) -> p j s", s=SP_), AX.X, ALU.max,
                                              negate=True).then_inc(dve_done, M.add(dve_done, name))
                        else:
                            dve.tensor_reduce(mx[:, z, t, j:j + 1], ps[:, a:a + 2, :], AX.XY, ALU.max, negate=True
                                              ).then_inc(dve_done, M.add(dve_done, name))
                    elif kind == "O" and cross:
                        g, n = step[1:]
                        dve.wait_ge(mm_done, upto(mm_done, (tag, "PV", g, n, 0), *[(tag, "OT", g - 2, n)] * (g > 1)))
                        dve.tensor_copy(ow[:, g % 2 * HALF:(g % 2 + 1) * HALF], ps[:, M.where((tag, "PV", g, n, 0)), :]
                                        ).then_inc(dve_done, M.add(dve_done, name))
                    elif kind == "OT":
                        g, n = step[1:]
                        o = ps[:, M.where(name), :].rearrange("p (t j d) -> p t j d", t=TPH, j=GH)
                        rcv = rc[:].rearrange("p (t j) -> p t j", j=GH)
                        dst = tok[:, TPH * n:TPH * n + TPH, GH * HD * g:GH * HD * (g + 1)].rearrange("p t (j d) -> p t j d", d=HD)
                        dve.wait_ge(mm_done, upto(mm_done, name))
                        if turned:
                            dve.wait_ge(dve_done, upto(dve_done, turned[-1]))
                        dve.reciprocal(rcv, o[:, :, :, HD]).then_inc(dve_done, M.add(dve_done, (tag, "rc", g, n)))
                        dve.wait_ge(dve_done, upto(dve_done, (tag, "rc", g, n)))
                        dve.tensor_tensor(dst, o[:, :, :, 0:HD], rcv.unsqueeze(3).to_broadcast([P, TPH, GH, HD]), ALU.mult
                                          ).then_inc(dve_done, M.add(dve_done, (tag, "tok", g, n)))
                        turned.append((tag, "tok", g, n))
            M.close("blocks")

        @block.gpsimd
        def _(pool):
            def rsqrt(upto, tag, h):
                tt = slice(TPH * h, TPH * h + TPH)
                pool.wait_ge(dve_done, upto(dve_done, (tag, "ve", h)))
                pool.tensor_tensor(rstd[:, tt], ve[:, tt], nhalf[:, tt], ALU.pow).then_inc(pool_done, M.add(pool_done, (tag, "rstd", h)))

            def split_tokens(upto, tag, lo, n):
                half = slice(n * HALF, (n + 1) * HALF)
                for c in range(KC):
                    pool.wait_ge(act_done, upto(act_done, (tag, "hT", n, c)))
                    pool.tensor_tensor(lo[:, c, half], whole[:, KC * n + c, :], hTh[:, c, half].bitcast(F32), ALU.subtract
                                       ).then_inc(pool_done, M.add(pool_done, (tag, "lo", n, c)))

            pool.wait_ge(dve_done, 1)
            pool.wait_ge(experts_loaded["tokens"], 3 * LOADED)
            parts = ((ew1h[:].rearrange("p c e r -> p (c e r)"), ew1l[:].rearrange("p c e r -> p (c e r)"),
                      ew1[:, 0:KC].rearrange("p c e r -> p (c e r)")),
                     (gw1h[:].rearrange("p c r -> p (c r)"), gw1l[:].rearrange("p c r -> p (c r)"), gw1[:, 0:KC].rearrange("p c r -> p (c r)")))
            for hi, lo, w in parts:
                pool.tensor_tensor(hi, w, zero.to_broadcast(w.shape), ALU.add).then_inc(pool_done, M.add(pool_done))
            pool.wait_ge(pool_done, len(parts))
            for hi, lo, w in parts:
                pool.tensor_tensor(lo, w, hi.bitcast(F32), ALU.subtract).then_inc(pool_done, M.add(pool_done))
            M.open("experts")
            with pool.Fori(0, B) as it:
                def upto(sem, *steps):
                    return M.upto("experts", it, sem, steps)

                rsqrt(upto, "ln0", 0)
                rsqrt(upto, "ln0", 1)
                for n in range(NH):
                    split_tokens(upto, "ln0", hTl0, n)
            M.close("experts")
            M.open("blocks")
            with pool.Fori(0, B) as it:
                def upto(sem, *steps):
                    return M.upto("blocks", it, sem, steps)

                for name in PASS:
                    tag, step = name[0], name[1:]
                    kind, cross, ln = step[0], KIND[tag] == "cross", LN_OF[tag]
                    if kind == "begin":
                        rsqrt(upto, ln, step[1])
                    elif kind == "o" and step[1] % 2 and tag in NEXT_LN:
                        rsqrt(upto, NEXT_LN[tag], step[1] // 2)
                    elif kind == "context":
                        pool.wait_ge(dve_done, upto(dve_done, "vec"))
                        pool.tensor_tensor(rstdc[:], vec[:], nhalf[0:S, 0:1], ALU.pow).then_inc(pool_done, M.add(pool_done, "rstdc"))
                    elif kind == "add":
                        if tag == "L1sa":
                            for t2 in range(4):
                                pool.wait_ge(out_stored[t2], upto(out_stored[t2]))
                        pool.wait_ge(dve_done, upto(dve_done, ("row", tag), (ln, "xh", NT - 1)))
                        pool.tensor_tensor(x[:], xin[:] if tag == "L1sa" else x[:], rrow[:].unsqueeze(1).to_broadcast([P, NT, D]), ALU.add
                                           ).then_inc(pool_done, M.add(pool_done, ("row", tag)))
                    elif kind == "T" and KIND[tag] == "mlp":
                        split_tokens(upto, ln, hTl, step[1])
                    elif kind == "up":
                        n, m = step[1:]
                        pool.wait_ge(act_done, upto(act_done, name))
                        pool.tensor_tensor(hidl[:, n, m, :], hid[:, n, m, :], hidh[:, n, m, :].bitcast(F32), ALU.subtract
                                           ).then_inc(pool_done, M.add(pool_done, name))
                    elif kind == "split":
                        w, hi, lo, loaded = (W1, W1h, W1l, slot_loaded[2]) if step[1] == "W1" else (W2, W2h, W2l, slot_loaded[3])
                        pool.wait_ge(loaded, upto(loaded, tag))
                        if step[1] == "W1":
                            before = MODULES[[m for m, _ in MODULES].index(tag) - 2][0]
                            pool.wait_ge(mm_done, upto(mm_done, (before, "S", GROUPS - 1, NH - 1, NT - 1, GH - 1)))
                        pool.tensor_tensor(hi[:], w, zero.unsqueeze(2).to_broadcast(w.shape), ALU.add).then_inc(pool_done, M.add(pool_done, name + ("hi",)))
                        pool.wait_ge(pool_done, upto(pool_done, name + ("hi",)))
                        pool.tensor_tensor(lo[:], w, hi[:].bitcast(F32), ALU.subtract).then_inc(pool_done, M.add(pool_done, name))
                    elif kind == "P":
                        which, c, n = step[1:]
                        hi, lo, kn = (qh, ql, HALF) if which == "q" else (kh, kl, SP_ if cross else HALF)
                        part = slice(n * HALF, n * HALF + kn)
                        pool.wait_ge(act_done, upto(act_done, name))
                        pool.tensor_tensor(lo[:, c, part], whole[:, whole_of(name)[0], 0:kn], hi[:, c, part].bitcast(F32), ALU.subtract
                                           ).then_inc(pool_done, M.add(pool_done, name))
            M.close("blocks")


_OUT = (B, N, D)


def kernel(**inputs):
    import numpy as np
    import concourse.bacc as bacc
    from concourse.bass_utils import run_bass_kernel_spmd

    def given(name):
        for full in (name, name.replace("_", "_xcond_", 1)):
            if full in inputs:
                return np.asarray(inputs[full])
        raise KeyError(name)

    def again(a):
        return np.concatenate([a, a[B - 1:B]])

    fixed = {"qs_rows": constant_rows(MASKROW), "ks_rows": constant_rows(MAXROW)}
    cols = np.concatenate([fixed[n].T if n in fixed else given(n).reshape(-1, P) for n, _ in COLS]).T
    tp_b, ada = given("L1_tp_b").reshape(3, D), given("L2_adaln_b").reshape(6, D)
    router_b = np.zeros((D,), np.float32)
    router_b[0:E] = given("L0_router_b")
    rows = np.stack([given("L0_out_b"), given("L0_gate_b2"), given("L1_sa_bo"), tp_b[0], tp_b[1], tp_b[2], given("L1_ca_bo"),
                     given("L1_b2"), given("L2_sa_proj_b"), ada[2], ada[5], given("L2_ca_proj_b"), given("L2_fc2_b"),
                     given("L3_bp"), router_b])
    ctx, cond, mask = given("ctx_1024"), given("cond_1024"), given("mask_BxS2_ik0")
    twice = np.concatenate([ctx, ctx[:, S - 1:S]], axis=1)
    arrays = {
        "x": again(given("x")), "ctx": ctx, "ctxT": again(twice.transpose(0, 2, 1)), "condT": again(cond.reshape(B, KC, P).transpose(0, 2, 1)),
        "mask": np.concatenate([mask, mask[:, S - 1:S]], axis=1).reshape(B, 1, SP_), "maskT": mask.reshape(B, S, 1),
        "cols": cols, "rows": rows, "ident": np.eye(P, dtype=np.float32), "sel": selections(),
        "e_b2": given("L0_e_b2"), "router_W": given("L0_router_W"), "L0_WqT": given("L0_Wq").T,
    }
    for n in ("L0_Wk", "L0_Wv", "L0_e_w1", "L0_e_w2", "L0_gate_w1", "L0_gate_w2", "L0_out_w", "L1_sa_wq", "L1_sa_wk", "L1_sa_wv",
              "L1_sa_wo", "L1_ca_wq", "L1_ca_wk", "L1_ca_wv", "L1_ca_wo", "L1_tp_w", "L1_w1", "L1_w2", "L2_adaln_w", "L2_qkv_w",
              "L2_sa_proj_w", "L2_q_w", "L2_kv_w", "L2_ca_proj_w", "L2_fc1_w", "L2_fc2_w", "L3_Wq", "L3_Wkv", "L3_Wp",
              "L3_Wss_q", "L3_Wss_kv"):
        arrays[n] = given(n)
    arrays = {n: np.ascontiguousarray(a) for n, a in arrays.items()}

    def program(marks):
        nc = bacc.Bacc("TRN2", target_bir_lowering=False, num_devices=1)
        T = {n: nc.dram_tensor(f"in_{n}", a.shape, mybir.dt.from_np(a.dtype), kind="ExternalInput").ap() for n, a in arrays.items()}
        T["x0"] = nc.dram_tensor("x_after_block0", (B + 1, N, D), F32, kind="Internal").ap()
        T["out"] = nc.dram_tensor("out", _OUT, F32, kind="ExternalOutput").ap()
        build(nc, T, marks)
        return nc

    counted = Marks()
    program(counted)
    nc = program(Marks(counted))
    r = run_bass_kernel_spmd(nc, [{f"in_{n}": a for n, a in arrays.items()}], core_ids=[0])
    return r.results[0]["out"]
```
